# Optimizing a Trainium2 kernel written in Bass

```python
import numpy as np
import jax
import jax.numpy as jnp

def _softmax(x, axis=-1):
    return jax.nn.softmax(x, axis=axis)

def _gelu(x):
    return jax.nn.gelu(x, approximate=True)

def _silu(x):
    return jax.nn.silu(x)

def _sigmoid(x):
    return jax.nn.sigmoid(x)

def _layernorm(x, axis=-1, eps=1e-05):
    m = jnp.mean(x, axis=axis, keepdims=True)
    v = jnp.var(x, axis=axis, keepdims=True)
    return (x - m) / jnp.sqrt(v + eps)

def _scatter_add(tgt, idx, src, axis=0):
    return tgt.at[idx].add(src)

def _segment_sum(src, seg, n):
    return jax.ops.segment_sum(src, seg, n)
kernel_name = 'mk_macaron_d1_jaxref_r4_e671de'

def setup_inputs(seed: int=0):
    np.random.seed(seed)
    _w = jnp.asarray

    def _L0_attn_setup():
        import jax, jax.numpy as jnp
        import numpy as np
        EMB, HEADS = (256, 16)
        S = EMB // HEADS
        key = jax.random.key(seed)
        ks = jax.random.split(key, 7)
        b, t = (2, 512)
        sc = 0.02
        return {'x': jax.random.normal(ks[0], (b, t, EMB), jnp.float32), 'W_down': jax.random.normal(ks[1], (EMB, EMB), jnp.float32) * sc, 'tokeys': jax.random.normal(ks[2], (HEADS, S, S), jnp.float32) * sc, 'toqueries': jax.random.normal(ks[3], (HEADS, S, S), jnp.float32) * sc, 'tovalues': jax.random.normal(ks[4], (HEADS, S, S), jnp.float32) * sc, 'W_unify': jax.random.normal(ks[5], (EMB, EMB), jnp.float32) * sc, 'b_unify': jax.random.normal(ks[6], (EMB,), jnp.float32) * sc}
    _L0_attn_in = _L0_attn_setup()

    def _L0_ffn_setup():
        import jax, jax.numpy as jnp
        import numpy as np
        E = 8
        C = 320
        D = 256
        H = 1024
        B, S = (4, 512)
        key = jax.random.key(seed)
        ks = jax.random.split(key, 12)
        sc = 0.02
        return {'input': jax.random.normal(ks[0], (B, S, D), jnp.float32), 'router_w': jax.random.normal(ks[1], (D, E), jnp.float32) * sc, 'router_b': jnp.zeros((E,), jnp.float32), 'w1': jax.random.normal(ks[2], (E, D, H), jnp.float32) * sc, 'b1': jnp.zeros((E, H), jnp.float32), 'w2': jax.random.normal(ks[3], (E, H, D), jnp.float32) * sc, 'b2': jnp.zeros((E, D), jnp.float32), 'ow1': jax.random.normal(ks[4], (D, H), jnp.float32) * sc, 'ob1': jnp.zeros((H,), jnp.float32), 'ow2': jax.random.normal(ks[5], (H, D), jnp.float32) * sc, 'ob2': jnp.zeros((D,), jnp.float32)}
    _L0_ffn_in = _L0_ffn_setup()
    _d = {'L0_attn_x': _L0_attn_in['x'], 'L0_attn_W_down': _L0_attn_in['W_down'], 'L0_attn_tokeys': _L0_attn_in['tokeys'], 'L0_attn_toqueries': _L0_attn_in['toqueries'], 'L0_attn_tovalues': _L0_attn_in['tovalues'], 'L0_attn_W_unify': _L0_attn_in['W_unify'], 'L0_attn_b_unify': _L0_attn_in['b_unify'], 'L0_ffn_router_w': _L0_ffn_in['router_w'], 'L0_ffn_router_b': _L0_ffn_in['router_b'], 'L0_ffn_w1': _L0_ffn_in['w1'], 'L0_ffn_b1': _L0_ffn_in['b1'], 'L0_ffn_w2': _L0_ffn_in['w2'], 'L0_ffn_b2': _L0_ffn_in['b2'], 'L0_ffn_ow1': _L0_ffn_in['ow1'], 'L0_ffn_ob1': _L0_ffn_in['ob1'], 'L0_ffn_ow2': _L0_ffn_in['ow2'], 'L0_ffn_ob2': _L0_ffn_in['ob2']}
    _x0 = _d['L0_attn_x']
    _d['L0_attn_x'] = jax.random.normal(jax.random.fold_in(jax.random.key(seed), 1), (8, 1024, 256), dtype=_x0.dtype)
    del _x0
    return _d

def reference(L0_attn_x, L0_attn_W_down, L0_attn_tokeys, L0_attn_toqueries, L0_attn_tovalues, L0_attn_W_unify, L0_attn_b_unify, L0_ffn_router_w, L0_ffn_router_b, L0_ffn_w1, L0_ffn_b1, L0_ffn_w2, L0_ffn_b2, L0_ffn_ow1, L0_ffn_ob1, L0_ffn_ow2, L0_ffn_ob2):

    def _L0_attn_ref(x, W_down, tokeys, toqueries, tovalues, W_unify, b_unify):
        import jax, jax.numpy as jnp
        import numpy as np
        EMB, HEADS = (256, 16)
        S = EMB // HEADS
        b, t, e = x.shape
        h, s = (HEADS, S)
        scale = s ** (-0.25)
        xd = (x @ W_down).reshape(b, t, h, s)
        keys = jnp.einsum('bthk,hik->bthi', xd, tokeys) * scale
        queries = jnp.einsum('bthk,hik->bthi', xd, toqueries) * scale
        values = jnp.einsum('bthk,hik->bthi', xd, tovalues)
        dot = jnp.einsum('bqhs,bkhs->bhqk', queries, keys)
        attn = jax.nn.softmax(dot, axis=-1)
        out = jnp.einsum('bhqk,bkhs->bqhs', attn, values).reshape(b, t, e)
        return out @ W_unify + b_unify

    def _L0_ffn_ref(input, router_w, router_b, w1, b1, w2, b2, ow1, ob1, ow2, ob2):
        import jax, jax.numpy as jnp
        import numpy as np
        E = 8
        C = 320
        D = 256
        H = 1024
        B, S = (4, 512)
        Bq, Sq, Dq = input.shape
        N = Bq * Sq
        xf = input.reshape(N, Dq)
        probs = jax.nn.softmax(xf @ router_w + router_b, axis=-1)
        eid = jnp.argmax(probs, axis=-1)
        onehot = jax.nn.one_hot(eid, E, dtype=xf.dtype)
        rank = (jnp.cumsum(onehot, axis=0)[jnp.arange(N), eid] - 1.0).astype(jnp.int32)
        valid = rank < C
        pos = jnp.where(valid, rank, 0)
        vmask = valid.astype(xf.dtype)[:, None]
        buf = jnp.zeros((E, C, Dq), xf.dtype).at[eid, pos].add(xf * vmask)
        h = jax.nn.relu(jnp.einsum('ecd,edh->ech', buf, w1) + b1[:, None, :])
        y = jnp.einsum('ech,ehd->ecd', h, w2) + b2[:, None, :]
        y_tok = y[eid, pos] * vmask
        yov = jax.nn.relu(xf @ ow1 + ob1) @ ow2 + ob2
        out = y_tok + yov * (1.0 - vmask)
        return out.reshape(Bq, Sq, Dq)
    x = L0_attn_x
    x = x + 0.5 * _L0_ffn_ref(_layernorm(x, axis=-1), L0_ffn_router_w, L0_ffn_router_b, L0_ffn_w1, L0_ffn_b1, L0_ffn_w2, L0_ffn_b2, L0_ffn_ow1, L0_ffn_ob1, L0_ffn_ow2, L0_ffn_ob2)
    x = x + _L0_attn_ref(_layernorm(x, axis=-1), L0_attn_W_down, L0_attn_tokeys, L0_attn_toqueries, L0_attn_tovalues, L0_attn_W_unify, L0_attn_b_unify)
    x = x + 0.5 * _L0_ffn_ref(_layernorm(x, axis=-1), L0_ffn_router_w, L0_ffn_router_b, L0_ffn_w1, L0_ffn_b1, L0_ffn_w2, L0_ffn_b2, L0_ffn_ow1, L0_ffn_ob1, L0_ffn_ow2, L0_ffn_ob2)
    return x

_drawn_inputs = setup_inputs


def setup_inputs(seed=0):
    import zlib

    import numpy as np

    out = dict(_drawn_inputs(seed))
    spreads = {'L0_ffn_router_b': (0.0, 0.1),
     'L0_ffn_b1': (0.0, 0.285),
     'L0_ffn_b2': (0.0, 0.1),
     'L0_ffn_ob1': (0.0, 0.1),
     'L0_ffn_ob2': (0.0, 0.1)}
    factors = {'L0_attn_W_down': 8.0,
     'L0_attn_tokeys': 8.0,
     'L0_attn_toqueries': 8.0,
     'L0_attn_tovalues': 8.0,
     'L0_attn_W_unify': 8.0,
     'L0_attn_b_unify': 7.205}
    for name, (base, spread) in spreads.items():
        noise = np.random.default_rng([zlib.crc32(name.encode()), seed]).standard_normal(out[name].shape)
        drawn = base * np.exp(spread * noise) if base else spread * noise
        out[name] = jnp.asarray(drawn.astype(out[name].dtype))
    for name, factor in factors.items():
        out[name] = (out[name] * factor).astype(out[name].dtype)
    return out
```

```python
from contextlib import ExitStack

import concourse.bass as bass
from concourse import mybir

F32 = mybir.dt.float32
F32R = mybir.dt.float32r
BF16 = mybir.dt.bfloat16
I32 = mybir.dt.int32
ALU = mybir.AluOpType
ACT = mybir.ActivationFunctionType
AX = mybir.AxisListType

P = 128
D = 256
DT = D // P
H = 1024
HT = H // P
E = 8
C = 320
CCH = [(0, 128), (128, 128), (256, 64)]
EPS = 1e-5
CREDIT = 16


class Sem:

    def __init__(self, ctx, nc, name):
        self.sem = ctx.enter_context(nc.semaphore(name))

    def open(self, eng):
        eng.sem_inc(self.sem, CREDIT)

    def wait(self, eng, n):
        eng.wait_ge(self.sem, n + CREDIT)


def split_token_tiles(x):
    return x.rearrange("(t p) d -> p t d", p=P)


class Consts:

    def __init__(self, ctx, nc):
        sb = lambda name, shape, dt: ctx.enter_context(nc.sbuf_tensor(name, shape, dt))
        self.ident = sb("ident", [P, P], F32)
        self.tri = sb("tri", [P, P], F32)
        self.ones = sb("ones", [P, P], F32)
        self.esc = sb("esc", [P, E], F32)
        self.neghalf = sb("neghalf", [P, 32], F32)
        self.tokid = sb("tokid", [P, 64], I32)
        self.rw = sb("rw", [P, DT, E], F32)
        self.rb = sb("rb", [P, E], F32)
        self.b1T = sb("b1T", [P, E + 1, HT], F32)


def setup(nc, k, router_w, router_b, b1, ob1):
    with ExitStack() as ctx:
        sem = lambda n: ctx.enter_context(nc.semaphore(n))
        s_in, s_b, s_set, s_mk, s_t = (sem("su_" + n) for n in ("in", "b", "set", "mk", "t"))
        b1rows = ctx.enter_context(nc.sbuf_tensor("su_b1rows", [(E + 1) * HT, P], F32))
        pt = ctx.enter_context(nc.psum_tensor("su_pt", [P, 512], F32))
        block = ctx.enter_context(nc.Block())

        @block.sync
        def _(eng):
            eng.dma_start(b1rows[0:E * HT, :], b1.rearrange("e (c p) -> (e c) p", p=P)).then_inc(s_b, 16)
            eng.dma_start(b1rows[E * HT:, :], ob1.rearrange("(c p) -> c p", p=P)).then_inc(s_b, 16)
            eng.dma_start(k.rw[:, :, :], router_w.rearrange("(c p) e -> p c e", p=P)).then_inc(s_in, 16)
            eng.dma_start(k.rb[:, :], router_b.rearrange("(a e) -> a e", a=1).broadcast_to([P, E])).then_inc(s_in, 16)
            eng.wait_ge(s_in, 32)

        @block.gpsimd
        def _(eng):
            eng.memset(k.ident[:, :], 0.0).then_inc(s_set, 1)
            eng.memset(k.tri[:, :], 1.0).then_inc(s_set, 1)
            eng.memset(k.ones[:, :], 1.0)
            eng.memset(k.neghalf[:, :], -0.5)
            eng.iota(k.tokid[:, :], [[P, 64]], base=0, channel_multiplier=1)
            eng.iota(k.esc[:, :], [[-1, E]], base=E, channel_multiplier=0, allow_small_or_imprecise_dtypes=True)
            eng.wait_ge(s_set, 2)
            eng.affine_select(out=k.ident[:, :], in_=k.ident[:, :], compare_op=ALU.not_equal, fill=1.0,
                              base=0, pattern=[[-1, P]], channel_multiplier=1).then_inc(s_mk, 1)
            eng.affine_select(out=k.tri[:, :], in_=k.tri[:, :], compare_op=ALU.is_ge, fill=0.0,
                              base=0, pattern=[[1, P]], channel_multiplier=-1).then_inc(s_mk, 1)

        @block.tensor
        def _(eng):
            n = (E + 1) * HT
            eng.wait_ge(s_mk, 1)
            eng.wait_ge(s_b, 32)
            eng.transpose(pt[:, 0:n], b1rows[:, :], k.ident[0:n, 0:n]).then_inc(s_t, 1)

        @block.vector
        def _(eng):
            eng.wait_ge(s_t, 1)
            eng.tensor_copy(k.b1T[:, :, :].rearrange("p e c -> p (e c)"), pt[:, 0:(E + 1) * HT])


class Norm:

    def __init__(self, ctx, nc, k, name):
        sb = lambda n, shape: ctx.enter_context(nc.sbuf_tensor(name + n, shape, F32))
        self.k = k
        self.stats = sb("stats", [P, 4, 6])
        self.mv = sb("mv", [P, 4, 2])
        self.ve = sb("ve", [P, 4])
        self.rstd = sb("rstd", [P, 4])
        self.pad = sb("pad", [P, 1])
        self.s_dve = Sem(ctx, nc, name + "s_dve")
        self.s_pow = Sem(ctx, nc, name + "s_pow")

    def open_vector(self, eng):
        self.s_dve.open(eng)

    def open_pool(self, eng):
        self.s_pow.open(eng)

    def stats_step(self, eng, n, src, rows):
        last = None
        self.s_pow.wait(eng, n)
        self.s_dve.wait(eng, 3 * n)
        for j, r in enumerate(rows):
            last = eng.bn_stats(self.stats[0:r, j, :], src[0:r, j, :])
        last.then_inc(self.s_dve.sem, 1)
        self.s_dve.wait(eng, 3 * n + 1)
        eng.memset(self.pad[:, :], 0.0)
        for j, r in enumerate(rows):
            last = eng.bn_aggr(self.mv[0:r, j, :], self.stats[0:r, j, :])
        last.then_inc(self.s_dve.sem, 1)
        self.s_dve.wait(eng, 3 * n + 2)
        last = eng.tensor_scalar(self.ve[:, 0:len(rows)], self.mv[:, 0:len(rows), 1], EPS, None, ALU.add)
        last.then_inc(self.s_dve.sem, 1)

    def pow_step(self, eng, n, count):
        self.s_dve.wait(eng, 3 * n + 3)
        eng.tensor_tensor(self.rstd[:, 0:count], self.ve[:, 0:count], self.k.neghalf[:, 0:count],
                          ALU.pow).then_inc(self.s_pow.sem, 1)

    def apply_step(self, eng, n, dst, src, rows):
        self.s_pow.wait(eng, n + 1)
        last = None
        for j, r in enumerate(rows):
            last = eng.tensor_scalar(dst[0:r, j, :], src[0:r, j, :], self.mv[0:r, j, 0:1], self.rstd[0:r, j:j + 1],
                                     ALU.subtract, ALU.mult)
        return last


class Route:

    def __init__(self, ctx, nc, name):
        sb = lambda n, shape, dt: ctx.enter_context(nc.sbuf_tensor(name + n, shape, dt))
        self.valid = sb("valid", [P, 64], F32)
        self.over = sb("over", [P, 64], F32)
        self.put = sb("put", [P, 64], I32)
        self.get = sb("get", [P, 64], I32)


def router(nc, k, logits, name, x_in, b2s, b2, ob2):
    x_t = split_token_tiles(x_in)
    nt = x_t.shape[1]
    n_it = nt // 8
    with ExitStack() as ctx:
        sb = lambda n, shape, dt: ctx.enter_context(nc.sbuf_tensor(name + n, shape, dt))
        xr = [sb(f"xr{i}", [P, 4, D], F32) for i in range(2)]
        xn = [sb(f"xn{i}", [P, 4, D], F32) for i in range(2)]
        xT = [sb(f"xT{i}", [P, DT, 4 * P], F32) for i in range(2)]
        norm = Norm(ctx, nc, k, name + "ln_")
        pT = [ctx.enter_context(nc.psum_tensor(name + f"pT{i}", [P, 512], F32)) for i in range(4)]
        pL = [ctx.enter_context(nc.psum_tensor(name + f"pL{i}", [P, 512], F32)) for i in range(2)]
        s_ld = [Sem(ctx, nc, name + f"s_ld{i}") for i in range(2)]
        s_b2 = ctx.enter_context(nc.semaphore(name + "s_b2"))
        s_xn, s_tp, s_ev, s_ev2, s_lg, s_out = (Sem(ctx, nc, name + n) for n in
                                         ("s_xn", "s_tp", "s_ev", "s_ev2", "s_lg", "s_out"))
        block = ctx.enter_context(nc.Block())

        @block.sync
        def _(eng):
            for s in s_ld:
                s.open(eng)
            for e in range(E):
                eng.dma_start(b2s[:, e, :], b2[e:e + 1, :].broadcast_to([P, D])).then_inc(s_b2, 16)
            eng.dma_start(b2s[:, E, :], ob2.rearrange("(a e) -> a e", a=1).broadcast_to([P, D])).then_inc(s_b2, 16)
            with eng.Fori(0, n_it) as i:
                for b in range(2):
                    s_xn.wait(eng, 2 * i + b - 1)
                    eng.dma_start(xr[b][:, :, :], x_t[:, bass.ds(8 * i + 4 * b, 4), :]).then_inc(s_ld[b].sem, 16)
            eng.wait_ge(s_b2, 16 * (E + 1))

        @block.gpsimd
        def _(eng):
            norm.open_pool(eng)
            with eng.Fori(0, n_it) as i:
                for b in range(2):
                    norm.pow_step(eng, 2 * i + b, 4)

        @block.vector
        def _(eng):
            norm.open_vector(eng)
            s_xn.open(eng)
            s_ev.open(eng)
            s_out.open(eng)
            with eng.Fori(0, n_it) as i:
                for b in range(2):
                    n = 2 * i + b
                    s_ld[b].wait(eng, 16 * i + 16)
                    norm.stats_step(eng, n, xr[b], [P] * 4)
                    s_tp.wait(eng, 2 * n - 2)
                    norm.apply_step(eng, n, xn[b], xr[b], [P] * 4).then_inc(s_xn.sem, 1)
                    s_tp.wait(eng, 2 * n + 1)
                    s_lg.wait(eng, n - 1)
                    eng.tensor_copy(xT[b][:, 0, :], pT[2 * b][:, :]).then_inc(s_ev.sem, 1)
                    s_lg.wait(eng, n + 1)
                    eng.tensor_tensor(logits[:, bass.ds(8 * i + 4 * b, 4), :],
                                      pL[b][:, 0:4 * E].rearrange("p (t e) -> p t e", e=E),
                                      k.rb[:, :].unsqueeze(1).broadcast_to([P, 4, E]), ALU.add).then_inc(s_out.sem, 1)

        @block.scalar
        def _(eng):
            s_ev2.open(eng)
            with eng.Fori(0, n_it) as i:
                for b in range(2):
                    n = 2 * i + b
                    s_tp.wait(eng, 2 * n + 2)
                    s_lg.wait(eng, n - 1)
                    eng.activation(xT[b][:, 1, :], pT[2 * b + 1][:, :], ACT.Copy).then_inc(s_ev2.sem, 1)

        @block.tensor
        def _(eng):
            s_tp.open(eng)
            s_lg.open(eng)
            with eng.Fori(0, n_it) as i:
                for b in range(2):
                    n = 2 * i + b
                    s_xn.wait(eng, n + 1)
                    for f in range(DT):
                        (s_ev if f == 0 else s_ev2).wait(eng, n - 1)
                        for j in range(4):
                            mm = eng.transpose(pT[2 * b + f][:, j * P:(j + 1) * P], xn[b][:, j, f * P:(f + 1) * P],
                                               k.ident[:, :])
                        mm.then_inc(s_tp.sem, 1)
                    s_ev.wait(eng, n + 1)
                    s_ev2.wait(eng, n + 1)
                    s_out.wait(eng, n - 1)
                    for j in range(4):
                        for f in range(DT):
                            mm = eng.matmul(pL[b][:, j * E:(j + 1) * E], xT[b][:, f, j * P:(j + 1) * P],
                                            k.rw[:, f, :], start=(f == 0), stop=(f == DT - 1))
                    mm.then_inc(s_lg.sem, 1)


def decide(nc, k, r, logits, name, table):
    nt = 64
    with ExitStack() as ctx:
        sb = lambda n, shape, dt: ctx.enter_context(nc.sbuf_tensor(name + n, shape, dt))
        mx = sb("mx", [P, nt], F32)
        cand = sb("cand", [P, nt, E], F32)
        best = sb("best", [P, nt], F32)
        onehot = sb("onehot", [P, nt, E], F32)
        tot = sb("tot", [P, nt, E], F32)
        incl = sb("incl", [P, nt, E], F32)
        one_t = sb("one_t", [P, nt], F32)
        rank = sb("rank", [P, nt], F32)
        pos = sb("pos", [P, nt], F32)
        tmp = sb("tmp", [P, nt], F32)
        zero = sb("zero", [P, E * C // P], I32)
        pc = ctx.enter_context(nc.psum_tensor(name + "pc", [P, 512], F32))
        pt = ctx.enter_context(nc.psum_tensor(name + "pt", [P, 512], F32))
        sem = lambda n: ctx.enter_context(nc.semaphore(name + n))
        s_v, s_mm, s_z, s_tab = sem("s_v"), sem("s_mm"), sem("s_z"), sem("s_tab")
        block = ctx.enter_context(nc.Block())
        flat = lambda t: t[:, :, :].rearrange("p t e -> p (t e)")
        wide = lambda t: t[:, :].unsqueeze(2).broadcast_to([P, nt, E])

        @block.gpsimd
        def _(eng):
            eng.memset(zero[:, :], 0).then_inc(s_z, 1)

        @block.sync
        def _(eng):
            eng.wait_ge(s_z, 1)
            eng.dma_start(table.rearrange("(p c) a -> p (c a)", p=P), zero[:, :]).then_inc(s_tab, 16)
            eng.wait_ge(s_tab, 16)

        @block.tensor
        def _(eng):
            eng.wait_ge(s_v, 5)
            eng.matmul(pc[:, :], k.tri[:, :], flat(onehot), start=True, stop=True)
            eng.matmul(pt[:, :], k.ones[:, :], flat(onehot), start=True, stop=True).then_inc(s_mm, 1)

        @block.vector
        def _(eng):
            n = 0

            def link(ins):
                nonlocal n
                n += 1
                ins.then_inc(s_v, 1)
                eng.wait_ge(s_v, n)

            link(eng.tensor_reduce(mx[:, :], logits[:, :, :], AX.X, ALU.max))
            link(eng.tensor_tensor(cand[:, :, :], logits[:, :, :], wide(mx), ALU.is_ge))
            link(eng.tensor_tensor(cand[:, :, :], cand[:, :, :], k.esc[:, :].unsqueeze(1).broadcast_to([P, nt, E]),
                                   ALU.mult))
            link(eng.tensor_reduce(best[:, :], cand[:, :, :], AX.X, ALU.max))
            link(eng.tensor_tensor(onehot[:, :, :], cand[:, :, :], wide(best), ALU.is_equal))
            link(eng.memset(one_t[:, :], 1.0))
            eng.wait_ge(s_mm, 1)
            for e in range(E):
                ins = eng.tensor_tensor_scan(tot[:, :, e], one_t[:, :], pt[:, e:512:E], 0.0, ALU.mult, ALU.add)
            link(ins)
            link(eng.tensor_tensor(flat(incl), pc[:, :], flat(tot), ALU.add))
            link(eng.scalar_tensor_tensor(flat(incl), pt[:, :], -1.0, flat(incl), ALU.mult, ALU.add))
            link(eng.tensor_tensor(flat(incl), flat(incl), flat(onehot), ALU.mult))
            link(eng.tensor_reduce(rank[:, :], incl[:, :, :], AX.X, ALU.add))
            link(eng.tensor_scalar(r.valid[:, :], rank[:, :], float(C), None, ALU.is_le))
            link(eng.tensor_scalar(r.over[:, :], r.valid[:, :], -1.0, 1.0, ALU.mult, ALU.add))
            link(eng.tensor_scalar(rank[:, :], rank[:, :], -1.0, None, ALU.add))
            link(eng.tensor_tensor(rank[:, :], rank[:, :], r.valid[:, :], ALU.mult))
            link(eng.tensor_scalar(tmp[:, :], best[:, :], -float(C), float(E * C), ALU.mult, ALU.add))
            link(eng.tensor_tensor(pos[:, :], tmp[:, :], rank[:, :], ALU.add))
            link(eng.tensor_copy(r.get[:, :], pos[:, :]))
            link(eng.scalar_tensor_tensor(tmp[:, :], r.over[:, :], float(2 * E * C), pos[:, :], ALU.mult, ALU.add))
            link(eng.tensor_copy(r.put[:, :], tmp[:, :]))


def mlps(nc, k, r, name, x_in, b2s, w1, w2, ow1, ow2, yov, table, yexp):
    x_t = split_token_tiles(x_in)
    NT = x_t.shape[1]
    NB = NT // 4
    RING = 4
    LAG = 2
    PIECES = 8
    WN = DT * H + HT * D
    PW = WN // PIECES
    with ExitStack() as ctx:
        sb = lambda n, shape, dt: ctx.enter_context(nc.sbuf_tensor(name + n, shape, dt))
        xr = [sb(f"xr{i}", [P, 4, D], F32) for i in range(2)]
        xn = sb("xn", [P, 4, D], F32)
        xTh = [sb(f"xTh{i}", [P, DT, 512], F32R) for i in range(2)]
        xTl = [sb(f"xTl{i}", [P, DT, 512], F32R) for i in range(2)]
        h32 = [sb(f"h32{i}", [P, 512], F32) for i in range(2)]
        hh = [sb(f"hh{i}", [P, 512], F32R) for i in range(RING)]
        hl = [sb(f"hl{i}", [P, 512], F32R) for i in range(RING)]
        wraw = sb("wraw", [P, WN], F32)
        wh = [sb(f"wh{i}", [P, WN], F32R) for i in range(2)]
        wl = [sb(f"wl{i}", [P, WN], F32R) for i in range(2)]
        ye = sb("ye", [P, 3, D], F32)
        idx = sb("idx", [P, E, 3], I32)
        norm = Norm(ctx, nc, k, name + "ln_")
        pL = [ctx.enter_context(nc.psum_tensor(name + f"pL{i}", [P, 512], F32)) for i in range(2)]
        pA = [ctx.enter_context(nc.psum_tensor(name + f"pA{i}", [P, 2, 512], F32)) for i in range(2)]
        pT = [ctx.enter_context(nc.psum_tensor(name + f"pT{i}", [P, 512], F32)) for i in range(DT)]
        S = lambda n: Sem(ctx, nc, name + n)
        s_ld = [S(f"s_ld{i}") for i in range(2)]
        s_ga = [ctx.enter_context(nc.semaphore(name + f"s_ga{i}")) for i in range(2)]
        s_raw = [S(f"s_raw{i}") for i in range(PIECES)]
        s_st = S("s_st")
        s_xn = S("s_xn")
        s_tp = S("s_tp")
        s_thi = S("s_thi")
        s_tlo = S("s_tlo")
        s_l1 = S("s_l1")
        s_h = S("s_h")
        s_hi = S("s_hi")
        s_lo = S("s_lo")
        s_l2 = S("s_l2")
        s_y = S("s_y")
        s_whi = S("s_whi")
        s_wlo = S("s_wlo")
        s_scat = ctx.enter_context(nc.semaphore(name + "s_scat"))
        s_idx = ctx.enter_context(nc.semaphore(name + "s_idx"))

        W1 = lambda w, c, h: w[:, c * H + h * P:c * H + (h + 1) * P]
        W2 = lambda w, h: w[:, DT * H + h * D:DT * H + (h + 1) * D]
        chunks = {"dense": [(j * P, P) for j in range(4)], "expert": CCH}
        width = {"dense": 512, "expert": C}

        def stream(eng, prologue, block):
            prologue()
            with eng.Fori(0, NB // 2 - 1) as i:
                block(i, 2 * i, 0, "dense", "dense")
                block(i, 2 * i + 1, 1, "dense", "dense")
            block(NB // 2 - 1, NB - 2, 0, "dense", "dense")
            block(NB // 2 - 1, NB - 1, 1, "dense", "expert")
            with eng.Fori(0, E // 2 - 1) as i:
                block(i, NB + 2 * i, 0, "expert", "expert")
                block(i, NB + 2 * i + 1, 1, "expert", "expert")
            block(E // 2 - 1, NB + E - 2, 0, "expert", "expert")
            block(E // 2 - 1, NB + E - 1, 1, "expert", None)

        def split_at(i, n, b, kind):
            if kind == "expert":
                last = isinstance(n, int) and n == NB + E - 1
                return None if last else (2 * i + b + 2, b)
            return (1, 1) if isinstance(n, int) and n == NB - 2 else None

        def pieces_at(s):
            return [2 * s, 2 * s + 1] if s < 2 else [s + 2] if s < HT - LAG else []

        def wbuf(b, kind):
            return 0 if kind == "dense" else 1 - b

        block = ctx.enter_context(nc.Block())

        @block.sync
        def _(eng):
            for s in (*s_ld, *s_raw, s_st):
                s.open(eng)

            def load_piece(m, q, a1, a2):
                s_wlo.wait(eng, PIECES * (m - 1) + q + 1)
                dst = wraw[:, q * PW:(q + 1) * PW]
                if q < PIECES // 2:
                    c, f = q // 2, q % 2
                    src = a1[c * P:(c + 1) * P, f * PW:(f + 1) * PW]
                else:
                    q2 = q - PIECES // 2
                    dst = dst.rearrange("p (c d) -> p c d", d=D)
                    src = a2[2 * q2 * P:(2 * q2 + 2) * P, :].rearrange("(c p) d -> p c d", p=P)
                eng.dma_start(dst, src).then_inc(s_raw[q].sem, 16)

            def of_expert(w, e):
                return w[bass.ds(e, 1), :, :].rearrange("a r c -> (a r) c")

            def load_rows(n, b):
                s_xn.wait(eng, n - 1)
                eng.dma_start(xr[b][:, :, :], x_t[:, bass.ds(4 * n, 4), :]).then_inc(s_ld[b].sem, 16)

            for n in range(2):
                load_rows(n, n)
            for q in range(PIECES):
                load_piece(0, q, ow1, ow2)
            for q in range(PIECES):
                load_piece(1, q, w1[0], w2[0])
            with eng.Fori(1, NB // 2) as i:
                for b in range(2):
                    load_rows(2 * i + b, b)
            for q in range(PIECES):
                load_piece(2, q, w1[1], w2[1])
            eng.wait_ge(s_scat, 16 * NT)
            slots = table.rearrange("(e c) a -> c e a", e=E)
            for j, (c0, m) in enumerate(CCH):
                eng.dma_start(idx[0:m, :, j:j + 1], slots[c0:c0 + m], allow_slow_non_contiguous=True).then_inc(s_idx, 16)
            def store(e):
                s_y.wait(eng, NB + e + 1)
                for j, (c0, m) in enumerate(CCH):
                    eng.dma_start(yexp[bass.ds(e * C + c0, m), :], ye[0:m, j, :]).then_inc(s_st.sem, 16)

            with eng.Fori(0, E - 2) as e:
                for q in range(PIECES):
                    load_piece(e + 3, q, of_expert(w1, e + 2), of_expert(w2, e + 2))
                store(e)
            for e in (E - 2, E - 1):
                store(e)
            s_st.wait(eng, 16 * len(CCH) * E)

        @block.gpsimd
        def _(eng):
            norm.open_pool(eng)
            norm.pow_step(eng, 0, 4)
            for n in range(NB + E):
                if n + 1 < NB + E:
                    norm.pow_step(eng, n + 1, 4 if n + 1 < NB else 3)
                if 8 * n < NT:
                    for t in range(8 * n, 8 * n + 8):
                        eng.indirect_dma_start(
                            out=table[:, :], out_offset=bass.IndirectOffsetOnAxis(ap=r.put[:, t:t + 1], axis=0),
                            in_=k.tokid[:, t:t + 1], in_offset=None,
                            bounds_check=E * C - 1, oob_is_err=False).then_inc(s_scat, 16)
                e = n + 2 - NB
                if 0 <= e < E:
                    if e == 0:
                        eng.wait_ge(s_idx, 16 * len(CCH))
                    s_xn.wait(eng, n + 1)
                    for j, (c0, m) in enumerate(CCH):
                        eng.indirect_dma_start(
                            out=xr[n % 2][0:m, j, :], out_offset=None, in_=x_in[:, :],
                            in_offset=bass.IndirectOffsetOnAxis(ap=idx[0:m, e, j:j + 1], axis=0),
                            bounds_check=NT * P - 1, oob_is_err=False).then_inc(s_ga[n % 2], 16)

        @block.vector
        def _(eng):
            norm.open_vector(eng)
            for s in (s_xn, s_tlo, s_lo, s_y, s_wlo):
                s.open(eng)

            def stats(i, n, b, kind):
                rows = [m for _, m in chunks[kind]]
                if kind == "dense":
                    s_ld[b].wait(eng, 16 * i + 16)
                else:
                    eng.wait_ge(s_ga[b], 16 * len(CCH) * (i + 1))
                norm.stats_step(eng, n, xr[b], rows)

            def apply(n, b, kind):
                s_tp.wait(eng, 2 * n)
                norm.apply_step(eng, n, xn, xr[b], [m for _, m in chunks[kind]]).then_inc(s_xn.sem, 1)

            def rows_low(n, b, f, w):
                s_thi.wait(eng, 2 * n + f + 1)
                eng.tensor_tensor(xTl[b][:, f, 0:w], pT[f][:, 0:w], xTh[b][:, f, 0:w].bitcast(F32),
                                  ALU.subtract).then_inc(s_tlo.sem, 1)

            def hidden_low(n, b, h, w):
                s_hi.wait(eng, HT * n + h + 1)
                eng.tensor_tensor(hl[h % RING][:, 0:w], h32[h % 2][:, 0:w], hh[h % RING][:, 0:w].bitcast(F32),
                                  ALU.subtract).then_inc(s_lo.sem, 1)

            def weights_low(m, buf, q):
                s_whi.wait(eng, PIECES * m + q + 1)
                sl = slice(q * PW, (q + 1) * PW)
                eng.tensor_tensor(wl[buf][:, sl], wraw[:, sl], wh[buf][:, sl].bitcast(F32),
                                  ALU.subtract).then_inc(s_wlo.sem, 1)

            def results(i, n, b, kind):
                s_l2.wait(eng, HT * (n + 1))
                if kind == "dense":
                    bias = b2s[:, E:E + 1, :].broadcast_to([P, 2, D])
                    for a in range(2):
                        ins = eng.tensor_tensor(yov[:, bass.ds(4 * n + 2 * a, 2), :],
                                                pA[b][:, a, :].rearrange("p (t d) -> p t d", d=D), bias, ALU.add)
                else:
                    e = 2 * i + b
                    s_st.wait(eng, 48 * e)
                    eng.tensor_tensor(ye[:, 0:2, :], pA[b][:, 0, :].rearrange("p (t d) -> p t d", d=D),
                                      b2s[:, bass.ds(e, 1), :].broadcast_to([P, 2, D]), ALU.add)
                    m = CCH[2][1]
                    ins = eng.tensor_tensor(ye[0:m, 2:3, :], pA[b][0:m, 1:2, 0:D], b2s[0:m, bass.ds(e, 1), :], ALU.add)
                ins.then_inc(s_y.sem, 1)

            def prologue():
                stats(0, 0, 0, "dense")
                for q in range(PIECES):
                    weights_low(0, 0, q)
                apply(0, 0, "dense")
                for f in range(DT):
                    rows_low(0, 0, f, 512)
                for h in range(LAG):
                    hidden_low(0, 0, h, 512)

            def block_(i, n, b, kind, nxt):
                sp = split_at(i, n, b, kind)
                i1 = i + b if nxt == kind else 0
                for s in range(HT):
                    if s + LAG < HT:
                        hidden_low(n, b, s + LAG, width[kind])
                    elif nxt:
                        hidden_low(n + 1, 1 - b, s + LAG - HT, width[nxt])
                    for q in pieces_at(s) if sp else ():
                        weights_low(sp[0], sp[1], q)
                    if nxt and s == 0:
                        stats(i1, n + 1, 1 - b, nxt)
                    if nxt and s == 1:
                        apply(n + 1, 1 - b, nxt)
                    if nxt and s in (2, 4):
                        rows_low(n + 1, 1 - b, s // 2 - 1, width[nxt])
                results(i, n, b, kind)

            stream(eng, prologue, block_)


        @block.scalar
        def _(eng):
            for t in (s_thi, s_h, s_hi, s_whi):
                t.open(eng)

            def rows_high(n, b, f, w):
                s_tp.wait(eng, 2 * n + f + 1)
                s_l1.wait(eng, HT * (n - 1))
                eng.activation(xTh[b][:, f, 0:w], pT[f][:, 0:w], ACT.Copy).then_inc(s_thi.sem, 1)

            def hidden_high(i, n, b, kind, h):
                w = width[kind]
                g = HT * n + h
                bias = k.b1T[:, E, h:h + 1] if kind == "dense" else k.b1T[:, bass.ds(2 * i + b, 1), h]
                s_l1.wait(eng, g + 1)
                s_lo.wait(eng, g - 1)
                eng.activation(h32[h % 2][:, 0:w], pL[h % 2][:, 0:w], ACT.Relu, bias=bias).then_inc(s_h.sem, 1)
                s_h.wait(eng, g + 1)
                s_l2.wait(eng, g - RING + 1)
                eng.activation(hh[h % RING][:, 0:w], h32[h % 2][:, 0:w], ACT.Copy).then_inc(s_hi.sem, 1)

            def weights_high(i, n, m, buf, q):
                s_raw[q].wait(eng, 16 * m + 16)
                if q == 0 and n is not None:
                    s_l2.wait(eng, HT * n)
                sl = slice(q * PW, (q + 1) * PW)
                eng.activation(wh[buf][:, sl], wraw[:, sl], ACT.Copy).then_inc(s_whi.sem, 1)

            def prologue():
                for q in range(PIECES):
                    weights_high(0, None, 0, 0, q)
                for f in range(DT):
                    rows_high(0, 0, f, 512)
                for h in range(LAG):
                    hidden_high(0, 0, 0, "dense", h)

            def block_(i, n, b, kind, nxt):
                sp = split_at(i, n, b, kind)
                i1 = i + b if nxt == kind else 0
                for s in range(HT):
                    if s + LAG < HT:
                        hidden_high(i, n, b, kind, s + LAG)
                    elif nxt:
                        hidden_high(i1, n + 1, 1 - b, nxt, s + LAG - HT)
                    for q in pieces_at(s) if sp else ():
                        weights_high(i, n, sp[0], sp[1], q)
                    if nxt and s in (2, 4):
                        rows_high(n + 1, 1 - b, s // 2 - 1, width[nxt])

            stream(eng, prologue, block_)

        @block.tensor
        def _(eng):
            for t in (s_tp, s_l1, s_l2):
                t.open(eng)

            def turn(n, b, kind, f):
                s_xn.wait(eng, n + 1)
                s_tlo.wait(eng, 2 * (n - 1) + f + 1)
                for j, (c0, m) in enumerate(chunks[kind]):
                    mm = eng.transpose(pT[f][:, c0:c0 + m], xn[0:m, j, f * P:(f + 1) * P], k.ident[0:m, 0:m])
                mm.then_inc(s_tp.sem, 1)

            def into_hidden(n, b, kind, h):
                w, wb = width[kind], wbuf(b, kind)
                if h == 0:
                    s_tlo.wait(eng, 2 * n + 2)
                s_h.wait(eng, HT * n + h - 1)
                out = pL[h % 2][:, 0:w]
                for c in range(DT):
                    eng.matmul(out, W1(wh[wb], c, h), xTh[b][:, c, 0:w], start=(c == 0), stop=False)
                    eng.matmul(out, W1(wh[wb], c, h), xTl[b][:, c, 0:w], start=False, stop=False)
                    mm = eng.matmul(out, W1(wl[wb], c, h), xTh[b][:, c, 0:w], start=False, stop=(c == DT - 1))
                mm.then_inc(s_l1.sem, 1)

            def out_of_hidden(n, b, kind, h):
                wb = wbuf(b, kind)
                s_lo.wait(eng, HT * n + h + 1)
                if h == 0:
                    s_y.wait(eng, n - 1)
                for j, (c0, m) in enumerate(chunks[kind]):
                    out = pA[b][0:m, j // 2, (j % 2) * D:(j % 2 + 1) * D]
                    hi, lo = hh[h % RING][:, c0:c0 + m], hl[h % RING][:, c0:c0 + m]
                    eng.matmul(out, hi, W2(wh[wb], h), start=(h == 0 and j % 2 == 0), stop=False,
                               skip_group_check=True)
                    eng.matmul(out, hi, W2(wl[wb], h), start=False, stop=False, skip_group_check=True)
                    mm = eng.matmul(out, lo, W2(wh[wb], h), start=False, stop=(h == HT - 1), skip_group_check=True)
                mm.then_inc(s_l2.sem, 1)

            def prologue():
                for f in range(DT):
                    turn(0, 0, "dense", f)
                s_wlo.wait(eng, PIECES)
                for h in range(LAG):
                    into_hidden(0, 0, "dense", h)

            def block_(i, n, b, kind, nxt):
                for s in range(HT):
                    if nxt and s in (2, 4):
                        turn(n + 1, 1 - b, nxt, s // 2 - 1)
                    out_of_hidden(n, b, kind, s)
                    if s + LAG < HT:
                        into_hidden(n, b, kind, s + LAG)
                    elif nxt:
                        if nxt == "expert" and s + LAG == HT:
                            s_wlo.wait(eng, PIECES * (n + 1 - NB + 2))
                        into_hidden(n + 1, 1 - b, nxt, s + LAG - HT)

            stream(eng, prologue, block_)


def combine(nc, k, r, name, x_in, x_out, yov, yexp):
    x_t, o_t = split_token_tiles(x_in), split_token_tiles(x_out)
    NB = x_t.shape[1] // 4
    with ExitStack() as ctx:
        sb = lambda n, shape, dt: ctx.enter_context(nc.sbuf_tensor(name + n, shape, dt))
        xr = [sb(f"xr{i}", [P, 4, D], F32) for i in range(2)]
        yt = [sb(f"yt{i}", [P, 4, D], F32) for i in range(2)]
        u = [sb(f"u{i}", [P, 4, D], F32) for i in range(2)]
        S = lambda n: Sem(ctx, nc, name + n)
        s_ld, s_st = ([S(f"{n}{i}") for i in range(2)] for n in ("s_ld", "s_st"))
        s_ga = [ctx.enter_context(nc.semaphore(name + f"s_ga{i}")) for i in range(2)]
        s_u, s_v, s_x = S("s_u"), S("s_v"), S("s_x")
        block = ctx.enter_context(nc.Block())

        @block.sync
        def _(eng):
            for s in s_ld:
                s.open(eng)
            with eng.Fori(0, NB // 2) as i:
                for b in range(2):
                    s_x.wait(eng, 2 * i + b - 1)
                    eng.dma_start(xr[b][:, :, :], x_t[:, bass.ds(8 * i + 4 * b, 4), :]).then_inc(s_ld[b].sem, 16)

        @block.gpsimd
        def _(eng):
            for n in range(NB):
                s_v.wait(eng, n - 1)
                for j in range(4):
                    eng.indirect_dma_start(
                        out=yt[n % 2][:, j, :], out_offset=None, in_=yexp[:, :],
                        in_offset=bass.IndirectOffsetOnAxis(ap=r.get[:, 4 * n + j:4 * n + j + 1], axis=0),
                        bounds_check=E * C - 1, oob_is_err=False).then_inc(s_ga[n % 2], 16)

        @block.vector
        def _(eng):
            for s in (s_u, s_v, s_x):
                s.open(eng)
            with eng.Fori(0, NB // 2) as i:
                for b in range(2):
                    n = 2 * i + b
                    s_st[b].wait(eng, 16 * i)
                    for j in range(4):
                        ins = eng.tensor_scalar(u[b][:, j:j + 1, :], yov[:, bass.ds(8 * i + 4 * b + j, 1), :],
                                                r.over[:, bass.ds(8 * i + 4 * b + j, 1)], None, ALU.mult)
                    ins.then_inc(s_u.sem, 1)
                    s_u.wait(eng, n + 1)
                    eng.wait_ge(s_ga[b], 64 * i + 64)
                    for j in range(4):
                        ins = eng.scalar_tensor_tensor(u[b][:, j, :], yt[b][:, j, :],
                                                       r.valid[:, bass.ds(8 * i + 4 * b + j, 1)], u[b][:, j, :],
                                                       ALU.mult, ALU.add)
                    ins.then_inc(s_v.sem, 1)
                    s_v.wait(eng, n + 1)
                    s_ld[b].wait(eng, 16 * i + 16)
                    eng.scalar_tensor_tensor(u[b][:, :, :], u[b][:, :, :], 0.5, xr[b][:, :, :],
                                             ALU.mult, ALU.add).then_inc(s_x.sem, 1)

        @block.scalar
        def _(eng):
            for s in s_st:
                s.open(eng)
            with eng.Fori(0, NB // 2) as i:
                for b in range(2):
                    s_x.wait(eng, 2 * i + b + 1)
                    eng.dma_start(o_t[:, bass.ds(8 * i + 4 * b, 4), :], u[b][:, :, :]).then_inc(s_st[b].sem, 16)
            for s in s_st:
                s.wait(eng, 16 * (NB // 2))


def ffn(nc, k, name, x_in, x_out, w1, b2, w2, ow1, ow2, ob2):
    table = nc.dram_tensor(name + "table", (E * C, 1), I32).ap()
    yexp = nc.dram_tensor(name + "yexp", (E * C, D), F32).ap()
    with ExitStack() as ctx:
        r = Route(ctx, nc, name)
        b2s = ctx.enter_context(nc.sbuf_tensor(name + "b2s", [P, E + 1, D], F32))
        with nc.sbuf_tensor(name + "logits", [P, 64, E], F32) as logits:
            router(nc, k, logits, name + "ro_", x_in, b2s, b2, ob2)
            decide(nc, k, r, logits, name + "de_", table)
        yov = ctx.enter_context(nc.sbuf_tensor(name + "yov", [P, 64, D], F32))
        mlps(nc, k, r, name + "ml_", x_in, b2s, w1, w2, ow1, ow2, yov, table, yexp)
        combine(nc, k, r, name + "co_", x_in, x_out, yov, yexp)


HEADS = 16
HS = D // HEADS
GH = 4
VW = 32
SLOTS = 6
Q_PARTS = [0, 1, 2, 0, 1, 0]
K_PARTS = [0, 0, 0, 1, 1, 2]
KROWS = SLOTS * HS
SCALE = float(HS) ** -0.25
MROWS = 3


class Heads:

    def __init__(self, ctx, nc):
        sb = lambda n, shape, dt: ctx.enter_context(nc.sbuf_tensor("at_" + n, shape, dt))
        self.wd = sb("wd", [P, DT, D], F32)
        self.wu = sb("wu", [P, DT, D], F32)
        self.bu = sb("bu", [P, D], F32)
        self.bd = sb("bd", [P, 3, DT, P], F32)


def attention_setup(nc, w, k, W_down, toqueries, tokeys, tovalues, W_unify, b_unify):
    with ExitStack() as ctx:
        sem = lambda n: ctx.enter_context(nc.semaphore("as_" + n))
        s_z, s_in, s_bl, s_t, s_e = (sem(n) for n in ("z", "in", "bl", "t", "e"))
        raw = ctx.enter_context(nc.sbuf_tensor("as_raw", [P, 3, DT, P], F32))
        pt = ctx.enter_context(nc.psum_tensor("as_pt", [P, 2, 512], F32))
        block = ctx.enter_context(nc.Block())

        @block.gpsimd
        def _(eng):
            eng.memset(raw[:, :, :, :], 0.0).then_inc(s_z, 1)

        @block.sync
        def _(eng):
            eng.dma_start(w.wd[:, :, :], W_down.rearrange("(c p) n -> p c n", p=P)).then_inc(s_in, 16)
            eng.dma_start(w.wu[:, :, :], W_unify.rearrange("(c p) n -> p c n", p=P)).then_inc(s_in, 16)
            eng.dma_start(w.bu[:, :], b_unify.rearrange("(a e) -> a e", a=1).broadcast_to([P, D])).then_inc(s_in, 16)
            eng.wait_ge(s_z, 1)
            for m, a in enumerate((toqueries, tokeys, tovalues)):
                for h in range(HEADS):
                    r = HS * (h % 8)
                    eng.dma_start(raw[r:r + HS, m, h // 8, r:r + HS], a[h]).then_inc(s_bl, 16)
            eng.wait_ge(s_in, 48)

        @block.tensor
        def _(eng):
            eng.wait_ge(s_bl, 16 * 3 * HEADS)
            for q in range(3 * DT):
                mm = eng.transpose(pt[:, q // 4, (q % 4) * P:(q % 4 + 1) * P], raw[:, q // 2, q % 2, :], k.ident[:, :])
            mm.then_inc(s_t, 1)

        @block.vector
        def _(eng):
            eng.wait_ge(s_t, 1)
            for q in range(3 * DT):
                eng.tensor_copy(w.bd[:, q // 2, q % 2, :], pt[:, q // 4, (q % 4) * P:(q % 4 + 1) * P])


def attention(nc, k, w, x_in, x_out, NBAT):
    T = 1024
    NT = T // P
    NQ = 512
    RES = 4
    FILLS = 9
    ST = 2 * NT
    CH = GH * NT * 2
    scr = nc.dram_tensor("at_scr", (2, 3, D, T), BF16).ap()
    x_t, o_t = split_token_tiles(x_in), split_token_tiles(x_out)
    with ExitStack() as ctx:
        sb = lambda n, shape, dt: ctx.enter_context(nc.sbuf_tensor("at_" + n, shape, dt))
        ps = lambda n, shape: ctx.enter_context(nc.psum_tensor("at_" + n, shape, F32))
        xr = sb("xr", [P, NT, D], F32)
        xn = sb("xn", [P, NT, D], F32)
        xT = sb("xT", [P, DT, T], F32)
        xd = xn[:, :, :].rearrange("p t d -> p (t d)").rearrange("p (c t) -> p c t", c=DT)
        res = [sb(f"res{i}", [P, 512], F32) for i in range(RES)]
        parts = sb("parts", [P, 2, 3, DT, T], BF16)
        qa = [sb(f"qa{g}", [P, GH, T], BF16) for g in range(4)]
        ka = [sb(f"ka{g}", [P, GH, T], BF16) for g in range(4)]
        va = [sb(f"va{i}", [P, NT, HEADS, VW], F32) for i in range(2)]
        ex = [sb(f"ex{i}", [P, GH, NQ], F32) for i in range(2)]
        zeros = sb("zeros", [P, 1], F32)
        mxc = sb("mxc", [P, 2 * GH * NT], F32)
        nm = sb("nm", [P, GH * NT], F32)
        mparts = sb("mparts", [GH * NT, 3, P], BF16)
        os_ = sb("os", [P, NQ], F32)
        rec = sb("rec", [P, 4, GH], F32)
        ao = sb("ao", [P, NT, D], F32)
        aT = sb("aT", [P, DT, NQ], F32)
        xres = sb("xres", [P, NT, D], F32)
        yo = [sb(f"yo{i}", [P, 2, D], F32) for i in range(2)]
        norm = Norm(ctx, nc, k, "at_ln_")
        pb = [ps(f"pb{i}", [P, 512]) for i in range(2)]
        pd = [ps(f"pd{i}", [P, 2, 512]) for i in range(2)]
        po = ps("po", [P, 512])
        px = ps("px", [P, 512])

        S = lambda n: Sem(ctx, nc, "at_" + n)
        S = lambda n: Sem(ctx, nc, "at_" + n)
        s_one = ctx.enter_context(nc.semaphore("at_s_one"))
        s_xr = S("s_xr")
        s_xn = S("s_xn")
        s_ax = S("s_ax")
        s_ac = S("s_ac")
        s_hi = S("s_hi")
        s_mi = S("s_mi")
        s_lo = S("s_lo")
        s_scr = S("s_scr")
        s_ld = [S(f"s_ld{g}") for g in range(4)]
        s_mr = [S(f"s_mr{g}") for g in range(4)]
        s_b = S("s_b")
        s_mx = S("s_mx")
        s_nm = S("s_nm")
        s_d = S("s_d")
        s_ex = S("s_ex")
        s_pv = S("s_pv")
        s_o = S("s_o")
        s_rc = S("s_rc")
        s_xl = S("s_xl")
        s_xb = S("s_xb")
        s_st = [S(f"s_st{i}") for i in range(2)]

        XT = [("xT", c, f) for f in range(2) for c in range(DT)]
        XD = [("xd", c, f) for f in range(2) for c in range(DT)]
        QK = [("qk", m, c, f) for m in range(2) for c in range(DT) for f in range(2)]
        V = [("v", a) for a in range(NT // 2)]
        OUT = lambda f: [("aT", f, 0), ("aT", f, 1), ("u", f, 0), ("u", f, 1)]

        def task_at(g, t, prev, last):
            if t == 0:
                return None if last and g == 3 else ("mx",)
            if t % NT == NT - 1:
                return ("f", t // NT)
            table = {}
            if g == 0 and prev:
                table.update(zip((1, 2, 3, 4), OUT(1)))
            if g == 3:
                table.update(zip((9, 10, 11, 12), OUT(0)))
            if g == 0 and not last:
                table.update(zip((6, 8, 9, 10, 11, 12, 13, 14), XT + XD))
            if g == 1 and not last:
                table.update(zip((1, 2, 3, 4, 5, 6, 8, 9, 10, 11, 12, 13), QK + V))
            return table.get(t)

        class Aux:

            def __init__(self, task, b, par, g, n, ns, slot):
                self.kind, self.at = task[0], task[1:]
                self.b, self.par, self.g, self.n, self.ns, self.slot = b, par, g, n, ns, slot

        splits = lambda task: task[0] in ("qk", "mx")
        ROUND = [(g, bl) for bl, g in ((0, 1), (0, 2), (0, 3), (1, 0), (1, 1), (1, 2), (1, 3), (2, 0))]

        class Walk:

            def __init__(self, eng, do):
                self.n, self.ns, self.slot = 0, 0, 0
                do.start([self.next(task, 0, 0, 0) for task in XT + XD + QK + V + [("mx",)]])
                self.phase(do, 0, 0, 0, prev=False)
                n0, ns0 = self.n, self.ns
                tasks = [x for g, _ in ROUND for t in range(ST) if (x := task_at(g, t, True, False))]
                dn, dns = len(tasks), sum(map(splits, tasks))
                assert dns % RES == 0
                rounds = NBAT // 2 - 1
                with eng.Fori(0, rounds) as i:
                    self.n, self.ns = n0 + dn * i, ns0 + dns * i
                    for g, bl in ROUND:
                        self.phase(do, 2 * i + bl, bl % 2, g)
                self.n, self.ns = n0 + dn * rounds, ns0 + dns * rounds
                for g, bl in ROUND[:-1]:
                    self.phase(do, 2 * rounds + bl, bl, g, last=(bl == 1))
                do.end([self.next(task, NBAT - 1, 1, 0) for task in OUT(1)])

            def next(self, task, b, par, g):
                a = Aux(task, b, par, g, self.n, self.ns, self.slot)
                self.n = self.n + 1
                if splits(task):
                    self.ns, self.slot = self.ns + 1, (self.slot + 1) % RES
                return a

            def phase(self, do, b, par, g, prev=True, last=False):
                before = None
                for t in range(ST):
                    task = task_at(g, t, prev, last)
                    now, n, ns = None, self.n, self.ns
                    if task and task[0] in ("xT", "xd", "qk", "v"):
                        now = self.next(task, b + 1, 1 - par, g)
                    elif task and task[0] == "mx":
                        now = self.next(task, *((b, par, g + 1) if g < 3 else (b + 1, 1 - par, 0)))
                    elif task and task[0] in ("aT", "u") and g == 0:
                        now = self.next(task, b - 1, 1 - par, g)
                    elif task:
                        now = self.next(task, b, par, g)
                    do.step(b, par, g, t, n, ns, before, now, last)
                    before = now

        unit = lambda b, g: 4 * b + g
        block = ctx.enter_context(nc.Block())

        @block.sync
        def _(eng):
            for s in (s_xr, s_scr, *s_ld, *s_mr, s_xl, *s_st):
                s.open(eng)

            def load_rows(b):
                s_xn.wait(eng, 2 * b)
                eng.dma_start(xr[:, :, :], x_t[:, bass.ds(NT * b, NT), :]).then_inc(s_xr.sem, 16)

            def store_parts(b, ns):
                s_lo.wait(eng, ns)
                for g in range(4):
                    s_ld[g].wait(eng, 32 * SLOTS * b)
                for m in range(2):
                    for p in range(3):
                        eng.dma_start(scr[m, p].rearrange("(c r) t -> r c t", r=P),
                                      parts[:, m, p, :, :]).then_inc(s_scr.sem, 16)
                s_scr.wait(eng, 96 * (b + 1))

            def load_unit(b, g):
                if not (isinstance(b, int) and b == 0):
                    s_pv.wait(eng, ST * (unit(b, g) - 3))
                for m, (dst, order) in enumerate(((qa[g], Q_PARTS), (ka[g], K_PARTS))):
                    for s, p in enumerate(order):
                        src = scr[m, p, GH * HS * g:GH * HS * (g + 1), :].rearrange("(j r) t -> r j t", r=HS)
                        eng.dma_start(dst[HS * s:HS * (s + 1), :, :], src).then_inc(s_ld[g].sem, 16)

            def load_maxima(a):
                s_lo.wait(eng, a.ns + 1)
                for p in range(MROWS):
                    eng.dma_start(qa[a.g][KROWS + p:KROWS + p + 1, :, :].rearrange("a j (t q) -> a (j t) q", q=P),
                                  mparts[:, p, :]).then_inc(s_mr[a.g].sem, 16)

            def store_out(a):
                f, half = a.at
                s_ac.wait(eng, a.n + 1)
                eng.dma_start(o_t[:, bass.ds(NT * a.b + 4 * f + 2 * half, 2), :],
                              yo[half][:, :, :]).then_inc(s_st[half].sem, 16)

            class Do:
                def start(self, tasks):
                    load_rows(0)
                    store_parts(0, len(QK))
                    for g in range(3):
                        load_unit(0, g)
                    load_maxima(tasks[-1])

                def step(self, b, par, g, t, n, ns, before, now, last):
                    if t == 0:
                        if g == 0 and not last:
                            load_rows(b + 1)
                        if g == 2:
                            s_ac.wait(eng, n)
                            eng.dma_start(xres[:, :, :], x_t[:, bass.ds(NT * b, NT), :]).then_inc(s_xl.sem, 16)
                        if now:
                            load_maxima(now)
                        if g == 0:
                            load_unit(b, 3)
                        elif g > 1 and not last:
                            load_unit(b + 1, g - 1)
                    if g == 1 and t == 10 and not last:
                        store_parts(b + 1, ns)
                        load_unit(b + 1, 0)
                    if now and now.kind == "u":
                        store_out(now)

                def end(self, tasks):
                    for a in tasks[2:]:
                        store_out(a)
                    for s in s_st:
                        s.wait(eng, 16 * 2 * NBAT)

            Walk(eng, Do())

        @block.tensor
        def _(eng):
            for s in (s_ax, s_b, s_d, s_pv):
                s.open(eng)

            def scores_for_max(b, g, c):
                j, qt, kh = c // (2 * NT), (c // 2) % NT, c % 2
                if c == 0:
                    s_ld[g].wait(eng, 32 * SLOTS * (b + 1))
                s_mx.wait(eng, CH * unit(b, g) + c - 1)
                eng.matmul(pb[c % 2][:, :], qa[g][0:KROWS, j, qt * P:(qt + 1) * P],
                           ka[g][0:KROWS, j, kh * 512:(kh + 1) * 512], start=True, stop=True).then_inc(s_b.sem, 1)

            def scores(b, g, t, half):
                qh, kt = t // NT, t % NT
                if t == 0 and half == 0:
                    s_mr[g].wait(eng, 16 * MROWS * (b + 1))
                s_ex.wait(eng, 2 * (ST * unit(b, g) + t) + half - 1)
                for a in range(2):
                    j = 2 * half + a
                    mm = eng.matmul(pd[half][:, a, :], ka[g][0:KROWS + MROWS, j, kt * P:(kt + 1) * P],
                                    qa[g][0:KROWS + MROWS, j, qh * NQ:(qh + 1) * NQ], start=True, stop=True)
                mm.then_inc(s_d.sem, 1)

            def times_v(b, par, g, t):
                kt = t % NT
                if kt == 0:
                    s_o.wait(eng, 2 * unit(b, g) + t // NT)
                s_ex.wait(eng, 2 * (ST * unit(b, g) + t) + 2)
                for j in range(GH):
                    mm = eng.matmul(po[VW * j:VW * (j + 1), :], va[par][:, kt, GH * g + j, :], ex[t % 2][:, j, :],
                                    start=(kt == 0), stop=(kt == NT - 1), skip_group_check=True)
                mm.then_inc(s_pv.sem, 1)

            def aux(a):
                s_ac.wait(eng, a.n)
                turn = lambda src: [eng.transpose(px[:, j * P:(j + 1) * P], src(j), k.ident[:, :]) for j in range(4)][-1]
                if a.kind == "xT":
                    c, f = a.at
                    s_xn.wait(eng, 2 * a.b + f + 1)
                    mm = turn(lambda j: xn[:, 4 * f + j, c * P:(c + 1) * P])
                elif a.kind == "xd":
                    c, f = a.at
                    for d in range(DT):
                        mm = eng.matmul(px[:, :], w.wd[:, d, c * P:(c + 1) * P], xT[:, d, f * 512:(f + 1) * 512],
                                        start=(d == 0), stop=(d == DT - 1))
                elif a.kind == "qk":
                    m, c, f = a.at
                    mm = eng.matmul(px[:, :], w.bd[:, m, c, :], xd[:, c, f * 512:(f + 1) * 512], start=True, stop=True)
                elif a.kind == "v":
                    for i in range(2):
                        tile = 2 * a.at[0] + i
                        for c in range(DT):
                            mm = eng.matmul(px[:, i * D + c * P:i * D + (c + 1) * P], xd[:, c, tile * P:(tile + 1) * P],
                                            w.bd[:, 2, c, :], start=True, stop=True)
                elif a.kind == "mx":
                    s_nm.wait(eng, unit(a.b, a.g) + 1)
                    mm = eng.transpose(px[0:GH * NT, 0:P], nm[:, :], k.ident[:, :])
                elif a.kind == "f":
                    s_o.wait(eng, 2 * unit(a.b, a.g) + a.at[0] + 1)
                    mm = turn(lambda j: os_[:, j * P:(j + 1) * P])
                elif a.kind == "aT":
                    f, c = a.at
                    mm = turn(lambda j: ao[:, 4 * f + j, c * P:(c + 1) * P])
                elif a.kind == "u":
                    f, half = a.at
                    for i in range(2):
                        q = (2 * half + i) * P
                        for c in range(DT):
                            mm = eng.matmul(px[:, i * D:(i + 1) * D], aT[:, c, q:q + P], w.wu[:, c, :],
                                            start=(c == 0), stop=(c == DT - 1))
                mm.then_inc(s_ax.sem, 1)

            class Do:
                def start(self, tasks):
                    eng.wait_ge(s_one, FILLS)
                    for a in tasks[:-1]:
                        aux(a)
                    for c in range(CH):
                        scores_for_max(0, 0, c)
                    aux(tasks[-1])
                    for c in range(CH):
                        scores_for_max(0, 1, c)
                    for half in range(2):
                        scores(0, 0, 0, half)

                def step(self, b, par, g, t, n, ns, before, now, last):
                    b1, g1, t1 = (b, g, t + 1) if t < ST - 1 else (b, g + 1, 0) if g < 3 else (b + 1, 0, 0)
                    b2, g2 = (b, g + 2) if g < 2 else (b + 1, g - 2)
                    ahead = not (last and g > 1)
                    ends = last and g == 3 and t == ST - 1
                    for half in range(2):
                        if not ends:
                            scores(b1, g1, t1, half)
                        if half == 0 and ahead:
                            for c in (4 * t, 4 * t + 1):
                                scores_for_max(b2, g2, c)
                    times_v(b, par, g, t)
                    if ahead:
                        for c in (4 * t + 2, 4 * t + 3):
                            scores_for_max(b2, g2, c)
                    if now:
                        aux(now)

                def end(self, tasks):
                    for a in tasks:
                        aux(a)

            Walk(eng, Do())

        @block.scalar
        def _(eng):
            for s in (s_hi, s_ex, s_ac):
                s.open(eng)

            def aux(a):
                if a is None or a.kind in ("f", "u"):
                    return
                s_ax.wait(eng, a.n + 1)
                if a.kind == "qk":
                    m, c, f = a.at
                    s_scr.wait(eng, 96 * a.b)
                    eng.activation(parts[:, m, 0, c, f * 512:(f + 1) * 512], px[:, :], ACT.Copy,
                                   scale=SCALE).then_inc(s_hi.sem, 1)
                    return
                if a.kind == "mx":
                    s_mr[(a.g - 1) % 4].wait(eng, 16 * MROWS * (a.b + 1 if a.g else a.b))
                    eng.activation(mparts[:, 0, :], px[0:GH * NT, 0:P], ACT.Copy).then_inc(s_hi.sem, 1)
                    return
                if a.kind == "v":
                    for i in range(2):
                        ins = eng.activation(va[a.par][:, 2 * a.at[0] + i, :, 0:HS],
                                             px[:, i * D:(i + 1) * D].rearrange("p (h s) -> p h s", s=HS), ACT.Copy)
                elif a.kind == "aT":
                    ins = eng.activation(aT[:, a.at[1], :], px[:, :], ACT.Copy)
                else:
                    c, f = a.at
                    dst = xT if a.kind == "xT" else xd
                    ins = eng.activation(dst[:, c, f * 512:(f + 1) * 512], px[:, :], ACT.Copy)
                ins.then_inc(s_ac.sem, 1)

            class Do:
                def start(self, tasks):
                    eng.wait_ge(s_one, FILLS)
                    for a in tasks:
                        aux(a)

                def step(self, b, par, g, t, n, ns, before, now, last):
                    for half in range(2):
                        s_d.wait(eng, 2 * (ST * unit(b, g) + t) + half + 1)
                        eng.activation(ex[t % 2][:, 2 * half:2 * half + 2, :], pd[half][:, :, :],
                                       ACT.Exp).then_inc(s_ex.sem, 1)
                        if half == 0:
                            aux(before)

                def end(self, tasks):
                    for a in tasks:
                        aux(a)

            Walk(eng, Do())

        @block.vector
        def _(eng):
            norm.open_vector(eng)
            for s in (s_xn, s_mx, s_nm, s_o, s_rc):
                s.open(eng)

            def maxima(b, g, c):
                s_b.wait(eng, CH * unit(b, g) + c + 1)
                if c == 0:
                    s_nm.wait(eng, unit(b, g))
                eng.tensor_reduce(mxc[:, c:c + 1], pb[c % 2][:, :], AX.X, ALU.max).then_inc(s_mx.sem, 1)

            def negate(b, g, n):
                s_mx.wait(eng, CH * (unit(b, g) + 1))
                s_ax.wait(eng, n)
                eng.tensor_reduce(nm[:, :], mxc[:, :].rearrange("p (q h) -> p q h", h=2), AX.X, ALU.max,
                                  negate=True).then_inc(s_nm.sem, 1)

            def stats(b, f):
                s_xr.wait(eng, 16 * (b + 1))
                norm.stats_step(eng, 2 * b + f, xr[:, 4 * f:4 * f + 4, :], [P] * 4)

            def apply(b, f, n):
                s_ax.wait(eng, n)
                norm.apply_step(eng, 2 * b + f, xn[:, 4 * f:4 * f + 4, :], xr[:, 4 * f:4 * f + 4, :],
                                [P] * 4).then_inc(s_xn.sem, 1)

            def aux(a):
                if a is None or a.kind not in ("qk", "mx", "f", "u"):
                    return
                if a.kind in ("qk", "mx"):
                    s_hi.wait(eng, a.ns + 1)
                    s_lo.wait(eng, a.ns - RES + 1)
                    if a.kind == "qk":
                        m, c, f = a.at
                        eng.scalar_tensor_tensor(res[a.slot][:, :], px[:, :], SCALE,
                                                 parts[:, m, 0, c, f * 512:(f + 1) * 512],
                                                 ALU.mult, ALU.subtract).then_inc(s_ac.sem, 1)
                    else:
                        eng.tensor_tensor(res[a.slot][0:GH * NT, 0:P], px[0:GH * NT, 0:P], mparts[:, 0, :],
                                          ALU.subtract).then_inc(s_ac.sem, 1)
                    return
                s_ax.wait(eng, a.n + 1)
                if a.kind == "f":
                    u = unit(a.b, a.g)
                    v = px[:, :].rearrange("p (t j s) -> p t j s", t=4, j=GH)
                    eng.reciprocal(rec[:, :, :], v[:, :, :, HS]).then_inc(s_rc.sem, 1)
                    s_rc.wait(eng, 2 * u + a.at[0] + 1)
                    out = ao[:, 4 * a.at[0]:4 * a.at[0] + 4, GH * HS * a.g:GH * HS * (a.g + 1)]
                    ins = eng.tensor_tensor(out.rearrange("p t (j s) -> p t j s", j=GH), v[:, :, :, 0:HS],
                                            rec[:, :, :].unsqueeze(3).broadcast_to([P, 4, GH, HS]), ALU.mult)
                else:
                    f, half = a.at
                    s_xb.wait(eng, a.b + 1)
                    s_st[half].wait(eng, 16 * (2 * a.b + f))
                    r0 = 4 * f + 2 * half
                    ins = eng.tensor_tensor(yo[half][:, :, :], px[:, :].rearrange("p (t d) -> p t d", d=D),
                                            xres[:, r0:r0 + 2, :], ALU.add)
                ins.then_inc(s_ac.sem, 1)

            class Do:
                def start(self, tasks):
                    for f in range(2):
                        stats(0, f)
                        apply(0, f, 0)
                    for a in tasks[:-1]:
                        aux(a)
                    for g in range(2):
                        for c in range(CH):
                            maxima(0, g, c)
                        negate(0, g, len(tasks) if g else 0)
                        if g == 0:
                            aux(tasks[-1])

                def step(self, b, par, g, t, n, ns, before, now, last):
                    b2, g2 = (b, g + 2) if g < 2 else (b + 1, g - 2)
                    ahead = not (last and g > 1)
                    if ahead:
                        for c in (4 * t, 4 * t + 1):
                            maxima(b2, g2, c)
                    if before and before.kind != "f":
                        aux(before)
                    if t % NT == NT - 1:
                        s_pv.wait(eng, ST * unit(b, g) + t + 1)
                        s_ax.wait(eng, n)
                        eng.tensor_copy(os_[:, :], po[:, :]).then_inc(s_o.sem, 1)
                    if ahead:
                        for c in (4 * t + 2, 4 * t + 3):
                            maxima(b2, g2, c)
                        if t == ST - 1:
                            negate(b2, g2, n)
                    if now and now.kind == "f":
                        aux(now)
                    if g == 0 and not last and t in (2, 3, 4, 5):
                        if t % 2 == 0:
                            stats(b + 1, (t - 2) // 2)
                        else:
                            apply(b + 1, (t - 2) // 2, n)

                def end(self, tasks):
                    for a in tasks:
                        aux(a)

            Walk(eng, Do())

        @block.gpsimd
        def _(eng):
            norm.open_pool(eng)
            for s in (s_mi, s_lo, s_xb):
                s.open(eng)
            fills = [(zeros[:, :], 0.0)] + [(va[i][:, :, :, :], 0.0) for i in range(2)] + [
                (va[i][:, :, :, HS:HS + 1], 1.0) for i in range(2)] + [
                (ka[g][KROWS:KROWS + MROWS, :, :], 1.0) for g in range(4)]
            assert len(fills) == FILLS
            for i, (dst, value) in enumerate(fills):
                eng.wait_ge(s_one, i)
                eng.memset(dst, value).then_inc(s_one, 1)
            eng.wait_ge(s_one, FILLS)

            def aux(a):
                if a is None or not splits((a.kind,)):
                    return
                if a.kind == "qk":
                    m, c, f = a.at
                    mid, low = (parts[:, m, p, c, f * 512:(f + 1) * 512] for p in (1, 2))
                    r = res[a.slot][:, :]
                else:
                    mid, low = mparts[:, 1, :], mparts[:, 2, :]
                    r = res[a.slot][0:GH * NT, 0:P]
                s_ac.wait(eng, a.n + 1)
                eng.tensor_tensor(mid, r, zeros[0:r.shape[0], :].broadcast_to(list(r.shape)), ALU.add).then_inc(s_mi.sem, 1)
                s_mi.wait(eng, a.ns + 1)
                eng.tensor_tensor(low, r, mid, ALU.subtract).then_inc(s_lo.sem, 1)

            class Do:
                def start(self, tasks):
                    for f in range(2):
                        norm.pow_step(eng, f, 4)
                    for a in tasks:
                        aux(a)

                def step(self, b, par, g, t, n, ns, before, now, last):
                    if g == 0 and not last and t in (2, 4):
                        norm.pow_step(eng, 2 * (b + 1) + (t - 2) // 2, 4)
                    aux(before)
                    if g == 2 and t == 8:
                        s_xl.wait(eng, 16 * (b + 1))
                        for q in range(0, NT, 2):
                            ins = eng.tensor_tensor(xres[:, q:q + 2, :], xres[:, q:q + 2, :],
                                                    w.bu[:, :].unsqueeze(1).broadcast_to([P, 2, D]), ALU.add)
                        ins.then_inc(s_xb.sem, 1)

                def end(self, tasks):
                    pass

            Walk(eng, Do())


_INS = ["L0_attn_x", "L0_attn_W_down", "L0_attn_tokeys", "L0_attn_toqueries", "L0_attn_tovalues", "L0_attn_W_unify",
        "L0_attn_b_unify", "L0_ffn_router_w", "L0_ffn_router_b", "L0_ffn_w1", "L0_ffn_b1", "L0_ffn_w2", "L0_ffn_b2",
        "L0_ffn_ow1", "L0_ffn_ob1", "L0_ffn_ow2", "L0_ffn_ob2"]
STAGE = 0


def program(nc, x, W_down, tokeys, toqueries, tovalues, W_unify, b_unify, router_w, router_b, w1, b1, w2, b2,
            ow1, ob1, ow2, ob2, out):
    rows = lambda a: a.rearrange("b t d -> (b t) d")
    with ExitStack() as ctx:
        k = Consts(ctx, nc)
        setup(nc, k, router_w, router_b, b1, ob1)
        x1 = nc.dram_tensor("x1", (x.shape[0] * x.shape[1], D), F32).ap()
        x2 = nc.dram_tensor("x2", (x.shape[0] * x.shape[1], D), F32).ap()
        if STAGE == 1:
            ffn(nc, k, "f1_", rows(x), rows(out), w1, b2, w2, ow1, ow2, ob2)
        if STAGE == 0:
            ffn(nc, k, "f1_", rows(x), x1, w1, b2, w2, ow1, ow2, ob2)
        if STAGE != 1:
            with ExitStack() as c2:
                w = Heads(c2, nc)
                attention_setup(nc, w, k, W_down, toqueries, tokeys, tovalues, W_unify, b_unify)
                attention(nc, k, w, rows(x) if STAGE == 2 else x1, rows(out) if STAGE == 2 else x2, x.shape[0])
        if STAGE == 0:
            ffn(nc, k, "f2_", x2, rows(out), w1, b2, w2, ow1, ow2, ob2)


def kernel(**inputs):
    import numpy as np
    import concourse.bacc as bacc
    from concourse.bass_utils import run_bass_kernel_spmd

    nc = bacc.Bacc("TRN2", target_bir_lowering=False, num_devices=1)
    arrays, args = {}, []
    for name in _INS:
        a = np.ascontiguousarray(inputs[name])
        arrays[f"in_{name}"] = a
        args.append(nc.dram_tensor(f"in_{name}", a.shape, mybir.dt.from_np(a.dtype), kind="ExternalInput").ap())
    shape = inputs["L0_attn_x"].shape
    args.append(nc.dram_tensor("out_0", shape, F32, kind="ExternalOutput").ap())
    program(nc, *args)
    r = run_bass_kernel_spmd(nc, [arrays], core_ids=[0])
    return r.results[0]["out_0"]
```

```python
from contextlib import ExitStack

import concourse.bass as bass
from concourse import mybir

F32 = mybir.dt.float32
F32R = mybir.dt.float32r
BF16 = mybir.dt.bfloat16
I32 = mybir.dt.int32
ALU = mybir.AluOpType
ACT = mybir.ActivationFunctionType
AX = mybir.AxisListType

P = 128
D = 256
DT = D // P
H = 1024
HT = H // P
E = 8
C = 320
CCH = [(0, 128), (128, 128), (256, 64)]
EPS = 1e-5
CREDIT = 16


class Sem:

    def __init__(self, ctx, nc, name):
        self.sem = ctx.enter_context(nc.semaphore(name))

    def open(self, eng):
        eng.sem_inc(self.sem, CREDIT)

    def wait(self, eng, n):
        eng.wait_ge(self.sem, n + CREDIT)


def split_token_tiles(x):
    return x.rearrange("(t p) d -> p t d", p=P)


class Consts:

    def __init__(self, ctx, nc):
        sb = lambda name, shape, dt: ctx.enter_context(nc.sbuf_tensor(name, shape, dt))
        self.ident = sb("ident", [P, P], F32)
        self.tri = sb("tri", [P, P], F32)
        self.ones = sb("ones", [P, P], F32)
        self.esc = sb("esc", [P, E], F32)
        self.neghalf = sb("neghalf", [P, 32], F32)
        self.tokid = sb("tokid", [P, 64], I32)
        self.rw = sb("rw", [P, DT, E], F32)
        self.rb = sb("rb", [P, E], F32)
        self.b1T = sb("b1T", [P, E + 1, HT], F32)


def setup(nc, k, router_w, router_b, b1, ob1, w, attention_weights):
    with ExitStack() as ctx:
        sem = lambda n: ctx.enter_context(nc.semaphore(n))
        s_in, s_b, s_set, s_mk, s_t = (sem("su_" + n) for n in ("in", "b", "set", "mk", "t"))
        b1rows = ctx.enter_context(nc.sbuf_tensor("su_b1rows", [(E + 1) * HT, P], F32))
        pt = ctx.enter_context(nc.psum_tensor("su_pt", [P, 512], F32))
        block = ctx.enter_context(nc.Block())

        @block.sync
        def _(eng):
            eng.dma_start(b1rows[0:E * HT, :], b1.rearrange("e (c p) -> (e c) p", p=P)).then_inc(s_b, 16)
            eng.dma_start(b1rows[E * HT:, :], ob1.rearrange("(c p) -> c p", p=P)).then_inc(s_b, 16)
            eng.dma_start(k.rw[:, :, :], router_w.rearrange("(c p) e -> p c e", p=P)).then_inc(s_in, 16)
            eng.dma_start(k.rb[:, :], router_b.rearrange("(a e) -> a e", a=1).broadcast_to([P, E])).then_inc(s_in, 16)
            w.load(eng, *attention_weights)
            eng.wait_ge(s_in, 32)

        @block.gpsimd
        def _(eng):
            eng.memset(k.ident[:, :], 0.0).then_inc(s_set, 1)
            eng.memset(k.tri[:, :], 1.0).then_inc(s_set, 1)
            eng.memset(k.ones[:, :], 1.0)
            eng.memset(k.neghalf[:, :], -0.5)
            eng.iota(k.tokid[:, :], [[P, 64]], base=0, channel_multiplier=1)
            eng.iota(k.esc[:, :], [[-1, E]], base=E, channel_multiplier=0, allow_small_or_imprecise_dtypes=True)
            eng.wait_ge(s_set, 2)
            eng.affine_select(out=k.ident[:, :], in_=k.ident[:, :], compare_op=ALU.not_equal, fill=1.0,
                              base=0, pattern=[[-1, P]], channel_multiplier=1).then_inc(s_mk, 1)
            eng.affine_select(out=k.tri[:, :], in_=k.tri[:, :], compare_op=ALU.is_ge, fill=0.0,
                              base=0, pattern=[[1, P]], channel_multiplier=-1).then_inc(s_mk, 1)

        @block.tensor
        def _(eng):
            n = (E + 1) * HT
            eng.wait_ge(s_mk, 1)
            eng.wait_ge(s_b, 32)
            eng.transpose(pt[:, 0:n], b1rows[:, :], k.ident[0:n, 0:n]).then_inc(s_t, 1)

        @block.vector
        def _(eng):
            eng.wait_ge(s_t, 1)
            eng.tensor_copy(k.b1T[:, :, :].rearrange("p e c -> p (e c)"), pt[:, 0:(E + 1) * HT])


class Norm:

    def __init__(self, ctx, nc, k, name):
        sb = lambda n, shape: ctx.enter_context(nc.sbuf_tensor(name + n, shape, F32))
        self.k = k
        self.stats = sb("stats", [P, 4, 6])
        self.mv = sb("mv", [P, 4, 2])
        self.ve = sb("ve", [P, 4])
        self.rstd = sb("rstd", [P, 4])
        self.pad = sb("pad", [P, 1])
        self.s_dve = Sem(ctx, nc, name + "s_dve")
        self.s_pow = Sem(ctx, nc, name + "s_pow")

    def open_vector(self, eng):
        self.s_dve.open(eng)

    def open_pool(self, eng):
        self.s_pow.open(eng)

    def stats_step(self, eng, n, src, rows):
        last = None
        self.s_pow.wait(eng, n)
        self.s_dve.wait(eng, 3 * n)
        for j, r in enumerate(rows):
            last = eng.bn_stats(self.stats[0:r, j, :], src[0:r, j, :])
        last.then_inc(self.s_dve.sem, 1)
        self.s_dve.wait(eng, 3 * n + 1)
        eng.memset(self.pad[:, :], 0.0)
        for j, r in enumerate(rows):
            last = eng.bn_aggr(self.mv[0:r, j, :], self.stats[0:r, j, :])
        last.then_inc(self.s_dve.sem, 1)
        self.s_dve.wait(eng, 3 * n + 2)
        last = eng.tensor_scalar(self.ve[:, 0:len(rows)], self.mv[:, 0:len(rows), 1], EPS, None, ALU.add)
        last.then_inc(self.s_dve.sem, 1)

    def pow_step(self, eng, n, count):
        self.s_dve.wait(eng, 3 * n + 3)
        eng.tensor_tensor(self.rstd[:, 0:count], self.ve[:, 0:count], self.k.neghalf[:, 0:count],
                          ALU.pow).then_inc(self.s_pow.sem, 1)

    def apply_step(self, eng, n, dst, src, rows):
        self.s_pow.wait(eng, n + 1)
        last = None
        for j, r in enumerate(rows):
            last = eng.tensor_scalar(dst[0:r, j, :], src[0:r, j, :], self.mv[0:r, j, 0:1], self.rstd[0:r, j:j + 1],
                                     ALU.subtract, ALU.mult)
        return last


def router(nc, k, logits, name, x_in, b2s, b2, ob2):
    x_t = split_token_tiles(x_in)
    NB = x_t.shape[1] // 4
    with ExitStack() as ctx:
        sb = lambda n, shape, dt: ctx.enter_context(nc.sbuf_tensor(name + n, shape, dt))
        xr = [sb(f"xr{i}", [P, 4, D], F32) for i in range(2)]
        xn = [sb(f"xn{i}", [P, 4, D], F32) for i in range(2)]
        xT = [sb(f"xT{i}", [P, DT, 4 * P], F32) for i in range(2)]
        norm = Norm(ctx, nc, k, name + "ln_")
        pT = [[ctx.enter_context(nc.psum_tensor(name + f"pT{i}{f}", [P, 512], F32)) for f in range(DT)] for i in range(2)]
        S = lambda n: Sem(ctx, nc, name + n)
        s_ld = [S(f"s_ld{i}") for i in range(2)]
        s_xn = S("s_xn")
        s_tp = S("s_tp")
        s_ev = [S(f"s_ev{f}") for f in range(DT)]
        s_lg = S("s_lg")
        s_b2 = ctx.enter_context(nc.semaphore(name + "s_b2"))
        block = ctx.enter_context(nc.Block())

        @block.sync
        def _(eng):
            for s in s_ld:
                s.open(eng)
            with eng.Fori(0, NB // 2) as i:
                for b in range(2):
                    s_xn.wait(eng, 2 * i + b - 1)
                    eng.dma_start(xr[b][:, :, :], x_t[:, bass.ds(8 * i + 4 * b, 4), :]).then_inc(s_ld[b].sem, 16)
            for e in range(E):
                eng.dma_start(b2s[:, e, :], b2[e:e + 1, :].broadcast_to([P, D])).then_inc(s_b2, 16)
            eng.dma_start(b2s[:, E, :], ob2.rearrange("(a e) -> a e", a=1).broadcast_to([P, D])).then_inc(s_b2, 16)
            eng.wait_ge(s_b2, 16 * (E + 1))

        @block.gpsimd
        def _(eng):
            norm.open_pool(eng)
            with eng.Fori(0, NB) as n:
                norm.pow_step(eng, n, 4)

        @block.vector
        def _(eng):
            norm.open_vector(eng)
            s_xn.open(eng)
            s_ev[0].open(eng)

            def stats(i, n, b):
                s_ld[b].wait(eng, 16 * i + 16)
                norm.stats_step(eng, n, xr[b], [P] * 4)

            def apply(n, b):
                s_tp.wait(eng, 2 * n - 2)
                norm.apply_step(eng, n, xn[b], xr[b], [P] * 4).then_inc(s_xn.sem, 1)

            def evacuate(n, b):
                s_tp.wait(eng, 2 * n + 1)
                s_lg.wait(eng, n - 1)
                eng.tensor_copy(xT[b][:, 0, :], pT[b][0][:, :]).then_inc(s_ev[0].sem, 1)

            stats(0, 0, 0)
            apply(0, 0)
            stats(0, 1, 1)
            with eng.Fori(0, NB // 2 - 1) as i:
                for b in range(2):
                    n = 2 * i + b
                    apply(n + 1, 1 - b)
                    stats(i + 1, n + 2, b)
                    evacuate(n, b)
            apply(NB - 1, 1)
            evacuate(NB - 2, 0)
            evacuate(NB - 1, 1)

        @block.scalar
        def _(eng):
            s_ev[1].open(eng)
            with eng.Fori(0, NB // 2) as i:
                for b in range(2):
                    n = 2 * i + b
                    s_tp.wait(eng, 2 * n + 2)
                    s_lg.wait(eng, n - 1)
                    eng.activation(xT[b][:, 1, :], pT[b][1][:, :], ACT.Copy).then_inc(s_ev[1].sem, 1)

        @block.tensor
        def _(eng):
            s_tp.open(eng)
            s_lg.open(eng)

            def turn(n, b):
                s_xn.wait(eng, n + 1)
                for f in range(DT):
                    s_ev[f].wait(eng, n - 1)
                    for j in range(4):
                        mm = eng.transpose(pT[b][f][:, j * P:(j + 1) * P], xn[b][:, j, f * P:(f + 1) * P],
                                           k.ident[:, :])
                    mm.then_inc(s_tp.sem, 1)

            def products(n, b):
                for f in range(DT):
                    s_ev[f].wait(eng, n + 1)
                for j in range(4):
                    for f in range(DT):
                        mm = eng.matmul(logits[:, bass.ds((4 * n + j) * E, E)], xT[b][:, f, j * P:(j + 1) * P],
                                        k.rw[:, f, :], start=(f == 0), stop=(f == DT - 1))
                mm.then_inc(s_lg.sem, 1)

            turn(0, 0)
            with eng.Fori(0, NB // 2 - 1) as i:
                for b in range(2):
                    turn(2 * i + b + 1, 1 - b)
                    products(2 * i + b, b)
            turn(NB - 1, 1)
            products(NB - 2, 0)
            products(NB - 1, 1)


NO_TOKEN = 1 << 20


def decide(nc, k, put, logits, name, table, b2s):
    nt = 64
    with ExitStack() as ctx:
        sb = lambda n, shape, dt: ctx.enter_context(nc.sbuf_tensor(name + n, shape, dt))
        lg = sb("lg", [P, nt, E], F32)
        mx = sb("mx", [P, nt], F32)
        cand = sb("cand", [P, nt, E], F32)
        best = sb("best", [P, nt], F32)
        onehot = sb("onehot", [P, nt, E], F32)
        tot = sb("tot", [P, nt, E], F32)
        incl = sb("incl", [P, nt, E], F32)
        one_t = sb("one_t", [P, nt], F32)
        rank = sb("rank", [P, nt], F32)
        none = sb("none", [P, nt], F32)
        tmp = sb("tmp", [P, nt], F32)
        empty = sb("empty", [P, E * C // P], I32)
        pc = ctx.enter_context(nc.psum_tensor(name + "pc", [P, 512], F32))
        pt = ctx.enter_context(nc.psum_tensor(name + "pt", [P, 512], F32))
        sem = lambda n: ctx.enter_context(nc.semaphore(name + n))
        s_v, s_oh, s_mm, s_z, s_tab = sem("s_v"), sem("s_oh"), sem("s_mm"), sem("s_z"), sem("s_tab")
        block = ctx.enter_context(nc.Block())
        flat = lambda t: t[:, :, :].rearrange("p t e -> p (t e)")
        wide = lambda t: t[:, :].unsqueeze(2).broadcast_to([P, nt, E])
        each = lambda t: t[:, :].unsqueeze(1).broadcast_to([P, nt, E])

        @block.gpsimd
        def _(eng):
            eng.memset(empty[:, :], NO_TOKEN).then_inc(s_z, 1)

        @block.sync
        def _(eng):
            eng.wait_ge(s_z, 1)
            eng.dma_start(table.rearrange("(p c) a -> p (c a)", p=P), empty[:, :]).then_inc(s_tab, 16)
            eng.wait_ge(s_tab, 16)

        @block.tensor
        def _(eng):
            eng.wait_ge(s_oh, 1)
            eng.matmul(pc[:, :], k.tri[:, :], flat(onehot), start=True, stop=True)
            eng.matmul(pt[:, :], k.ones[:, :], flat(onehot), start=True, stop=True).then_inc(s_mm, 1)

        @block.vector
        def _(eng):
            n = 0

            def link(ins):
                nonlocal n
                n += 1
                ins.then_inc(s_v, 1)
                eng.wait_ge(s_v, n)

            link(eng.tensor_tensor(lg[:, :, :], logits[:, :].rearrange("p (t e) -> p t e", e=E), each(k.rb), ALU.add))
            link(eng.tensor_reduce(mx[:, :], lg[:, :, :], AX.X, ALU.max))
            link(eng.tensor_tensor(cand[:, :, :], lg[:, :, :], wide(mx), ALU.is_ge))
            link(eng.tensor_tensor(cand[:, :, :], cand[:, :, :], each(k.esc), ALU.mult))
            link(eng.tensor_reduce(best[:, :], cand[:, :, :], AX.X, ALU.max))
            eng.tensor_tensor(onehot[:, :, :], cand[:, :, :], wide(best), ALU.is_equal).then_inc(s_oh, 1)
            link(eng.memset(one_t[:, :], 1.0))
            eng.tensor_scalar(b2s[:, :, :], b2s[:, :, :], 0.5, None, ALU.mult)
            eng.wait_ge(s_mm, 1)
            for e in range(E):
                ins = eng.tensor_tensor_scan(tot[:, :, e], one_t[:, :], pt[:, e:512:E], 0.0, ALU.mult, ALU.add)
            link(ins)
            link(eng.tensor_tensor(flat(incl), pc[:, :], flat(tot), ALU.add))
            link(eng.scalar_tensor_tensor(flat(incl), pt[:, :], -1.0, flat(incl), ALU.mult, ALU.add))
            link(eng.tensor_tensor(flat(incl), flat(incl), flat(onehot), ALU.mult))
            link(eng.tensor_reduce(rank[:, :], incl[:, :, :], AX.X, ALU.add))
            link(eng.tensor_scalar(none[:, :], rank[:, :], float(C), float(2 * E * C), ALU.is_gt, ALU.mult))
            link(eng.tensor_scalar(tmp[:, :], best[:, :], -float(C), float(E * C - 1), ALU.mult, ALU.add))
            link(eng.tensor_tensor(tmp[:, :], tmp[:, :], rank[:, :], ALU.add))
            link(eng.tensor_tensor(tmp[:, :], tmp[:, :], none[:, :], ALU.add))
            link(eng.tensor_copy(put[:, :], tmp[:, :]))


def mlps(nc, k, put, name, x_in, x_out, b2s, w1, w2, ow1, ow2, table):
    x_t, o_t = split_token_tiles(x_in), split_token_tiles(x_out)
    NT = x_t.shape[1]
    NB = NT // 4
    RING = 4
    LAG = 3
    PIECES = 8
    WN = DT * H + HT * D
    PW = WN // PIECES
    HIGH = "VVVAAAAA"
    LOW = "VVVVVVVG"
    with ExitStack() as ctx:
        sb = lambda n, shape, dt: ctx.enter_context(nc.sbuf_tensor(name + n, shape, dt))
        xr = [sb(f"xr{i}", [P, 4, D], F32) for i in range(2)]
        xs = [sb(f"xs{i}", [P, 4, D], F32) for i in range(2)]
        xn = [sb(f"xn{i}", [P, 4, D], F32) for i in range(2)]
        xTh = [sb(f"xTh{i}", [P, DT, 512], F32R) for i in range(2)]
        xTl = [sb(f"xTl{i}", [P, DT, 512], F32R) for i in range(2)]
        h32 = [sb(f"h32{i}", [P, 512], F32) for i in range(2)]
        hh = [sb(f"hh{i}", [P, 512], F32R) for i in range(RING)]
        hl = [sb(f"hl{i}", [P, 512], F32R) for i in range(RING)]
        wraw = sb("wraw", [P, WN], F32)
        wh = [sb(f"wh{i}", [P, WN], F32R) for i in range(2)]
        wl = [sb(f"wl{i}", [P, WN], F32R) for i in range(2)]
        yo = [sb(f"yo{i}", [P, 4, D], F32) for i in range(2)]
        idx = sb("idx", [P, E, 3], I32)
        norm = Norm(ctx, nc, k, name + "ln_")
        pL = [ctx.enter_context(nc.psum_tensor(name + f"pL{i}", [P, 512], F32)) for i in range(2)]
        pA = [ctx.enter_context(nc.psum_tensor(name + f"pA{i}", [P, 2, 512], F32)) for i in range(2)]
        pT = [ctx.enter_context(nc.psum_tensor(name + f"pT{i}", [P, 512], F32)) for i in range(DT)]
        S = lambda n: Sem(ctx, nc, name + n)
        raw_sem = lambda n: ctx.enter_context(nc.semaphore(name + n))
        s_ld = [S(f"s_ld{i}") for i in range(2)]
        s_ga = [raw_sem(f"s_ga{i}") for i in range(2)]
        s_raw = [S(f"s_raw{i}") for i in range(PIECES)]
        s_st = [S(f"s_st{i}") for i in range(2)]
        s_sc = [raw_sem(f"s_sc{i}") for i in range(2)]
        s_put = raw_sem("s_put")
        s_idx = raw_sem("s_idx")
        s_xn = S("s_xn")
        s_xs = S("s_xs")
        s_tp = S("s_tp")
        s_thi = S("s_thi")
        s_tlo = S("s_tlo")
        s_l1 = S("s_l1")
        s_h = S("s_h")
        s_hi = S("s_hi")
        s_lo = S("s_lo")
        s_l2 = S("s_l2")
        s_y = S("s_y")
        s_wh = {who: S("s_wh" + who) for who in "VA"}
        s_wl = {who: S("s_wl" + who) for who in "VG"}

        def count(plan, who, m, q):
            return plan.count(who) * m + plan[:q + 1].count(who)

        W1 = lambda w, c, h: w[:, c * H + h * P:c * H + (h + 1) * P]
        W2 = lambda w, h: w[:, DT * H + h * D:DT * H + (h + 1) * D]
        chunks = {"dense": [(j * P, P) for j in range(4)], "expert": CCH}
        width = {"dense": 512, "expert": C}
        rows_of = {kind: [m for _, m in chunks[kind]] for kind in chunks}

        def stream(eng, prologue, block):
            prologue()
            with eng.Fori(0, NB // 2 - 1) as i:
                block(i, 2 * i, 0, "dense", "dense", "dense")
                block(i, 2 * i + 1, 1, "dense", "dense", "dense")
            block(NB // 2 - 1, NB - 2, 0, "dense", "dense", "expert")
            block(NB // 2 - 1, NB - 1, 1, "dense", "expert", "expert")
            with eng.Fori(0, E // 2 - 1) as i:
                block(i, NB + 2 * i, 0, "expert", "expert", "expert")
                block(i, NB + 2 * i + 1, 1, "expert", "expert", "expert")
            block(E // 2 - 1, NB + E - 2, 0, "expert", "expert", None)
            block(E // 2 - 1, NB + E - 1, 1, "expert", None, None)

        def split_at(i, n, b, kind):
            if kind == "expert":
                return None if isinstance(n, int) and n == NB + E - 1 else (2 * i + b + 2, b)
            return (1, 1) if isinstance(n, int) and n == NB - 2 else None

        def pieces_at(s):
            return [q for q in range(PIECES) if q * (HT - LAG) // PIECES == s]

        def pair_after(i, b, kind, other, ahead):
            if kind == other:
                return i + (b + ahead) // 2
            return 0

        wbuf = lambda b, kind: 0 if kind == "dense" else 1 - b

        block = ctx.enter_context(nc.Block())

        @block.sync
        def _(eng):
            for s in (*s_ld, *s_raw, *s_st):
                s.open(eng)

            def load_piece(m, q, a1, a2):
                s_wl[LOW[q]].wait(eng, count(LOW, LOW[q], m - 1, q))
                dst = wraw[:, q * PW:(q + 1) * PW]
                if q < PIECES // 2:
                    c, f = q // 2, q % 2
                    src = a1[c * P:(c + 1) * P, f * PW:(f + 1) * PW]
                else:
                    q2 = q - PIECES // 2
                    dst = dst.rearrange("p (c d) -> p c d", d=D)
                    src = a2[2 * q2 * P:(2 * q2 + 2) * P, :].rearrange("(c p) d -> p c d", p=P)
                eng.dma_start(dst, src).then_inc(s_raw[q].sem, 16)

            def of_expert(w, e):
                return w[bass.ds(e, 1), :, :].rearrange("a r c -> (a r) c")

            def load_rows(n, b):
                s_xn.wait(eng, n - 1)
                s_xs.wait(eng, n - 1)
                eng.dma_start(xr[b][:, :, :], x_t[:, bass.ds(4 * n, 4), :]).then_inc(s_ld[b].sem, 16)

            def store(n, b):
                s_y.wait(eng, n + 1)
                eng.dma_start(o_t[:, bass.ds(4 * n, 4), :], yo[b][:, :, :]).then_inc(s_st[b].sem, 16)

            load_rows(0, 0)
            for q in range(PIECES):
                load_piece(0, q, ow1, ow2)
            load_rows(1, 1)
            for q in range(PIECES):
                load_piece(1, q, w1[0], w2[0])
            load_rows(2, 0)
            load_rows(3, 1)
            with eng.Fori(0, NB // 2 - 2) as i:
                for b in range(2):
                    store(2 * i + b, b)
                    load_rows(2 * i + b + 4, b)
            eng.wait_ge(s_put, 16 * NT)
            slots = table.rearrange("(e c) a -> c e a", e=E)
            for j, (c0, m) in enumerate(CCH):
                eng.dma_start(idx[0:m, :, j:j + 1], slots[c0:c0 + m], allow_slow_non_contiguous=True).then_inc(s_idx, 16)
            store(NB - 4, 0)
            store(NB - 3, 1)
            for q in range(PIECES):
                load_piece(2, q, w1[1], w2[1])
            store(NB - 2, 0)
            store(NB - 1, 1)
            with eng.Fori(2, E) as e:
                for q in range(PIECES):
                    load_piece(e + 1, q, of_expert(w1, e), of_expert(w2, e))

        @block.gpsimd
        def _(eng):
            norm.open_pool(eng)
            s_xs.open(eng)
            s_wl["G"].open(eng)

            def with_bias(n):
                kind = "dense" if n < NB else "expert"
                e = E if n < NB else n - NB
                if n < NB:
                    s_ld[n % 2].wait(eng, 16 * (n // 2 + 1))
                else:
                    eng.wait_ge(s_ga[n % 2], 16 * len(CCH) * (e // 2 + 1))
                s_y.wait(eng, n - 1)
                for j in range(0, len(rows_of[kind]), 2):
                    w = min(2, len(rows_of[kind]) - j)
                    m = rows_of[kind][j]
                    ins = eng.tensor_tensor(xs[n % 2][0:m, j:j + w, :], xr[n % 2][0:m, j:j + w, :],
                                            b2s[0:m, e:e + 1, :].broadcast_to([m, w, D]), ALU.add)
                ins.then_inc(s_xs.sem, 1)

            def gather(e):
                n = NB + e
                if e == 0:
                    eng.wait_ge(s_idx, 16 * len(CCH))
                s_xn.wait(eng, n - 1)
                s_xs.wait(eng, n - 1)
                for j, (c0, m) in enumerate(CCH):
                    eng.indirect_dma_start(
                        out=xr[n % 2][0:m, j, :], out_offset=None, in_=x_in[:, :],
                        in_offset=bass.IndirectOffsetOnAxis(ap=idx[0:m, e, j:j + 1], axis=0),
                        bounds_check=NT * P - 1, oob_is_err=False).then_inc(s_ga[n % 2], 16)

            def scatter(e):
                if e == 0:
                    for s in s_st:
                        s.wait(eng, 16 * (NB // 2))
                s_y.wait(eng, NB + e + 1)
                for j, (c0, m) in enumerate(CCH):
                    eng.indirect_dma_start(
                        out=x_out[:, :], out_offset=bass.IndirectOffsetOnAxis(ap=idx[0:m, e, j:j + 1], axis=0),
                        in_=yo[e % 2][0:m, j, :], in_offset=None,
                        bounds_check=NT * P - 1, oob_is_err=False).then_inc(s_sc[e % 2], 16)

            def weights_low(m):
                for q in range(PIECES):
                    if LOW[q] == "G":
                        s_wh[HIGH[q]].wait(eng, count(HIGH, HIGH[q], m, q))
                        sl = slice(q * PW, (q + 1) * PW)
                        eng.tensor_tensor(wl[m % 2][:, sl], wraw[:, sl], wh[m % 2][:, sl].bitcast(F32),
                                          ALU.subtract).then_inc(s_wl["G"].sem, 1)

            norm.pow_step(eng, 0, 4)
            weights_low(0)
            norm.pow_step(eng, 1, 4)
            with_bias(0)
            PUTS = 2 * NT // NB
            for n in range(NB + E):
                if n >= NB - 2 and n + 2 < NB + E:
                    gather(n + 2 - NB)
                if n == NB - 2:
                    weights_low(1)
                elif NB <= n < NB + E - 1:
                    weights_low(n - NB + 2)
                if n + 2 < NB + E:
                    norm.pow_step(eng, n + 2, 4 if n + 2 < NB else 3)
                for t in range(PUTS * n, min(PUTS * (n + 1), NT)):
                    eng.indirect_dma_start(
                        out=table[:, :], out_offset=bass.IndirectOffsetOnAxis(ap=put[:, t:t + 1], axis=0),
                        in_=k.tokid[:, t:t + 1], in_offset=None,
                        bounds_check=E * C - 1, oob_is_err=False).then_inc(s_put, 16)
                if n + 1 < NB + E:
                    with_bias(n + 1)
                if n > NB:
                    scatter(n - NB - 1)
            scatter(E - 1)
            for s in s_sc:
                eng.wait_ge(s, 16 * len(CCH) * (E // 2))

        @block.vector
        def _(eng):
            norm.open_vector(eng)
            for s in (s_xn, s_tlo, s_lo, s_y, s_wh["V"], s_wl["V"]):
                s.open(eng)

            def stats(i, n, b, kind):
                if kind == "dense":
                    s_ld[b].wait(eng, 16 * i + 16)
                else:
                    eng.wait_ge(s_ga[b], 16 * len(CCH) * (i + 1))
                norm.stats_step(eng, n, xr[b], rows_of[kind])

            def apply(n, b, kind):
                s_tp.wait(eng, 2 * n - 2)
                norm.apply_step(eng, n, xn[b], xr[b], rows_of[kind]).then_inc(s_xn.sem, 1)

            def rows_low(n, b, f, w):
                s_thi.wait(eng, 2 * n + f + 1)
                eng.tensor_tensor(xTl[b][:, f, 0:w], pT[f][:, 0:w], xTh[b][:, f, 0:w].bitcast(F32),
                                  ALU.subtract).then_inc(s_tlo.sem, 1)

            def hidden_low(n, h, w):
                s_hi.wait(eng, HT * n + h + 1)
                eng.tensor_tensor(hl[h % RING][:, 0:w], h32[h % 2][:, 0:w], hh[h % RING][:, 0:w].bitcast(F32),
                                  ALU.subtract).then_inc(s_lo.sem, 1)

            def weights(m, buf, q, n):
                sl = slice(q * PW, (q + 1) * PW)
                if HIGH[q] == "V":
                    s_raw[q].wait(eng, 16 * m + 16)
                    if n is not None:
                        s_l2.wait(eng, HT * n)
                    eng.tensor_copy(wh[buf][:, sl], wraw[:, sl]).then_inc(s_wh["V"].sem, 1)
                if LOW[q] == "V":
                    s_wh[HIGH[q]].wait(eng, count(HIGH, HIGH[q], m, q))
                    eng.tensor_tensor(wl[buf][:, sl], wraw[:, sl], wh[buf][:, sl].bitcast(F32),
                                      ALU.subtract).then_inc(s_wl["V"].sem, 1)

            def results(i, n, b, kind):
                s_l2.wait(eng, HT * (n + 1))
                s_xs.wait(eng, n + 1)
                if kind == "dense":
                    s_st[b].wait(eng, 16 * i)
                else:
                    s_st[b].wait(eng, 16 * (NB // 2))
                    eng.wait_ge(s_sc[b], 16 * len(CCH) * i)
                for j in range(0, len(rows_of[kind]), 2):
                    m, w = rows_of[kind][j], min(2, len(rows_of[kind]) - j)
                    ins = eng.scalar_tensor_tensor(
                        yo[b][0:m, j:j + w, :], pA[b][0:m, j // 2, 0:w * D].rearrange("p (t d) -> p t d", d=D), 0.5,
                        xs[b][0:m, j:j + w, :], ALU.mult, ALU.add)
                ins.then_inc(s_y.sem, 1)

            def prologue():
                for n in range(2):
                    stats(0, n, n, "dense")
                    apply(n, n, "dense")
                    if n == 0:
                        for f in range(DT):
                            rows_low(0, 0, f, 512)
                        for q in range(PIECES):
                            weights(0, 0, q, None)
                for h in range(LAG):
                    hidden_low(0, h, 512)

            def block_(i, n, b, kind, nxt, nxt2):
                sp = split_at(i, n, b, kind)
                for s in range(HT):
                    if nxt and s in (0, 2):
                        rows_low(n + 1, 1 - b, s // 2, width[nxt])
                    if s + LAG < HT:
                        hidden_low(n, s + LAG, width[kind])
                    elif nxt:
                        hidden_low(n + 1, s + LAG - HT, width[nxt])
                    for q in pieces_at(s) if sp else ():
                        weights(sp[0], sp[1], q, n if q == 0 else None)
                    if nxt2 and s == 4:
                        stats(pair_after(i, b, kind, nxt2, 2), n + 2, b, nxt2)
                    if nxt2 and s == 6:
                        apply(n + 2, b, nxt2)
                results(i, n, b, kind)

            stream(eng, prologue, block_)

        @block.scalar
        def _(eng):
            for t in (s_thi, s_h, s_hi, s_wh["A"]):
                t.open(eng)

            def rows_high(n, b, f, w):
                s_tp.wait(eng, 2 * n + f + 1)
                s_l1.wait(eng, HT * (n - 1))
                eng.activation(xTh[b][:, f, 0:w], pT[f][:, 0:w], ACT.Copy).then_inc(s_thi.sem, 1)

            def hidden_high(i, n, b, kind, h):
                w = width[kind]
                g = HT * n + h
                bias = k.b1T[:, E, h:h + 1] if kind == "dense" else k.b1T[:, bass.ds(2 * i + b, 1), h]
                s_l1.wait(eng, g + 1)
                s_lo.wait(eng, g - 1)
                eng.activation(h32[h % 2][:, 0:w], pL[h % 2][:, 0:w], ACT.Relu, bias=bias).then_inc(s_h.sem, 1)
                s_h.wait(eng, g + 1)
                s_l2.wait(eng, g - RING + 1)
                eng.activation(hh[h % RING][:, 0:w], h32[h % 2][:, 0:w], ACT.Copy).then_inc(s_hi.sem, 1)

            def weights_high(m, buf, q, n):
                if HIGH[q] == "A":
                    s_raw[q].wait(eng, 16 * m + 16)
                    if n is not None:
                        s_l2.wait(eng, HT * n)
                    sl = slice(q * PW, (q + 1) * PW)
                    eng.activation(wh[buf][:, sl], wraw[:, sl], ACT.Copy).then_inc(s_wh["A"].sem, 1)

            def prologue():
                for f in range(DT):
                    rows_high(0, 0, f, 512)
                for q in range(PIECES):
                    weights_high(0, 0, q, None)
                for h in range(LAG):
                    hidden_high(0, 0, 0, "dense", h)

            def block_(i, n, b, kind, nxt, nxt2):
                sp = split_at(i, n, b, kind)
                i1 = pair_after(i, b, kind, nxt, 1)
                for s in range(HT):
                    if nxt and s in (0, 2):
                        rows_high(n + 1, 1 - b, s // 2, width[nxt])
                    if s + LAG < HT:
                        hidden_high(i, n, b, kind, s + LAG)
                    elif nxt:
                        hidden_high(i1, n + 1, 1 - b, nxt, s + LAG - HT)
                    for q in pieces_at(s) if sp else ():
                        weights_high(sp[0], sp[1], q, n)

            stream(eng, prologue, block_)

        @block.tensor
        def _(eng):
            for t in (s_tp, s_l1, s_l2):
                t.open(eng)

            def turn(n, b, kind, f):
                s_xn.wait(eng, n + 1)
                s_tlo.wait(eng, 2 * (n - 1) + f + 1)
                for j, (c0, m) in enumerate(chunks[kind]):
                    mm = eng.transpose(pT[f][:, c0:c0 + m], xn[b][0:m, j, f * P:(f + 1) * P], k.ident[0:m, 0:m])
                mm.then_inc(s_tp.sem, 1)

            def into_hidden(n, b, kind, h):
                w, wb = width[kind], wbuf(b, kind)
                if h == 0:
                    s_tlo.wait(eng, 2 * n + 2)
                s_h.wait(eng, HT * n + h - 1)
                out = pL[h % 2][:, 0:w]
                for c in range(DT):
                    eng.matmul(out, W1(wh[wb], c, h), xTh[b][:, c, 0:w], start=(c == 0), stop=False)
                    eng.matmul(out, W1(wh[wb], c, h), xTl[b][:, c, 0:w], start=False, stop=False)
                    mm = eng.matmul(out, W1(wl[wb], c, h), xTh[b][:, c, 0:w], start=False, stop=(c == DT - 1))
                mm.then_inc(s_l1.sem, 1)

            def out_of_hidden(n, b, kind, h):
                wb = wbuf(b, kind)
                s_lo.wait(eng, HT * n + h + 1)
                if h == 0:
                    s_y.wait(eng, n - 1)
                for j, (c0, m) in enumerate(chunks[kind]):
                    out = pA[b][0:m, j // 2, (j % 2) * D:(j % 2 + 1) * D]
                    hi, lo = hh[h % RING][:, c0:c0 + m], hl[h % RING][:, c0:c0 + m]
                    eng.matmul(out, hi, W2(wh[wb], h), start=(h == 0 and j % 2 == 0), stop=False,
                               skip_group_check=True)
                    eng.matmul(out, hi, W2(wl[wb], h), start=False, stop=False, skip_group_check=True)
                    mm = eng.matmul(out, lo, W2(wh[wb], h), start=False, stop=(h == HT - 1), skip_group_check=True)
                mm.then_inc(s_l2.sem, 1)

            def weights_ready(m):
                for who in "VG":
                    s_wl[who].wait(eng, LOW.count(who) * (m + 1))

            def prologue():
                for f in range(DT):
                    turn(0, 0, "dense", f)
                weights_ready(0)
                for h in range(LAG):
                    into_hidden(0, 0, "dense", h)

            def block_(i, n, b, kind, nxt, nxt2):
                for s in range(HT):
                    if nxt and s in (0, 2):
                        turn(n + 1, 1 - b, nxt, s // 2)
                    out_of_hidden(n, b, kind, s)
                    if s + LAG < HT:
                        into_hidden(n, b, kind, s + LAG)
                    elif nxt:
                        if nxt == "expert" and s + LAG == HT:
                            weights_ready(n + 1 - NB + 1)
                        into_hidden(n + 1, 1 - b, nxt, s + LAG - HT)

            stream(eng, prologue, block_)


def ffn(nc, k, name, x_in, x_out, w1, b2, w2, ow1, ow2, ob2):
    table = nc.dram_tensor(name + "table", (E * C, 1), I32).ap()
    with ExitStack() as ctx:
        put = ctx.enter_context(nc.sbuf_tensor(name + "put", [P, 64], I32))
        b2s = ctx.enter_context(nc.sbuf_tensor(name + "b2s", [P, E + 1, D], F32))
        with nc.psum_tensor(name + "logits", [P, 64 * E], F32) as logits:
            router(nc, k, logits, name + "ro_", x_in, b2s, b2, ob2)
            decide(nc, k, put, logits, name + "de_", table, b2s)
        mlps(nc, k, put, name + "ml_", x_in, x_out, b2s, w1, w2, ow1, ow2, table)


HEADS = 16
HS = D // HEADS
GH = 4
VW = 32
SLOTS = 6
Q_PARTS = [0, 1, 2, 0, 1, 0]
K_PARTS = [0, 0, 0, 1, 1, 2]
KROWS = SLOTS * HS
SCALE = float(HS) ** -0.25
MROWS = 3


class Heads:

    def __init__(self, ctx, nc):
        sb = lambda name, shape, dt: ctx.enter_context(nc.sbuf_tensor("at_" + name, shape, dt))
        self.wd = sb("wd", [P, DT, D], F32)
        self.wu = sb("wu", [P, DT, D], F32)
        self.bu = sb("bu", [P, D], F32)
        self.raw = sb("raw", [P, 3, DT, HS], F32)
        self.bd = sb("bd", [P, 3, DT, P], F32)
        self.s_in = ctx.enter_context(nc.semaphore("at_s_in"))

    LOADS = 3 + 3

    def load(self, eng, W_down, toqueries, tokeys, tovalues, W_unify, b_unify):
        eng.dma_start(self.wd[:, :, :], W_down.rearrange("(c p) n -> p c n", p=P)).then_inc(self.s_in, 16)
        eng.dma_start(self.wu[:, :, :], W_unify.rearrange("(c p) n -> p c n", p=P)).then_inc(self.s_in, 16)
        eng.dma_start(self.bu[:, :], b_unify.rearrange("(a e) -> a e", a=1).broadcast_to([P, D])).then_inc(self.s_in, 16)
        for m, a in enumerate((toqueries, tokeys, tovalues)):
            eng.dma_start(self.raw[:, m, :, :],
                          a.rearrange("(c h) i k -> (h i) c k", c=DT)).then_inc(self.s_in, 16)


def attention_setup(nc, w, k):
    with ExitStack() as ctx:
        sem = lambda n: ctx.enter_context(nc.semaphore("as_" + n))
        s_m, s_v, s_t = sem("m"), sem("v"), sem("t")
        ones = ctx.enter_context(nc.sbuf_tensor("as_ones", [P, 8, HS], F32))
        mask = ctx.enter_context(nc.sbuf_tensor("as_mask", [P, 8, HS], F32))
        diag = ctx.enter_context(nc.sbuf_tensor("as_diag", [P, 3 * DT, 8, HS], F32))
        pt = ctx.enter_context(nc.psum_tensor("as_pt", [P, 2, 512], F32))
        block = ctx.enter_context(nc.Block())

        @block.gpsimd
        def _(eng):
            eng.memset(ones[:, :, :], 1.0).then_inc(s_m, 1)
            eng.wait_ge(s_m, 1)
            eng.affine_select(out=mask[:, :, :], in_=ones[:, :, :], compare_op=ALU.is_ge, fill=0.0,
                              base=0, pattern=[[-HS, 8], [0, HS]], channel_multiplier=1).then_inc(s_m, 1)
            eng.wait_ge(s_m, 2)
            eng.affine_select(out=mask[:, :, :], in_=mask[:, :, :], compare_op=ALU.is_ge, fill=0.0,
                              base=HS - 1, pattern=[[HS, 8], [0, HS]], channel_multiplier=-1).then_inc(s_m, 1)

        @block.tensor
        def _(eng):
            for q in range(3 * DT):
                eng.wait_ge(s_v, q + 1)
                mm = eng.transpose(pt[:, q // 4, (q % 4) * P:(q % 4 + 1) * P],
                                   diag[:, q, :, :].rearrange("p h s -> p (h s)"), k.ident[:, :])
            mm.then_inc(s_t, 1)

        @block.vector
        def _(eng):
            eng.wait_ge(s_m, 3)
            eng.wait_ge(w.s_in, 16 * w.LOADS)
            for q in range(3 * DT):
                eng.tensor_tensor(diag[:, q, :, :], w.raw[:, q // DT, q % DT, :].unsqueeze(1).broadcast_to([P, 8, HS]),
                                  mask[:, :, :], ALU.mult).then_inc(s_v, 1)
            eng.wait_ge(s_t, 1)
            for q in range(3 * DT):
                eng.tensor_copy(w.bd[:, q // DT, q % DT, :], pt[:, q // 4, (q % 4) * P:(q % 4 + 1) * P])


def attention(nc, k, w, x_in, x_out, NBAT):
    T = 1024
    NT = T // P
    NQ = 512
    RES = 4
    ST = 2 * NT
    CH = GH * NT
    ULOADS = 3 * SLOTS
    MR = GH * NT // 2
    scr = nc.dram_tensor("at_scr", (2, 3, D, T), BF16).ap()
    x_t, o_t = split_token_tiles(x_in), split_token_tiles(x_out)
    with ExitStack() as ctx:
        sb = lambda n, shape, dt: ctx.enter_context(nc.sbuf_tensor("at_" + n, shape, dt))
        ps = lambda n, shape: ctx.enter_context(nc.psum_tensor("at_" + n, shape, F32))
        xr = sb("xr", [P, NT, D], F32)
        xn = sb("xn", [P, NT, D], F32)
        xT = sb("xT", [P, DT, T], F32)
        xd = xn[:, :, :].rearrange("p t d -> p (t d)").rearrange("p (c t) -> p c t", c=DT)
        res = [sb(f"res{i}", [P, 512], F32) for i in range(RES)]
        parts = sb("parts", [P, 2, 3, DT, T], BF16)
        qa = [sb(f"qa{g}", [P, 2, GH, NQ], BF16) for g in range(4)]
        ka = [sb(f"ka{g}", [P, GH, T], BF16) for g in range(4)]
        va = [sb(f"va{i}", [P, NT, HEADS, VW], F32) for i in range(2)]
        ex = [sb(f"ex{i}", [P, GH, NQ], F32) for i in range(2)]
        zeros = sb("zeros", [P, 1], F32)
        mxc = sb("mxc", [P, CH], F32)
        nm = sb("nm", [P, MR], F32)
        mparts = sb("mparts", [MR, 3, P], BF16)
        os_ = sb("os", [P, NQ], F32)
        rec = sb("rec", [P, 4, GH], F32)
        ao = sb("ao", [P, NT, D], F32)
        aT = sb("aT", [P, DT, NQ], F32)
        xres = sb("xres", [P, NT, D], F32)
        yo = [sb(f"yo{i}", [P, 2, D], F32) for i in range(2)]
        norm = Norm(ctx, nc, k, "at_ln_")
        pb = [ps(f"pb{i}", [P, 512]) for i in range(2)]
        pd = [ps(f"pd{i}", [P, 2, 512]) for i in range(2)]
        po = ps("po", [P, 512])
        px = ps("px", [P, 512])

        S = lambda n: Sem(ctx, nc, "at_" + n)
        s_one = ctx.enter_context(nc.semaphore("at_s_one"))
        s_zero = ctx.enter_context(nc.semaphore("at_s_zero"))
        s_xr = S("s_xr")
        s_xn = S("s_xn")
        s_ax = S("s_ax")
        s_ac = S("s_ac")
        s_hi = S("s_hi")
        s_mi = S("s_mi")
        s_lo = S("s_lo")
        s_scr = S("s_scr")
        s_ld = [S(f"s_ld{g}") for g in range(4)]
        s_mr = [S(f"s_mr{g}") for g in range(4)]
        s_b = S("s_b")
        s_mx = S("s_mx")
        s_nm = S("s_nm")
        s_d = S("s_d")
        s_ex = S("s_ex")
        s_pv = S("s_pv")
        s_o = S("s_o")
        s_rc = S("s_rc")
        s_xl = S("s_xl")
        s_xb = S("s_xb")
        s_st = [S(f"s_st{i}") for i in range(2)]

        XT = [("xT", c, f) for f in range(2) for c in range(DT)]
        XD = [("xd", c, f) for f in range(2) for c in range(DT)]
        QK = [("qk", m, c, f) for m in range(2) for c in range(DT) for f in range(2)]
        V = [("v", a) for a in range(NT // 2)]
        OUT = lambda f: [("aT", f, 0), ("aT", f, 1), ("u", f, 0), ("u", f, 1)]

        def task_at(g, t, prev, last):
            table = {0: ("f", 1), 8: ("f", 0), 2: ("mx", 1), 10: ("mx", 0)}
            if g == 0 and not prev:
                del table[0]
            if g == 3 and last:
                del table[10]
            if g == 0 and prev:
                table.update(zip((1, 3, 4, 5), OUT(1)))
            if g == 3:
                table.update(zip((9, 11, 12, 13), OUT(0)))
            if g == 0 and not last:
                table.update(zip((6, 7, 9, 11, 12, 13, 14), XT + XD))
            if g == 1 and not last:
                table.update(zip((1, 3, 5, 7, 9, 11, 13), XD[-1:] + QK))
            if g == 2 and not last:
                table.update(zip((1, 3, 4, 5, 6, 7), QK[-2:] + V))
            return table.get(t)

        class Aux:

            def __init__(self, task, b, par, g, n, ns, slot):
                self.kind, self.at = task[0], task[1:]
                self.b, self.par, self.g, self.n, self.ns, self.slot = b, par, g, n, ns, slot
                self.bank, self.slack = px, 0

        splits = lambda task: task[0] in ("qk", "mx")
        ROUND = [(g, bl) for bl, g in ((0, 1), (0, 2), (0, 3), (1, 0), (1, 1), (1, 2), (1, 3), (2, 0))]

        class Walk:

            def __init__(self, eng, do):
                self.n, self.ns, self.slot = 0, 0, 0
                first = [self.next(task, 0, 0, 0) for task in XT + XD + QK + V + [("mx", 0)]]
                for a, b in zip(first[1:], first):
                    a.bank = po if a.n % 2 and a.kind != "mx" else px
                    a.slack = 1 if a.kind == b.kind or a.kind in ("xd", "qk") else 0
                do.start(first)
                self.phase(do, 0, 0, 0, prev=False)
                n0, ns0 = self.n, self.ns
                tasks = [x for g, _ in ROUND for t in range(ST) if (x := task_at(g, t, True, False))]
                dn, dns = len(tasks), sum(map(splits, tasks))
                assert dns % RES == 0
                rounds = NBAT // 2 - 1
                with eng.Fori(0, rounds) as i:
                    self.n, self.ns = n0 + dn * i, ns0 + dns * i
                    for g, bl in ROUND:
                        self.phase(do, 2 * i + bl, bl % 2, g)
                self.n, self.ns = n0 + dn * rounds, ns0 + dns * rounds
                for g, bl in ROUND[:-1]:
                    self.phase(do, 2 * rounds + bl, bl, g, last=(bl == 1))
                do.end([self.next(task, NBAT - 1, 1, 3) for task in [("f", 1)] + OUT(1)])

            def next(self, task, b, par, g):
                a = Aux(task, b, par, g, self.n, self.ns, self.slot)
                self.n = self.n + 1
                if splits(task):
                    self.ns, self.slot = self.ns + 1, (self.slot + 1) % RES
                return a

            def phase(self, do, b, par, g, prev=True, last=False):
                before = None
                for t in range(ST):
                    task = task_at(g, t, prev, last)
                    now, n, ns = None, self.n, self.ns
                    if task and task[0] in ("xT", "xd", "qk", "v"):
                        now = self.next(task, b + 1, 1 - par, g)
                    elif task == ("mx", 0):
                        now = self.next(task, *((b, par, g + 1) if g < 3 else (b + 1, 1 - par, 0)))
                    elif task == ("f", 1):
                        now = self.next(task, *((b, par, g - 1) if g > 0 else (b - 1, 1 - par, 3)))
                    elif task and task[0] in ("aT", "u") and g == 0:
                        now = self.next(task, b - 1, 1 - par, g)
                    elif task:
                        now = self.next(task, b, par, g)
                    do.step(b, par, g, t, n, ns, before, now, last)
                    before = now

        unit = lambda b, g: 4 * b + g
        next_unit = lambda b, g: (b, g + 1) if g < 3 else (b + 1, 0)
        block = ctx.enter_context(nc.Block())

        @block.sync
        def _(eng):
            for s in (s_xr, s_scr, *s_ld, *s_mr, s_xl, *s_st):
                s.open(eng)

            def load_rows(b):
                s_xn.wait(eng, 2 * b)
                eng.dma_start(xr[:, :, :], x_t[:, bass.ds(NT * b, NT), :]).then_inc(s_xr.sem, 16)

            def store_parts(b, ns, keys=None):
                s_lo.wait(eng, ns)
                for g in range(4):
                    s_ld[g].wait(eng, 16 * ULOADS * b)
                for m in range(2):
                    if m == 1 and keys:
                        s_lo.wait(eng, keys)
                    for p in range(3):
                        eng.dma_start(scr[m, p].rearrange("(c r) t -> r c t", r=P),
                                      parts[:, m, p, :, :]).then_inc(s_scr.sem, 16)
                s_scr.wait(eng, 96 * (b + 1))

            def load_unit(b, g):
                if not (isinstance(b, int) and b == 0):
                    s_pv.wait(eng, ST * (unit(b, g) - 3))
                for m, dst, order, t0, t1 in ((0, qa[g][:, 0, :, :], Q_PARTS, 0, NQ), (1, ka[g], K_PARTS, 0, T),
                                              (0, qa[g][:, 1, :, :], Q_PARTS, NQ, T)):
                    for s, p in enumerate(order):
                        src = scr[m, p, GH * HS * g:GH * HS * (g + 1), t0:t1].rearrange("(j r) t -> r j t", r=HS)
                        eng.dma_start(dst[HS * s:HS * (s + 1), :, :], src).then_inc(s_ld[g].sem, 16)

            def load_maxima(a):
                s_lo.wait(eng, a.ns + 1)
                for p in range(MROWS):
                    eng.dma_start(qa[a.g][KROWS + p:KROWS + p + 1, a.at[0], :, :].rearrange("a j (t q) -> a (j t) q", q=P),
                                  mparts[:, p, :]).then_inc(s_mr[a.g].sem, 16)

            def store_out(a):
                f, half = a.at
                s_ac.wait(eng, a.n + 1)
                eng.dma_start(o_t[:, bass.ds(NT * a.b + 4 * f + 2 * half, 2), :],
                              yo[half][:, :, :]).then_inc(s_st[half].sem, 16)

            class Do:
                def start(self, tasks):
                    load_rows(0)
                    store_parts(0, len(QK) // 2, keys=len(QK))
                    for g in range(2):
                        load_unit(0, g)
                    load_maxima(tasks[-1])

                def step(self, b, par, g, t, n, ns, before, now, last):
                    if t == 0:
                        if g == 0 and not last:
                            load_rows(b + 1)
                        if g == 2:
                            s_ac.wait(eng, n)
                            eng.dma_start(xres[:, :, :], x_t[:, bass.ds(NT * b, NT), :]).then_inc(s_xl.sem, 16)
                    if now and now.kind == "mx":
                        load_maxima(now)
                    if t == 3:
                        if g < 2:
                            load_unit(b, g + 2)
                        elif g == 3 and not last:
                            load_unit(b + 1, 1)
                    if g == 2 and t == 5 and not last:
                        store_parts(b + 1, ns)
                        load_unit(b + 1, 0)
                    if now and now.kind == "u":
                        store_out(now)

                def end(self, tasks):
                    for a in tasks[3:]:
                        store_out(a)
                    for s in s_st:
                        s.wait(eng, 16 * 2 * NBAT)

            Walk(eng, Do())

        @block.tensor
        def _(eng):
            for s in (s_ax, s_b, s_d, s_pv):
                s.open(eng)

            def scores_for_max(b, g, c):
                qh, j, qt, kh = c // CH, c % CH // NT, c % NT // 2, c % 2
                if c == 0:
                    s_ld[g].wait(eng, 16 * ULOADS * (b + 1))
                s_mx.wait(eng, 2 * CH * unit(b, g) + c - 1)
                eng.matmul(pb[c % 2][:, :], qa[g][0:KROWS, qh, j, qt * P:(qt + 1) * P],
                           ka[g][0:KROWS, j, kh * 512:(kh + 1) * 512], start=True, stop=True).then_inc(s_b.sem, 1)

            def scores(b, g, t, half):
                qh, kt = t // NT, t % NT
                if kt == 0 and half == 0:
                    s_mr[g].wait(eng, 16 * MROWS * (2 * b + qh + 1))
                s_ex.wait(eng, 2 * (ST * unit(b, g) + t) + half - 1)
                for a in range(2):
                    j = 2 * half + a
                    mm = eng.matmul(pd[half][:, a, :], ka[g][0:KROWS + MROWS, j, kt * P:(kt + 1) * P],
                                    qa[g][0:KROWS + MROWS, qh, j, :], start=True, stop=True)
                mm.then_inc(s_d.sem, 1)

            def times_v(b, par, g, t):
                kt = t % NT
                if kt == 0:
                    s_o.wait(eng, 2 * unit(b, g) + t // NT)
                s_ex.wait(eng, 2 * (ST * unit(b, g) + t) + 2)
                for j in range(GH):
                    mm = eng.matmul(po[VW * j:VW * (j + 1), :], va[par][:, kt, GH * g + j, :], ex[t % 2][:, j, :],
                                    start=(kt == 0), stop=(kt == NT - 1), skip_group_check=True)
                mm.then_inc(s_pv.sem, 1)

            def aux(a):
                s_ac.wait(eng, a.n - a.slack)
                bank = a.bank
                turn = lambda src: [eng.transpose(bank[:, j * P:(j + 1) * P], src(j), k.ident[:, :]) for j in range(4)][-1]
                if a.kind == "xT":
                    c, f = a.at
                    s_xn.wait(eng, 2 * a.b + f + 1)
                    mm = turn(lambda j: xn[:, 4 * f + j, c * P:(c + 1) * P])
                elif a.kind == "xd":
                    c, f = a.at
                    for d in range(DT):
                        mm = eng.matmul(bank[:, :], w.wd[:, d, c * P:(c + 1) * P], xT[:, d, f * 512:(f + 1) * 512],
                                        start=(d == 0), stop=(d == DT - 1))
                elif a.kind == "qk":
                    m, c, f = a.at
                    mm = eng.matmul(bank[:, :], w.bd[:, m, c, :], xd[:, c, f * 512:(f + 1) * 512], start=True, stop=True)
                elif a.kind == "v":
                    for i in range(2):
                        tile = 2 * a.at[0] + i
                        for c in range(DT):
                            mm = eng.matmul(bank[:, i * D + c * P:i * D + (c + 1) * P], xd[:, c, tile * P:(tile + 1) * P],
                                            w.bd[:, 2, c, :], start=True, stop=True)
                elif a.kind == "mx":
                    s_nm.wait(eng, 2 * unit(a.b, a.g) + a.at[0] + 1)
                    mm = eng.transpose(bank[0:MR, 0:P], nm[:, :], k.ident[:, :])
                elif a.kind == "f":
                    s_o.wait(eng, 2 * unit(a.b, a.g) + a.at[0] + 1)
                    mm = turn(lambda j: os_[:, j * P:(j + 1) * P])
                elif a.kind == "aT":
                    f, c = a.at
                    mm = turn(lambda j: ao[:, 4 * f + j, c * P:(c + 1) * P])
                elif a.kind == "u":
                    f, half = a.at
                    for i in range(2):
                        q = (2 * half + i) * P
                        for c in range(DT):
                            mm = eng.matmul(bank[:, i * D:(i + 1) * D], aT[:, c, q:q + P], w.wu[:, c, :],
                                            start=(c == 0), stop=(c == DT - 1))
                mm.then_inc(s_ax.sem, 1)

            class Do:
                def start(self, tasks):
                    for a in tasks[:-1]:
                        aux(a)
                    for c in range(2 * CH):
                        scores_for_max(0, 0, c)
                        if c == CH + 1:
                            aux(tasks[-1])
                    eng.wait_ge(s_one, 6)
                    for half in range(2):
                        scores(0, 0, 0, half)

                def step(self, b, par, g, t, n, ns, before, now, last):
                    b1, g1 = next_unit(b, g)
                    ahead = not (last and g == 3)
                    ends = last and g == 3 and t == ST - 1
                    for i in range(4):
                        if ahead:
                            scores_for_max(b1, g1, 4 * t + i)
                        if i < 2 and not ends:
                            scores(*((b, g, t + 1) if t < ST - 1 else (b1, g1, 0)), i)
                        if i == 2:
                            times_v(b, par, g, t)
                    if now:
                        aux(now)

                def end(self, tasks):
                    for a in tasks:
                        aux(a)

            Walk(eng, Do())

        @block.scalar
        def _(eng):
            for s in (s_hi, s_ex, s_ac):
                s.open(eng)

            def aux(a):
                if a is None or a.kind in ("f", "u"):
                    return
                bank = a.bank
                s_ax.wait(eng, a.n + 1)
                if a.kind == "qk":
                    m, c, f = a.at
                    s_scr.wait(eng, 96 * a.b)
                    eng.activation(parts[:, m, 0, c, f * 512:(f + 1) * 512], bank[:, :], ACT.Copy,
                                   scale=SCALE).then_inc(s_hi.sem, 1)
                    return
                if a.kind == "mx":
                    if a.at[0] == 1:
                        s_mr[a.g].wait(eng, 16 * MROWS * (2 * a.b + 1))
                    else:
                        s_mr[(a.g - 1) % 4].wait(eng, 16 * MROWS * (2 * a.b + 2 if a.g else 2 * a.b))
                    eng.activation(mparts[:, 0, :], bank[0:MR, 0:P], ACT.Copy).then_inc(s_hi.sem, 1)
                    return
                if a.kind == "v":
                    for i in range(2):
                        ins = eng.activation(va[a.par][:, 2 * a.at[0] + i, :, 0:HS],
                                             bank[:, i * D:(i + 1) * D].rearrange("p (h s) -> p h s", s=HS), ACT.Copy)
                elif a.kind == "aT":
                    ins = eng.activation(aT[:, a.at[1], :], bank[:, :], ACT.Copy)
                else:
                    c, f = a.at
                    dst = xT if a.kind == "xT" else xd
                    ins = eng.activation(dst[:, c, f * 512:(f + 1) * 512], bank[:, :], ACT.Copy)
                ins.then_inc(s_ac.sem, 1)

            class Do:
                def start(self, tasks):
                    eng.wait_ge(s_one, 2)
                    for a in tasks:
                        aux(a)

                def step(self, b, par, g, t, n, ns, before, now, last):
                    for half in range(2):
                        s_d.wait(eng, 2 * (ST * unit(b, g) + t) + half + 1)
                        eng.activation(ex[t % 2][:, 2 * half:2 * half + 2, :], pd[half][:, :, :],
                                       ACT.Exp).then_inc(s_ex.sem, 1)
                    aux(before)

                def end(self, tasks):
                    for a in tasks:
                        aux(a)

            Walk(eng, Do())

        @block.vector
        def _(eng):
            norm.open_vector(eng)
            for s in (s_xn, s_mx, s_nm, s_o, s_rc):
                s.open(eng)

            def maxima(b, g, c):
                s_b.wait(eng, 2 * CH * unit(b, g) + c + 1)
                if c % CH == 0:
                    s_nm.wait(eng, 2 * unit(b, g) + c // CH)
                eng.tensor_reduce(mxc[:, c % CH:c % CH + 1], pb[c % 2][:, :], AX.X, ALU.max).then_inc(s_mx.sem, 1)

            def negate(b, g, qh, n):
                s_mx.wait(eng, CH * (2 * unit(b, g) + qh + 1))
                s_ax.wait(eng, n)
                eng.tensor_reduce(nm[:, :], mxc[:, :].rearrange("p (q h) -> p q h", h=2), AX.X, ALU.max,
                                  negate=True).then_inc(s_nm.sem, 1)

            def stats(b, f):
                s_xr.wait(eng, 16 * (b + 1))
                norm.stats_step(eng, 2 * b + f, xr[:, 4 * f:4 * f + 4, :], [P] * 4)

            def apply(b, f, n):
                s_ax.wait(eng, n)
                norm.apply_step(eng, 2 * b + f, xn[:, 4 * f:4 * f + 4, :], xr[:, 4 * f:4 * f + 4, :],
                                [P] * 4).then_inc(s_xn.sem, 1)

            def aux(a):
                if a is None or a.kind not in ("qk", "mx", "f", "u"):
                    return
                bank = a.bank
                if a.kind in ("qk", "mx"):
                    s_hi.wait(eng, a.ns + 1)
                    s_lo.wait(eng, a.ns - RES + 1)
                    if a.kind == "qk":
                        m, c, f = a.at
                        eng.scalar_tensor_tensor(res[a.slot][:, :], bank[:, :], SCALE,
                                                 parts[:, m, 0, c, f * 512:(f + 1) * 512],
                                                 ALU.mult, ALU.subtract).then_inc(s_ac.sem, 1)
                    else:
                        eng.tensor_tensor(res[a.slot][0:MR, 0:P], bank[0:MR, 0:P], mparts[:, 0, :],
                                          ALU.subtract).then_inc(s_ac.sem, 1)
                    return
                s_ax.wait(eng, a.n + 1)
                if a.kind == "f":
                    u = unit(a.b, a.g)
                    v = bank[:, :].rearrange("p (t j s) -> p t j s", t=4, j=GH)
                    eng.reciprocal(rec[:, :, :], v[:, :, :, HS]).then_inc(s_rc.sem, 1)
                    s_rc.wait(eng, 2 * u + a.at[0] + 1)
                    out = ao[:, 4 * a.at[0]:4 * a.at[0] + 4, GH * HS * a.g:GH * HS * (a.g + 1)]
                    ins = eng.tensor_tensor(out.rearrange("p t (j s) -> p t j s", j=GH), v[:, :, :, 0:HS],
                                            rec[:, :, :].unsqueeze(3).broadcast_to([P, 4, GH, HS]), ALU.mult)
                else:
                    f, half = a.at
                    s_xb.wait(eng, a.b + 1)
                    s_st[half].wait(eng, 16 * (2 * a.b + f))
                    r0 = 4 * f + 2 * half
                    ins = eng.tensor_tensor(yo[half][:, :, :], bank[:, :].rearrange("p (t d) -> p t d", d=D),
                                            xres[:, r0:r0 + 2, :], ALU.add)
                ins.then_inc(s_ac.sem, 1)

            class Do:
                def start(self, tasks):
                    for v in va:
                        eng.memset(v[:, :, :, HS + 1:VW], 0.0)
                        eng.memset(v[:, :, :, HS:HS + 1], 1.0).then_inc(s_one, 1)
                    for f in range(2):
                        stats(0, f)
                        apply(0, f, 0)
                    for a in tasks[:-1]:
                        aux(a)
                    for t in ka:
                        eng.memset(t[KROWS:KROWS + MROWS, :, :], 1.0).then_inc(s_one, 1)
                    for c in range(2 * CH):
                        maxima(0, 0, c)
                        if c % CH == CH - 1:
                            negate(0, 0, c // CH, len(tasks) if c // CH else 0)
                        if c == CH + 1:
                            aux(tasks[-1])

                def step(self, b, par, g, t, n, ns, before, now, last):
                    b1, g1 = next_unit(b, g)
                    ahead = not (last and g == 3)
                    for i in range(4):
                        if ahead:
                            maxima(b1, g1, 4 * t + i)
                        if i == 1:
                            aux(before)
                        if i == 2 and t % NT == NT - 1:
                            s_pv.wait(eng, ST * unit(b, g) + t + 1)
                            s_ax.wait(eng, n)
                            eng.tensor_copy(os_[:, :], po[:, :]).then_inc(s_o.sem, 1)
                    if ahead and t % NT == NT - 1:
                        negate(b1, g1, t // NT, n)
                    if g == 0 and not last and t in (2, 3, 4, 5):
                        if t % 2 == 0:
                            stats(b + 1, (t - 2) // 2)
                        else:
                            apply(b + 1, (t - 2) // 2, n)

                def end(self, tasks):
                    for a in tasks:
                        aux(a)

            Walk(eng, Do())

        @block.gpsimd
        def _(eng):
            norm.open_pool(eng)
            for s in (s_mi, s_lo, s_xb):
                s.open(eng)
            eng.memset(zeros[:, :], 0.0).then_inc(s_zero, 1)
            eng.wait_ge(s_zero, 1)

            def aux(a):
                if a is None or not splits((a.kind,)):
                    return
                if a.kind == "qk":
                    m, c, f = a.at
                    mid, low = (parts[:, m, p, c, f * 512:(f + 1) * 512] for p in (1, 2))
                    r = res[a.slot][:, :]
                else:
                    mid, low = mparts[:, 1, :], mparts[:, 2, :]
                    r = res[a.slot][0:MR, 0:P]
                s_ac.wait(eng, a.n + 1)
                eng.tensor_tensor(mid, r, zeros[0:r.shape[0], :].broadcast_to(list(r.shape)), ALU.add).then_inc(s_mi.sem, 1)
                s_mi.wait(eng, a.ns + 1)
                eng.tensor_tensor(low, r, mid, ALU.subtract).then_inc(s_lo.sem, 1)

            class Do:
                def start(self, tasks):
                    for f in range(2):
                        norm.pow_step(eng, f, 4)
                    for a in tasks:
                        aux(a)

                def step(self, b, par, g, t, n, ns, before, now, last):
                    if g == 0 and not last and t in (2, 4):
                        norm.pow_step(eng, 2 * (b + 1) + (t - 2) // 2, 4)
                    aux(before)
                    if g == 2 and t == 8:
                        s_xl.wait(eng, 16 * (b + 1))
                        for q in range(0, NT, 2):
                            ins = eng.tensor_tensor(xres[:, q:q + 2, :], xres[:, q:q + 2, :],
                                                    w.bu[:, :].unsqueeze(1).broadcast_to([P, 2, D]), ALU.add)
                        ins.then_inc(s_xb.sem, 1)

                def end(self, tasks):
                    pass

            Walk(eng, Do())


_INS = ["L0_attn_x", "L0_attn_W_down", "L0_attn_tokeys", "L0_attn_toqueries", "L0_attn_tovalues", "L0_attn_W_unify",
        "L0_attn_b_unify", "L0_ffn_router_w", "L0_ffn_router_b", "L0_ffn_w1", "L0_ffn_b1", "L0_ffn_w2", "L0_ffn_b2",
        "L0_ffn_ow1", "L0_ffn_ob1", "L0_ffn_ow2", "L0_ffn_ob2"]
STAGE = 0


def program(nc, x, W_down, tokeys, toqueries, tovalues, W_unify, b_unify, router_w, router_b, w1, b1, w2, b2,
            ow1, ob1, ow2, ob2, out):
    rows = lambda a: a.rearrange("b t d -> (b t) d")
    with ExitStack() as ctx:
        k = Consts(ctx, nc)
        w = Heads(ctx, nc)
        setup(nc, k, router_w, router_b, b1, ob1, w, (W_down, toqueries, tokeys, tovalues, W_unify, b_unify))
        x1 = nc.dram_tensor("x1", (x.shape[0] * x.shape[1], D), F32).ap()
        x2 = nc.dram_tensor("x2", (x.shape[0] * x.shape[1], D), F32).ap()
        if STAGE == 1:
            ffn(nc, k, "f1_", rows(x), rows(out), w1, b2, w2, ow1, ow2, ob2)
        if STAGE == 0:
            ffn(nc, k, "f1_", rows(x), x1, w1, b2, w2, ow1, ow2, ob2)
        if STAGE != 1:
            attention_setup(nc, w, k)
            attention(nc, k, w, rows(x) if STAGE == 2 else x1, rows(out) if STAGE == 2 else x2, x.shape[0])
        if STAGE == 0:
            ffn(nc, k, "f2_", x2, rows(out), w1, b2, w2, ow1, ow2, ob2)


def kernel(**inputs):
    import numpy as np
    import concourse.bacc as bacc
    from concourse.bass_utils import run_bass_kernel_spmd

    nc = bacc.Bacc("TRN2", target_bir_lowering=False, num_devices=1)
    arrays, args = {}, []
    for name in _INS:
        a = np.ascontiguousarray(inputs[name])
        arrays[f"in_{name}"] = a
        args.append(nc.dram_tensor(f"in_{name}", a.shape, mybir.dt.from_np(a.dtype), kind="ExternalInput").ap())
    shape = inputs["L0_attn_x"].shape
    args.append(nc.dram_tensor("out_0", shape, F32, kind="ExternalOutput").ap())
    program(nc, *args)
    r = run_bass_kernel_spmd(nc, [arrays], core_ids=[0])
    return r.results[0]["out_0"]
```

```python
from contextlib import ExitStack

import concourse.bass as bass
from concourse import mybir

F32 = mybir.dt.float32
F32R = mybir.dt.float32r
BF16 = mybir.dt.bfloat16
I32 = mybir.dt.int32
ALU = mybir.AluOpType
ACT = mybir.ActivationFunctionType
AX = mybir.AxisListType

P = 128
D = 256
DT = D // P
H = 1024
HT = H // P
E = 8
C = 320
CCH = [(0, 128), (128, 128), (256, 64)]
RW = 32
EPS = 1e-5
CREDIT = 16


class Sem:

    def __init__(self, ctx, nc, name, credit=CREDIT):
        self.sem = ctx.enter_context(nc.semaphore(name))
        self.credit = credit

    def open(self, eng):
        eng.sem_inc(self.sem, self.credit)

    def wait(self, eng, n):
        eng.wait_ge(self.sem, n + self.credit)


def split_token_tiles(x):
    return x.rearrange("(t p) d -> p t d", p=P)


class Consts:

    def __init__(self, ctx, nc):
        sb = lambda name, shape, dt: ctx.enter_context(nc.sbuf_tensor(name, shape, dt))
        self.ident = sb("ident", [P, P], F32)
        self.tri = sb("tri", [P, P], F32)
        self.ones = sb("ones", [P, P], F32)
        self.esc = sb("esc", [P, E], F32)
        self.neghalf = sb("neghalf", [P, 32], F32)
        self.tokid = sb("tokid", [P, 64], I32)
        self.rw = sb("rw", [P, DT, RW], F32)
        self.sel = sb("sel", [P, 4 * E], F32)
        self.rb = sb("rb", [P, E], F32)
        self.b1T = sb("b1T", [P, E + 1, HT], F32)


def setup(nc, k, router_w, router_b, b1, ob1, w, attention_weights):
    with ExitStack() as ctx:
        sem = lambda n: ctx.enter_context(nc.semaphore(n))
        s_in, s_b, s_set, s_mk, s_t, s_rw = (sem("su_" + n) for n in ("in", "b", "set", "mk", "t", "rw"))
        b1rows = ctx.enter_context(nc.sbuf_tensor("su_b1rows", [(E + 1) * HT, P], F32))
        pt = ctx.enter_context(nc.psum_tensor("su_pt", [P, 512], F32))
        block = ctx.enter_context(nc.Block())

        @block.sync
        def _(eng):
            eng.dma_start(b1rows[0:E * HT, :], b1.rearrange("e (c p) -> (e c) p", p=P)).then_inc(s_b, 16)
            eng.dma_start(b1rows[E * HT:, :], ob1.rearrange("(c p) -> c p", p=P)).then_inc(s_b, 16)
            eng.wait_ge(s_rw, 1)
            eng.dma_start(k.rw[:, :, 0:E], router_w.rearrange("(c p) e -> p c e", p=P)).then_inc(s_in, 16)
            eng.dma_start(k.rb[:, :], router_b.rearrange("(a e) -> a e", a=1).broadcast_to([P, E])).then_inc(s_in, 16)
            w.load(eng, *attention_weights)
            eng.wait_ge(s_in, 32)

        @block.gpsimd
        def _(eng):
            eng.memset(k.rw[:, :, :], 0.0).then_inc(s_rw, 1)
            eng.memset(k.ident[:, :], 0.0).then_inc(s_set, 1)
            eng.memset(k.tri[:, :], 1.0).then_inc(s_set, 1)
            eng.memset(k.ones[:, :], 1.0)
            eng.memset(k.neghalf[:, :], -0.5)
            eng.iota(k.tokid[:, :], [[P, 64]], base=0, channel_multiplier=1)
            eng.iota(k.esc[:, :], [[-1, E]], base=E, channel_multiplier=0, allow_small_or_imprecise_dtypes=True)
            eng.wait_ge(s_set, 2)
            eng.affine_select(out=k.ident[:, :], in_=k.ident[:, :], compare_op=ALU.not_equal, fill=1.0,
                              base=0, pattern=[[-1, P]], channel_multiplier=1).then_inc(s_mk, 1)
            eng.affine_select(out=k.tri[:, :], in_=k.tri[:, :], compare_op=ALU.is_ge, fill=0.0,
                              base=0, pattern=[[1, P]], channel_multiplier=-1).then_inc(s_mk, 1)

        @block.tensor
        def _(eng):
            n = (E + 1) * HT
            eng.wait_ge(s_mk, 1)
            eng.wait_ge(s_b, 32)
            eng.transpose(pt[:, 0:n], b1rows[:, :], k.ident[0:n, 0:n]).then_inc(s_t, 1)

        @block.vector
        def _(eng):
            eng.wait_ge(s_mk, 1)
            eng.tensor_copy(k.sel[:, :].rearrange("p (j e) -> p j e", e=E),
                            k.ident[:, :].rearrange("p (j e) -> p j e", e=RW)[:, :, 0:E])
            eng.wait_ge(s_t, 1)
            eng.tensor_copy(k.b1T[:, :, :].rearrange("p e c -> p (e c)"), pt[:, 0:(E + 1) * HT])


class Norm:

    def __init__(self, ctx, nc, k, name):
        sb = lambda n, shape: ctx.enter_context(nc.sbuf_tensor(name + n, shape, F32))
        self.k = k
        self.stats = sb("stats", [P, 4, 6])
        self.mv = sb("mv", [P, 4, 2])
        self.ve = sb("ve", [P, 4])
        self.rstd = sb("rstd", [P, 4])
        self.pad = sb("pad", [P, 1])
        self.s_dve = Sem(ctx, nc, name + "s_dve")
        self.s_pow = Sem(ctx, nc, name + "s_pow")

    def open_vector(self, eng):
        self.s_dve.open(eng)

    def open_pool(self, eng):
        self.s_pow.open(eng)

    def tile_stats(self, eng, n, src, rows, tiles=range(4)):
        last = None
        self.s_pow.wait(eng, n)
        self.s_dve.wait(eng, 3 * n)
        for j in tiles:
            if j < len(rows):
                last = eng.bn_stats(self.stats[0:rows[j], j, :], src[0:rows[j], j, :])
        return last

    def stats_step(self, eng, n, src, rows, tiles=range(4)):
        self.tile_stats(eng, n, src, rows, tiles).then_inc(self.s_dve.sem, 1)
        self.s_dve.wait(eng, 3 * n + 1)
        eng.memset(self.pad[:, :], 0.0)
        for j, r in enumerate(rows):
            last = eng.bn_aggr(self.mv[0:r, j, :], self.stats[0:r, j, :])
        last.then_inc(self.s_dve.sem, 1)
        self.s_dve.wait(eng, 3 * n + 2)
        last = eng.tensor_scalar(self.ve[:, 0:len(rows)], self.mv[:, 0:len(rows), 1], EPS, None, ALU.add)
        last.then_inc(self.s_dve.sem, 1)

    def pow_step(self, eng, n, count):
        self.s_dve.wait(eng, 3 * n + 3)
        eng.tensor_tensor(self.rstd[:, 0:count], self.ve[:, 0:count], self.k.neghalf[:, 0:count],
                          ALU.pow).then_inc(self.s_pow.sem, 1)

    def apply_step(self, eng, n, dst, src, rows, tiles=range(4)):
        self.s_pow.wait(eng, n + 1)
        last = None
        for j, r in enumerate(rows):
            if j in tiles:
                last = eng.tensor_scalar(dst[0:r, j, :], src[0:r, j, :], self.mv[0:r, j, 0:1], self.rstd[0:r, j:j + 1],
                                         ALU.subtract, ALU.mult)
        return last


PIECES = 8
WN = DT * H + HT * D
PW = WN // PIECES


def piece(q):
    c = q % DT * DT + q // DT if q < PIECES // 2 else q
    return slice(c * PW, (c + 1) * PW)


class Weights:

    def __init__(self, ctx, nc, name):
        sb = lambda n, dt: ctx.enter_context(nc.sbuf_tensor(name + n, [P, WN], dt))
        self.raw = sb("wraw", F32)
        self.high = [sb(f"wh{i}", F32R) for i in range(2)]
        self.low = [sb(f"wl{i}", F32R) for i in range(2)]

    def load_piece(self, eng, q, a1, a2):
        dst = self.raw[:, piece(q)]
        if q < PIECES // 2:
            c, f = q % DT, q // DT
            src = a1[c * P:(c + 1) * P, f * PW:(f + 1) * PW]
        else:
            q2 = q - PIECES // 2
            dst = dst.rearrange("p (c d) -> p c d", d=D)
            src = a2[2 * q2 * P:(2 * q2 + 2) * P, :].rearrange("(c p) d -> p c d", p=P)
        return eng.dma_start(dst, src)


def router(nc, k, lg, wts, name, x_in, b2s, b2, ob2, ow1, ow2):
    x_t = split_token_tiles(x_in)
    NB = x_t.shape[1] // 4
    AHEAD = 4
    HALF = NB // 2 // AHEAD
    assert PIECES == NB // 2
    with ExitStack() as ctx:
        sb = lambda n, shape, dt: ctx.enter_context(nc.sbuf_tensor(name + n, shape, dt))
        xr = [sb(f"xr{i}", [P, 4, D], F32) for i in range(AHEAD)]
        xn = [sb(f"xn{i}", [P, 4, D], F32) for i in range(2)]
        xT = [sb(f"xT{i}", [P, DT, 4 * P], F32) for i in range(2)]
        off = [sb(f"off{i}", [P, 2], F32) for i in range(2)]
        lgT = [sb(f"lgT{i}", [P, P], F32) for i in range(2)]
        norm = [Norm(ctx, nc, k, name + f"ln{i}_") for i in range(2)]
        ps = lambda n, w: ctx.enter_context(nc.psum_tensor(name + n, [P, w], F32))
        pT = [[ps(f"pT{i}{f}", 512) for f in range(DT)] for i in range(2)]
        pg = [ps(f"pg{i}", 512) for i in range(2)]
        logits = ps("logits", NB * 4 * E)
        S = lambda n: Sem(ctx, nc, name + n)
        s_ld = [S(f"s_ld{i}") for i in range(AHEAD)]
        s_off = S("s_off")
        s_xn = S("s_xn")
        s_xa = S("s_xa")
        s_tp = S("s_tp")
        s_ev = S("s_ev")
        s_lg = S("s_lg")
        s_le = S("s_le")
        s_tb = S("s_tb")
        s_wh = S("s_wh")
        s_w = ctx.enter_context(nc.semaphore(name + "s_w"))
        block = ctx.enter_context(nc.Block())

        def columns(q):
            return bass.ds(q * PW, PW)

        @block.sync
        def _(eng):
            for s in s_ld:
                s.open(eng)

            def load(i, b):
                n = AHEAD * i + b
                s_xn.wait(eng, n - AHEAD + 1)
                s_xa.wait(eng, n - AHEAD + 1)
                eng.dma_start(xr[b][:, :, :], x_t[:, bass.ds(4 * n, 4), :]).then_inc(s_ld[b].sem, 16)

            for b in range(AHEAD):
                load(0, b)
            for q in range(PIECES):
                wts.load_piece(eng, q, ow1, ow2).then_inc(s_w, 16)
            for e in range(E):
                eng.dma_start(b2s[:, e, :], b2[e:e + 1, :].broadcast_to([P, D])).then_inc(s_w, 16)
            eng.dma_start(b2s[:, E, :], ob2.rearrange("(a e) -> a e", a=1).broadcast_to([P, D])).then_inc(s_w, 16)
            with eng.Fori(1, NB // AHEAD) as i:
                for b in range(AHEAD):
                    load(i, b)

        @block.gpsimd
        def _(eng):
            for m in norm:
                m.open_pool(eng)

            def power(i, b):
                s_xa.wait(eng, 2 * i + b - 1)
                norm[b].pow_step(eng, i, 4)

            def low(q):
                s_wh.wait(eng, q + 1)
                eng.tensor_tensor(wts.low[0][:, columns(q)], wts.raw[:, columns(q)],
                                  wts.high[0][:, columns(q)].bitcast(F32), ALU.subtract)

            with eng.Fori(0, NB // 4 + 1) as i:
                for b in range(2):
                    power(i, b)
            with eng.Fori(0, NB // 4 - 1) as i:
                for b in range(2):
                    power(i + NB // 4 + 1, b)
                    low(2 * i + b)
            for q in (PIECES - 2, PIECES - 1):
                low(q)

        @block.vector
        def _(eng):
            for m in norm:
                m.open_vector(eng)
            s_xn.open(eng)
            s_off.open(eng)

            def stats(i, b):
                s_ld[b].wait(eng, 16 * i + 16)
                norm[b % 2].stats_step(eng, 2 * i + b // 2, xr[b], [P] * 4)

            def apply(i, b):
                n = AHEAD * i + b
                m = norm[b % 2]
                s_xa.wait(eng, n - 1)
                m.s_pow.wait(eng, 2 * i + b // 2 + 1)
                eng.scalar_tensor_tensor(off[b % 2][:, :], m.mv[:, 2:4, 0], -1.0, m.rstd[:, 2:4],
                                         ALU.mult, ALU.mult).then_inc(s_off.sem, 1)
                s_tp.wait(eng, n - 1)
                m.apply_step(eng, 2 * i + b // 2, xn[b % 2], xr[b], [P] * 2).then_inc(s_xn.sem, 1)

            stats(0, 0)
            with eng.Fori(0, NB // AHEAD - 1) as i:
                for b in range(AHEAD):
                    stats(i + (b + 1) // AHEAD, (b + 1) % AHEAD)
                    apply(i, b)
            last = NB // AHEAD - 1
            for b in range(AHEAD):
                if b + 1 < AHEAD:
                    stats(last, b + 1)
                apply(last, b)
            eng.wait_ge(s_w, 16 * (PIECES + E + 1))
            eng.tensor_scalar(b2s[:, :, :], b2s[:, :, :], 0.5, None, ALU.mult)
            s_tb.wait(eng, NB)
            eng.tensor_tensor(lg[:, :, :], logits[:, :].rearrange("p (t e) -> p t e", e=E),
                              k.rb[:, :].unsqueeze(1).broadcast_to([P, 4 * NB, E]), ALU.add)

        @block.scalar
        def _(eng):
            for s in (s_xa, s_ev, s_le, s_wh):
                s.open(eng)

            def apply(i, b):
                n = AHEAD * i + b
                s_ld[b].wait(eng, 16 * i + 16)
                s_off.wait(eng, n + 1)
                s_tp.wait(eng, n - 1)
                for j in (2, 3):
                    ins = eng.activation(xn[b % 2][:, j, :], xr[b][:, j, :], ACT.Identity,
                                         bias=off[b % 2][:, j - 2:j - 1], scale=norm[b % 2].rstd[:, j:j + 1])
                ins.then_inc(s_xa.sem, 1)

            def evacuate(n, b):
                s_tp.wait(eng, n + 1)
                s_lg.wait(eng, n - 1)
                for f in range(DT):
                    ins = eng.activation(xT[b % 2][:, f, :], pT[b % 2][f][:, :], ACT.Copy)
                ins.then_inc(s_ev.sem, 1)

            def products(n, b):
                s_lg.wait(eng, n + 1)
                s_tb.wait(eng, n - 1)
                eng.activation(lgT[b % 2][:, :], pg[b % 2][:, 0:P], ACT.Copy).then_inc(s_le.sem, 1)

            def body(i, b, split, left=2):
                if split:
                    if b == 0:
                        eng.wait_ge(s_w, 16 * (PIECES + E + 1))
                    q = columns(AHEAD * (i - HALF) + b)
                    eng.activation(wts.high[0][:, q], wts.raw[:, q], ACT.Copy).then_inc(s_wh.sem, 1)
                if left > 1:
                    apply(i + (b + 2) // AHEAD, (b + 2) % AHEAD)
                if left > 0:
                    evacuate(AHEAD * i + b + 1, b + 1)
                products(AHEAD * i + b, b)

            apply(0, 0)
            evacuate(0, 0)
            apply(0, 1)
            with eng.Fori(0, HALF) as i:
                for b in range(AHEAD):
                    body(i, b, False)
            with eng.Fori(HALF, 2 * HALF - 1) as i:
                for b in range(AHEAD):
                    body(i, b, True)
            for b in range(AHEAD):
                body(2 * HALF - 1, b, True, left=min(2, AHEAD - 1 - b))

        @block.tensor
        def _(eng):
            for s in (s_tp, s_lg, s_tb):
                s.open(eng)

            def turn(n, b):
                s_xn.wait(eng, n + 1)
                s_xa.wait(eng, n + 1)
                s_ev.wait(eng, n - 1)
                for f in range(DT):
                    for j in range(4):
                        mm = eng.transpose(pT[b % 2][f][:, j * P:(j + 1) * P], xn[b % 2][:, j, f * P:(f + 1) * P],
                                           k.ident[:, :])
                mm.then_inc(s_tp.sem, 1)

            def products(n, b):
                s_ev.wait(eng, n + 1)
                s_le.wait(eng, n - 1)
                for f in range(DT):
                    for j in range(4):
                        mm = eng.matmul(pg[b % 2][RW * j:RW * (j + 1), 0:P], k.rw[:, f, :],
                                        xT[b % 2][:, f, j * P:(j + 1) * P], start=(f == 0), stop=(f == DT - 1),
                                        skip_group_check=True)
                mm.then_inc(s_lg.sem, 1)

            def turn_back(n, b):
                s_le.wait(eng, n + 1)
                eng.matmul(logits[:, bass.ds(4 * E * n, 4 * E)], lgT[b % 2][:, :], k.sel[:, :],
                           start=True, stop=True).then_inc(s_tb.sem, 1)

            turn(0, 0)
            turn(1, 1)
            products(0, 0)
            with eng.Fori(0, NB // 2 - 1) as i:
                for b in (1, 2):
                    turn(2 * i + b + 1, b + 1)
                    products(2 * i + b, b)
                    turn_back(2 * i + b - 1, b - 1)
            products(NB - 1, 1)
            turn_back(NB - 2, 0)
            turn_back(NB - 1, 1)


NO_TOKEN = 1 << 20


class Slots:

    def __init__(self, ctx, nc, name, k, lg, counts):
        nt = lg.shape[1]
        sb = lambda n, shape: ctx.enter_context(nc.sbuf_tensor(name + n, shape, F32))
        self.nt, self.k, self.lg = nt, k, lg
        self.pc, self.pt = counts
        self.cand = sb("cand", [P, nt, E])
        self.onehot = sb("onehot", [P, nt, E])
        self.tot = sb("tot", [P, nt, E])
        self.incl = sb("incl", [P, nt, E])
        self.mx, self.best, self.one_t, self.rank, self.none, self.tmp = (
            sb(n, [P, nt]) for n in ("mx", "best", "one_t", "rank", "none", "tmp"))
        sem = lambda n: ctx.enter_context(nc.semaphore(name + n))
        self.s_v = sem("s_v")
        self.s_mm = sem("s_mm")
        self.n = 0

    ONEHOT, PUT = 5, 16

    def step(self, ins):
        self.n += 1
        ins.then_inc(self.s_v, 1)

    def link(self, eng, ins):
        self.step(ins)
        eng.wait_ge(self.s_v, self.n)

    def experts_step(self, eng):
        wide = lambda t: t[:, :].unsqueeze(2).broadcast_to([P, self.nt, E])
        cand, lg = self.cand[:, :, :], self.lg[:, :, :]
        self.link(eng, eng.tensor_reduce(self.mx[:, :], lg, AX.X, ALU.max))
        self.link(eng, eng.tensor_tensor(cand, lg, wide(self.mx), ALU.is_ge))
        self.link(eng, eng.tensor_tensor(cand, cand, self.k.esc[:, :].unsqueeze(1).broadcast_to([P, self.nt, E]),
                                         ALU.mult))
        self.link(eng, eng.tensor_reduce(self.best[:, :], cand, AX.X, ALU.max))
        self.step(eng.tensor_tensor(self.onehot[:, :, :], cand, wide(self.best), ALU.is_equal))
        assert self.n == self.ONEHOT
        self.link(eng, eng.memset(self.one_t[:, :], 1.0))

    def count_step(self, eng):
        flat = self.onehot[:, :, :].rearrange("p t e -> p (t e)")
        eng.wait_ge(self.s_v, self.ONEHOT)
        eng.matmul(self.pc, self.k.tri[:, :], flat, start=True, stop=True)
        eng.matmul(self.pt, self.k.ones[:, :], flat, start=True, stop=True).then_inc(self.s_mm, 1)

    def slots_step(self, eng, put):
        link = lambda ins: self.link(eng, ins)
        incl, flat = self.incl[:, :, :], lambda t: t[:, :, :].rearrange("p t e -> p (t e)")
        tmp, rank = self.tmp[:, :], self.rank[:, :]
        eng.wait_ge(self.s_mm, 1)
        for e in range(E):
            ins = eng.tensor_tensor_scan(self.tot[:, :, e], self.one_t[:, :], self.pt[:, e::E], 0.0, ALU.mult, ALU.add)
        link(ins)
        link(eng.tensor_tensor(flat(self.incl), self.pc, flat(self.tot), ALU.add))
        link(eng.scalar_tensor_tensor(flat(self.incl), self.pt, -1.0, flat(self.incl), ALU.mult, ALU.add))
        link(eng.tensor_tensor(incl, incl, self.onehot[:, :, :], ALU.mult))
        link(eng.tensor_reduce(rank, incl, AX.X, ALU.add))
        link(eng.tensor_scalar(self.none[:, :], rank, float(C), float(2 * E * C), ALU.is_gt, ALU.mult))
        link(eng.tensor_scalar(tmp, self.best[:, :], -float(C), float(E * C - 1), ALU.mult, ALU.add))
        link(eng.tensor_tensor(tmp, tmp, rank, ALU.add))
        link(eng.tensor_tensor(tmp, tmp, self.none[:, :], ALU.add))
        self.step(eng.tensor_copy(put[:, :], tmp))
        assert self.n == self.PUT, self.n


def mlps(nc, k, lg, wts, name, x_in, x_out, b2s, w1, w2, table):
    x_t, o_t = split_token_tiles(x_in), split_token_tiles(x_out)
    NT = x_t.shape[1]
    NB = NT // 4
    RING = 4
    LAG = 3
    LOW = "VVVVVVVG"
    with ExitStack() as ctx:
        sb = lambda n, shape, dt: ctx.enter_context(nc.sbuf_tensor(name + n, shape, dt))
        xr = [sb(f"xr{i}", [P, 4, D], F32) for i in range(2)]
        xs = [sb(f"xs{i}", [P, 4, D], F32) for i in range(2)]
        xn = [sb(f"xn{i}", [P, 4, D], F32) for i in range(2)]
        xTh = [sb(f"xTh{i}", [P, DT, 512], F32R) for i in range(2)]
        xTl = [sb(f"xTl{i}", [P, DT, 512], F32R) for i in range(2)]
        h32 = [sb(f"h32{i}", [P, 512], F32) for i in range(2)]
        hh = [sb(f"hh{i}", [P, 512], F32R) for i in range(RING)]
        hl = [sb(f"hl{i}", [P, 512], F32R) for i in range(RING)]
        wraw, wh, wl = wts.raw, wts.high, wts.low
        yo = [sb(f"yo{i}", [P, 4, D], F32) for i in range(2)]
        put = sb("put", [P, NT], I32)
        empty = sb("empty", [P, E * C // P], I32)
        idx = sb("idx", [P, E, 3], I32)
        norm = Norm(ctx, nc, k, name + "ln_")
        pL = [ctx.enter_context(nc.psum_tensor(name + f"pL{i}", [P, 512], F32)) for i in range(2)]
        pA = [ctx.enter_context(nc.psum_tensor(name + f"pA{i}", [P, 2, 512], F32)) for i in range(2)]
        pT = [ctx.enter_context(nc.psum_tensor(name + f"pT{i}", [P, 512], F32)) for i in range(DT)]
        slots = Slots(ctx, nc, name + "sl_", k, lg, [pA[1][:, j, :] for j in range(2)])
        S = lambda n: Sem(ctx, nc, name + n)
        raw_sem = lambda n: ctx.enter_context(nc.semaphore(name + n))
        s_empty = raw_sem("s_empty")
        s_tab = raw_sem("s_tab")
        s_ld = [S(f"s_ld{i}") for i in range(2)]
        s_ga = [raw_sem(f"s_ga{i}") for i in range(2)]
        s_raw = [S(f"s_raw{i}") for i in range(PIECES)]
        s_st = [S(f"s_st{i}") for i in range(2)]
        s_sc = [raw_sem(f"s_sc{i}") for i in range(2)]
        s_put = raw_sem("s_put")
        s_idx = raw_sem("s_idx")
        s_xn = S("s_xn")
        s_xs = S("s_xs")
        s_tp = S("s_tp")
        s_thi = S("s_thi")
        s_tlo = S("s_tlo")
        s_l1 = S("s_l1")
        s_h = S("s_h")
        s_hi = S("s_hi")
        s_lo = S("s_lo")
        s_l2 = S("s_l2")
        s_y = S("s_y")
        s_wh = S("s_wh")
        s_wl = {who: S("s_wl" + who) for who in "VG"}

        def lows(e, q):
            return LOW.count(LOW[q]) * e + LOW[:q + 1].count(LOW[q])

        W1 = lambda w, c, h: w[:, c * H + h * P:c * H + (h + 1) * P]
        W2 = lambda w, h: w[:, DT * H + h * D:DT * H + (h + 1) * D]
        chunks = {"dense": [(j * P, P) for j in range(4)], "expert": CCH}
        width = {"dense": 512, "expert": C}
        rows_of = {kind: [m for _, m in chunks[kind]] for kind in chunks}

        def stream(eng, prologue, block):
            prologue()
            with eng.Fori(0, NB // 2 - 1) as i:
                block(i, 2 * i, 0, "dense", "dense", "dense")
                block(i, 2 * i + 1, 1, "dense", "dense", "dense")
            block(NB // 2 - 1, NB - 2, 0, "dense", "dense", "expert")
            block(NB // 2 - 1, NB - 1, 1, "dense", "expert", "expert")
            with eng.Fori(0, E // 2 - 1) as i:
                block(i, NB + 2 * i, 0, "expert", "expert", "expert")
                block(i, NB + 2 * i + 1, 1, "expert", "expert", "expert")
            block(E // 2 - 1, NB + E - 2, 0, "expert", "expert", None)
            block(E // 2 - 1, NB + E - 1, 1, "expert", None, None)

        def split_at(i, n, b, kind):
            if kind == "expert":
                return None if isinstance(n, int) and n == NB + E - 1 else (2 * i + b + 1, b)
            return (0, 1) if isinstance(n, int) and n == NB - 2 else None

        def pieces_at(s, ahead=0):
            return [q for q in range(PIECES) if max(q - ahead, 0) == s]

        def pair_after(i, b, kind, other, ahead):
            if kind == other:
                return i + (b + ahead) // 2
            return 0

        expert = lambda i, b: 2 * i + b
        wbuf = lambda b, kind: 0 if kind == "dense" else 1 - b

        block = ctx.enter_context(nc.Block())

        @block.sync
        def _(eng):
            for s in (*s_ld, *s_raw, *s_st):
                s.open(eng)

            def load_piece(e, q, a1, a2):
                s_wl[LOW[q]].wait(eng, lows(e - 1, q))
                wts.load_piece(eng, q, a1, a2).then_inc(s_raw[q].sem, 16)

            def of_expert(w, e):
                return w[bass.ds(e, 1), :, :].rearrange("a r c -> (a r) c")

            def load_rows(n, b):
                s_xn.wait(eng, n - 1)
                s_xs.wait(eng, n - 1)
                eng.dma_start(xr[b][:, :, :], x_t[:, bass.ds(4 * n, 4), :]).then_inc(s_ld[b].sem, 16)

            def store(n, b):
                s_y.wait(eng, n + 1)
                eng.dma_start(o_t[:, bass.ds(4 * n, 4), :], yo[b][:, :, :]).then_inc(s_st[b].sem, 16)

            load_rows(0, 0)
            load_rows(1, 1)
            eng.wait_ge(s_empty, 1)
            eng.dma_start(table.rearrange("(p c) a -> p (c a)", p=P), empty[:, :]).then_inc(s_tab, 16)
            load_rows(2, 0)
            load_rows(3, 1)
            for q in range(PIECES):
                load_piece(0, q, w1[0], w2[0])
            with eng.Fori(0, NB // 2 - 2) as i:
                for b in range(2):
                    store(2 * i + b, b)
                    load_rows(2 * i + b + 4, b)
            eng.wait_ge(s_put, 16 * NT)
            filled = table.rearrange("(e c) a -> c e a", e=E)
            for j, (c0, m) in enumerate(CCH):
                eng.dma_start(idx[0:m, :, j:j + 1], filled[c0:c0 + m], allow_slow_non_contiguous=True).then_inc(s_idx, 16)
            store(NB - 4, 0)
            store(NB - 3, 1)
            for q in range(PIECES):
                load_piece(1, q, w1[1], w2[1])
            store(NB - 2, 0)
            store(NB - 1, 1)
            with eng.Fori(2, E) as e:
                for q in range(PIECES):
                    load_piece(e, q, of_expert(w1, e), of_expert(w2, e))

        @block.gpsimd
        def _(eng):
            norm.open_pool(eng)
            s_xs.open(eng)
            s_wl["G"].open(eng)

            def with_bias(n):
                kind = "dense" if n < NB else "expert"
                e = E if n < NB else n - NB
                if n < NB:
                    s_ld[n % 2].wait(eng, 16 * (n // 2 + 1))
                else:
                    eng.wait_ge(s_ga[n % 2], 16 * len(CCH) * (e // 2 + 1))
                s_y.wait(eng, n - 1)
                for j in range(0, len(rows_of[kind]), 2):
                    w = min(2, len(rows_of[kind]) - j)
                    m = rows_of[kind][j]
                    ins = eng.tensor_tensor(xs[n % 2][0:m, j:j + w, :], xr[n % 2][0:m, j:j + w, :],
                                            b2s[0:m, e:e + 1, :].broadcast_to([m, w, D]), ALU.add)
                ins.then_inc(s_xs.sem, 1)

            def gather(e):
                n = NB + e
                if e == 0:
                    eng.wait_ge(s_idx, 16 * len(CCH))
                s_xn.wait(eng, n - 1)
                s_xs.wait(eng, n - 1)
                for j, (c0, m) in enumerate(CCH):
                    eng.indirect_dma_start(
                        out=xr[n % 2][0:m, j, :], out_offset=None, in_=x_in[:, :],
                        in_offset=bass.IndirectOffsetOnAxis(ap=idx[0:m, e, j:j + 1], axis=0),
                        bounds_check=NT * P - 1, oob_is_err=False).then_inc(s_ga[n % 2], 16)

            def scatter(e):
                if e == 0:
                    for s in s_st:
                        s.wait(eng, 16 * (NB // 2))
                s_y.wait(eng, NB + e + 1)
                for j, (c0, m) in enumerate(CCH):
                    eng.indirect_dma_start(
                        out=x_out[:, :], out_offset=bass.IndirectOffsetOnAxis(ap=idx[0:m, e, j:j + 1], axis=0),
                        in_=yo[e % 2][0:m, j, :], in_offset=None,
                        bounds_check=NT * P - 1, oob_is_err=False).then_inc(s_sc[e % 2], 16)

            def weights_low(e):
                for q in range(PIECES):
                    if LOW[q] == "G":
                        s_wh.wait(eng, PIECES * e + q + 1)
                        sl, buf = piece(q), (e + 1) % 2
                        eng.tensor_tensor(wl[buf][:, sl], wraw[:, sl], wh[buf][:, sl].bitcast(F32),
                                          ALU.subtract).then_inc(s_wl["G"].sem, 1)

            eng.memset(empty[:, :], NO_TOKEN).then_inc(s_empty, 1)
            norm.pow_step(eng, 0, 4)
            norm.pow_step(eng, 1, 4)
            with_bias(0)
            PUTS = 2 * NT // NB
            for n in range(NB + E):
                if n > NB:
                    scatter(n - NB - 1)
                if n + 2 < NB + E:
                    norm.pow_step(eng, n + 2, 4 if n + 2 < NB else 3)
                if n == 0:
                    eng.wait_ge(slots.s_v, slots.PUT)
                    eng.wait_ge(s_tab, 16)
                for t in range(PUTS * n, min(PUTS * (n + 1), NT)):
                    eng.indirect_dma_start(
                        out=table[:, :], out_offset=bass.IndirectOffsetOnAxis(ap=put[:, t:t + 1], axis=0),
                        in_=k.tokid[:, t:t + 1], in_offset=None,
                        bounds_check=E * C - 1, oob_is_err=False).then_inc(s_put, 16)
                if n + 1 < NB + E:
                    with_bias(n + 1)
                if n == NB - 2:
                    weights_low(0)
                elif NB <= n < NB + E - 1:
                    weights_low(n - NB + 1)
                if n >= NB - 3 and n + 3 < NB + E:
                    gather(n + 3 - NB)
            scatter(E - 1)
            for s in s_sc:
                eng.wait_ge(s, 16 * len(CCH) * (E // 2))

        @block.vector
        def _(eng):
            norm.open_vector(eng)
            for s in (s_xn, s_tlo, s_lo, s_y, s_wl["V"]):
                s.open(eng)

            def stats(i, n, b, kind):
                if kind == "dense":
                    s_ld[b].wait(eng, 16 * i + 16)
                else:
                    eng.wait_ge(s_ga[b], 16 * len(CCH) * (i + 1))
                norm.stats_step(eng, n, xr[b], rows_of[kind])

            def apply(n, b, kind):
                s_tp.wait(eng, 2 * n - 2)
                norm.apply_step(eng, n, xn[b], xr[b], rows_of[kind]).then_inc(s_xn.sem, 1)

            def rows_low(n, b, f, w):
                s_thi.wait(eng, 2 * n + f + 1)
                eng.tensor_tensor(xTl[b][:, f, 0:w], pT[f][:, 0:w], xTh[b][:, f, 0:w].bitcast(F32),
                                  ALU.subtract).then_inc(s_tlo.sem, 1)

            def hidden_low(n, h, w):
                s_hi.wait(eng, HT * n + h + 1)
                eng.tensor_tensor(hl[h % RING][:, 0:w], h32[h % 2][:, 0:w], hh[h % RING][:, 0:w].bitcast(F32),
                                  ALU.subtract).then_inc(s_lo.sem, 1)

            def weights(e, buf, q):
                if LOW[q] == "V":
                    sl = piece(q)
                    s_wh.wait(eng, PIECES * e + q + 1)
                    eng.tensor_tensor(wl[buf][:, sl], wraw[:, sl], wh[buf][:, sl].bitcast(F32),
                                      ALU.subtract).then_inc(s_wl["V"].sem, 1)

            def results(i, n, b, kind):
                s_l2.wait(eng, HT * (n + 1))
                s_xs.wait(eng, n + 1)
                if kind == "dense":
                    s_st[b].wait(eng, 16 * i)
                else:
                    s_st[b].wait(eng, 16 * (NB // 2))
                    eng.wait_ge(s_sc[b], 16 * len(CCH) * i)
                for j in range(0, len(rows_of[kind]), 2):
                    m, w = rows_of[kind][j], min(2, len(rows_of[kind]) - j)
                    ins = eng.scalar_tensor_tensor(
                        yo[b][0:m, j:j + w, :], pA[b][0:m, j // 2, 0:w * D].rearrange("p (t d) -> p t d", d=D), 0.5,
                        xs[b][0:m, j:j + w, :], ALU.mult, ALU.add)
                ins.then_inc(s_y.sem, 1)

            def prologue():
                slots.experts_step(eng)
                for n in range(2):
                    stats(0, n, n, "dense")
                    apply(n, n, "dense")
                    if n == 0:
                        for f in range(DT):
                            rows_low(0, 0, f, 512)
                for h in range(LAG):
                    hidden_low(0, h, 512)
                slots.slots_step(eng, put)

            def block_(i, n, b, kind, nxt, nxt2):
                sp = split_at(i, n, b, kind)
                for s in range(HT):
                    if nxt and s in (0, 2):
                        rows_low(n + 1, 1 - b, s // 2, width[nxt])
                    if s + LAG < HT:
                        hidden_low(n, s + LAG, width[kind])
                    elif nxt:
                        hidden_low(n + 1, s + LAG - HT, width[nxt])
                    for q in pieces_at(s) if sp else ():
                        weights(sp[0], sp[1], q)
                    if nxt2 and s == 3:
                        stats(pair_after(i, b, kind, nxt2, 2), n + 2, b, nxt2)
                    if nxt2 and s == 5:
                        apply(n + 2, b, nxt2)
                results(i, n, b, kind)

            stream(eng, prologue, block_)

        @block.scalar
        def _(eng):
            for t in (s_thi, s_h, s_hi, s_wh):
                t.open(eng)

            def rows_high(n, b, f, w):
                s_tp.wait(eng, 2 * n + f + 1)
                s_l1.wait(eng, HT * (n - 1))
                eng.activation(xTh[b][:, f, 0:w], pT[f][:, 0:w], ACT.Copy).then_inc(s_thi.sem, 1)

            def hidden_high(i, n, b, kind, h):
                w = width[kind]
                g = HT * n + h
                bias = k.b1T[:, E, h:h + 1] if kind == "dense" else k.b1T[:, bass.ds(2 * i + b, 1), h]
                s_l1.wait(eng, g + 1)
                s_lo.wait(eng, g - 1)
                eng.activation(h32[h % 2][:, 0:w], pL[h % 2][:, 0:w], ACT.Relu, bias=bias).then_inc(s_h.sem, 1)
                s_h.wait(eng, g + 1)
                s_l2.wait(eng, g - RING + 1)
                eng.activation(hh[h % RING][:, 0:w], h32[h % 2][:, 0:w], ACT.Copy).then_inc(s_hi.sem, 1)

            def weights_high(e, buf, q, n):
                s_raw[q].wait(eng, 16 * e + 16)
                s_l2.wait(eng, HT * n)
                sl = piece(q)
                eng.activation(wh[buf][:, sl], wraw[:, sl], ACT.Copy).then_inc(s_wh.sem, 1)

            def prologue():
                for f in range(DT):
                    rows_high(0, 0, f, 512)
                for h in range(LAG):
                    hidden_high(0, 0, 0, "dense", h)

            def block_(i, n, b, kind, nxt, nxt2):
                sp = split_at(i, n, b, kind)
                i1 = pair_after(i, b, kind, nxt, 1)
                for s in range(HT):
                    if nxt and s in (0, 2):
                        rows_high(n + 1, 1 - b, s // 2, width[nxt])
                    if s + LAG < HT:
                        hidden_high(i, n, b, kind, s + LAG)
                    elif nxt:
                        hidden_high(i1, n + 1, 1 - b, nxt, s + LAG - HT)
                    for q in pieces_at(s, ahead=1) if sp else ():
                        weights_high(sp[0], sp[1], q, n)

            stream(eng, prologue, block_)

        @block.tensor
        def _(eng):
            for t in (s_tp, s_l1, s_l2):
                t.open(eng)

            def turn(n, b, kind, f):
                s_xn.wait(eng, n + 1)
                s_tlo.wait(eng, 2 * (n - 1) + f + 1)
                for j, (c0, m) in enumerate(chunks[kind]):
                    mm = eng.transpose(pT[f][:, c0:c0 + m], xn[b][0:m, j, f * P:(f + 1) * P], k.ident[0:m, 0:m])
                mm.then_inc(s_tp.sem, 1)

            def into_hidden(n, b, kind, h):
                w, wb = width[kind], wbuf(b, kind)
                if h == 0:
                    s_tlo.wait(eng, 2 * n + 2)
                s_h.wait(eng, HT * n + h - 1)
                out = pL[h % 2][:, 0:w]
                for c in range(DT):
                    eng.matmul(out, W1(wh[wb], c, h), xTh[b][:, c, 0:w], start=(c == 0), stop=False)
                    eng.matmul(out, W1(wh[wb], c, h), xTl[b][:, c, 0:w], start=False, stop=False)
                    mm = eng.matmul(out, W1(wl[wb], c, h), xTh[b][:, c, 0:w], start=False, stop=(c == DT - 1))
                mm.then_inc(s_l1.sem, 1)

            def out_of_hidden(n, b, kind, h):
                wb = wbuf(b, kind)
                s_lo.wait(eng, HT * n + h + 1)
                if h == 0:
                    s_y.wait(eng, n - 1)
                    if kind == "dense" and b == 1:
                        eng.wait_ge(slots.s_v, slots.PUT)
                for j, (c0, m) in enumerate(chunks[kind]):
                    out = pA[b][0:m, j // 2, (j % 2) * D:(j % 2 + 1) * D]
                    hi, lo = hh[h % RING][:, c0:c0 + m], hl[h % RING][:, c0:c0 + m]
                    eng.matmul(out, hi, W2(wh[wb], h), start=(h == 0 and j % 2 == 0), stop=False,
                               skip_group_check=True)
                    eng.matmul(out, hi, W2(wl[wb], h), start=False, stop=False, skip_group_check=True)
                    mm = eng.matmul(out, lo, W2(wh[wb], h), start=False, stop=(h == HT - 1), skip_group_check=True)
                mm.then_inc(s_l2.sem, 1)

            def weights_ready(e, q):
                for p in {LOW[p]: p for p in range(q + 1)}.values():
                    s_wl[LOW[p]].wait(eng, lows(e, p))

            def prologue():
                slots.count_step(eng)
                for f in range(DT):
                    turn(0, 0, "dense", f)
                for h in range(LAG):
                    into_hidden(0, 0, "dense", h)

            def block_(i, n, b, kind, nxt, nxt2):
                for s in range(HT):
                    if nxt and s in (0, 2):
                        turn(n + 1, 1 - b, nxt, s // 2)
                    if kind == "expert" and s % 2 == 0:
                        weights_ready(expert(i, b), PIECES // 2 + s // 2)
                    out_of_hidden(n, b, kind, s)
                    if s + LAG < HT:
                        if kind == "expert" and s + LAG == HT // 2:
                            weights_ready(expert(i, b), PIECES // 2 - 1)
                        into_hidden(n, b, kind, s + LAG)
                    elif nxt:
                        if nxt == "expert" and s + LAG == HT:
                            weights_ready(expert(i, b) + 1 if kind == "expert" else 0, DT - 1)
                        into_hidden(n + 1, 1 - b, nxt, s + LAG - HT)

            stream(eng, prologue, block_)


def ffn(nc, k, name, x_in, x_out, w1, b2, w2, ow1, ow2, ob2):
    table = nc.dram_tensor(name + "table", (E * C, 1), I32).ap()
    with ExitStack() as ctx:
        b2s = ctx.enter_context(nc.sbuf_tensor(name + "b2s", [P, E + 1, D], F32))
        lg = ctx.enter_context(nc.sbuf_tensor(name + "lg", [P, 64, E], F32))
        wts = Weights(ctx, nc, name)
        router(nc, k, lg, wts, name + "ro_", x_in, b2s, b2, ob2, ow1, ow2)
        mlps(nc, k, lg, wts, name + "ml_", x_in, x_out, b2s, w1, w2, table)


HEADS = 16
HS = D // HEADS
GH = 4
VW = 32
SLOTS = 6
Q_PARTS = [0, 1, 2, 0, 1, 0]
K_PARTS = [0, 0, 0, 1, 1, 2]
KROWS = SLOTS * HS
SCALE = float(HS) ** -0.25
MROWS = 3


def runs(order):
    starts = [s for s, p in enumerate(order) if s == 0 or p != order[s - 1] + 1]
    return [(s, order[s], e - s) for s, e in zip(starts, starts[1:] + [len(order)])]


class Heads:

    def __init__(self, ctx, nc):
        sb = lambda name, shape, dt: ctx.enter_context(nc.sbuf_tensor("at_" + name, shape, dt))
        self.wd = sb("wd", [P, DT, D], F32)
        self.wu = sb("wu", [P, DT, D], F32)
        self.bu = sb("bu", [P, D], F32)
        self.raw = sb("raw", [P, 3, DT, HS], F32)
        self.bd = sb("bd", [P, 3, DT, P], F32)
        self.s_in = ctx.enter_context(nc.semaphore("at_s_in"))

    LOADS = 3 + 3

    def load(self, eng, W_down, toqueries, tokeys, tovalues, W_unify, b_unify):
        eng.dma_start(self.wd[:, :, :], W_down.rearrange("(c p) n -> p c n", p=P)).then_inc(self.s_in, 16)
        eng.dma_start(self.wu[:, :, :], W_unify.rearrange("(c p) n -> p c n", p=P)).then_inc(self.s_in, 16)
        eng.dma_start(self.bu[:, :], b_unify.rearrange("(a e) -> a e", a=1).broadcast_to([P, D])).then_inc(self.s_in, 16)
        for m, a in enumerate((toqueries, tokeys, tovalues)):
            eng.dma_start(self.raw[:, m, :, :],
                          a.rearrange("(c h) i k -> (h i) c k", c=DT)).then_inc(self.s_in, 16)


class Diagonals:

    def __init__(self, ctx, nc, w, k, banks, room):
        self.w, self.k, self.banks = w, k, banks
        parts = room.rearrange("p t (q h s) -> p (t q) h s", h=8, s=HS)
        self.diag, self.mask = parts[:, 0:3 * DT, :, :], parts[:, 3 * DT, :, :]
        sem = lambda n: ctx.enter_context(nc.semaphore("at_s_diag_" + n))
        self.s_mask, self.s_diag, self.s_turned = sem("mask"), sem("diag"), sem("turned")

    def mask_step(self, eng):
        mask = self.mask
        eng.memset(mask, 1.0).then_inc(self.s_mask, 1)
        for n, (base, sign) in enumerate(((0, 1), (HS - 1, -1))):
            eng.wait_ge(self.s_mask, n + 1)
            eng.affine_select(out=mask, in_=mask, compare_op=ALU.is_ge, fill=0.0, base=base,
                              pattern=[[-sign * HS, 8], [0, HS]], channel_multiplier=sign).then_inc(self.s_mask, 1)

    def spread_step(self, eng):
        eng.wait_ge(self.s_mask, 3)
        eng.wait_ge(self.w.s_in, 16 * self.w.LOADS)
        for q in range(3 * DT):
            eng.tensor_tensor(self.diag[:, q, :, :],
                              self.w.raw[:, q // DT, q % DT, :].unsqueeze(1).broadcast_to([P, 8, HS]),
                              self.mask, ALU.mult).then_inc(self.s_diag, 1)

    def place(self, q):
        return self.banks[q // 4][:, q % 4 * P:(q % 4 + 1) * P]

    def turn_step(self, eng):
        for q in range(3 * DT):
            eng.wait_ge(self.s_diag, q + 1)
            mm = eng.transpose(self.place(q), self.diag[:, q, :, :].rearrange("p h s -> p (h s)"), self.k.ident[:, :])
        mm.then_inc(self.s_turned, 1)

    def copy_step(self, eng):
        eng.wait_ge(self.s_turned, 1)
        for q in range(3 * DT):
            ins = eng.tensor_copy(self.w.bd[:, q // DT, q % DT, :], self.place(q))
        ins.then_inc(self.s_diag, 1)

    def ready(self, eng):
        eng.wait_ge(self.s_diag, 3 * DT + 1)


def attention(nc, k, w, x_in, x_out, NBAT):
    T = 1024
    NT = T // P
    NQ = 512
    BANKS = 3
    RES = 4
    ST = 2 * NT
    CH = GH * NT
    ULOADS = 2 * len(runs(Q_PARTS)) + len(runs(K_PARTS))
    MR = GH * NT // 2
    scr = nc.dram_tensor("at_scr", (2, HEADS, 3, HS, T), BF16).ap()
    x_t, o_t = split_token_tiles(x_in), split_token_tiles(x_out)
    with ExitStack() as ctx:
        sb = lambda n, shape, dt: ctx.enter_context(nc.sbuf_tensor("at_" + n, shape, dt))
        ps = lambda n, shape: ctx.enter_context(nc.psum_tensor("at_" + n, shape, F32))
        xr = sb("xr", [P, NT, D], F32)
        xn = sb("xn", [P, NT, D], F32)
        xT = sb("xT", [P, DT, T], F32)
        xd = xn[:, :, :].rearrange("p t d -> p (t d)").rearrange("p (c t) -> p c t", c=DT)
        res = [sb(f"res{i}", [P, 512], F32) for i in range(RES)]
        parts = sb("parts", [P, 2, 3, DT, T], BF16)
        qa = [sb(f"qa{g}", [P, 2, GH, NQ], BF16) for g in range(4)]
        ka = [sb(f"ka{g}", [P, GH, T], BF16) for g in range(4)]
        va = [sb(f"va{i}", [P, NT, HEADS, VW], F32) for i in range(2)]
        ex = [sb(f"ex{i}", [P, GH, NQ], F32) for i in range(2)]
        zeros = sb("zeros", [P, 1], F32)
        mxc = sb("mxc", [P, CH], F32)
        nm = sb("nm", [P, MR], F32)
        mparts = sb("mparts", [MR, 3, P], BF16)
        os_ = sb("os", [P, NQ], F32)
        rec = sb("rec", [P, 4, GH], F32)
        ao = sb("ao", [P, NT, D], F32)
        aT = sb("aT", [P, DT, NQ], F32)
        xres = sb("xres", [P, NT, D], F32)
        yo = [sb(f"yo{i}", [P, 2, D], F32) for i in range(2)]
        norm = Norm(ctx, nc, k, "at_ln_")
        pb = [ps(f"pb{i}", [P, 512]) for i in range(BANKS)]
        pd = [ps(f"pd{i}", [P, 512]) for i in range(BANKS)]
        po = ps("po", [P, 512])
        px = ps("px", [P, 512])
        diagonals = Diagonals(ctx, nc, w, k, pb, ao[:, :, :])

        S = lambda n: Sem(ctx, nc, "at_" + n)
        s_one = ctx.enter_context(nc.semaphore("at_s_one"))
        s_row = ctx.enter_context(nc.semaphore("at_s_row"))
        s_zero = ctx.enter_context(nc.semaphore("at_s_zero"))
        s_xr = [S(f"s_xr{f}") for f in range(2)]
        s_xn = S("s_xn")
        s_ax = S("s_ax")
        s_ac = S("s_ac")
        s_hi = S("s_hi")
        s_mi = S("s_mi")
        s_lo = S("s_lo")
        s_scr = S("s_scr")
        s_ld = [S(f"s_ld{g}") for g in range(4)]
        s_mr = [S(f"s_mr{g}") for g in range(4)]
        s_b = S("s_b")
        s_mx = S("s_mx")
        s_nm = S("s_nm")
        s_d = S("s_d")
        s_ex = Sem(ctx, nc, "at_s_ex", credit=CREDIT + GH * ST)
        s_pv = S("s_pv")
        s_o = S("s_o")
        s_rc = S("s_rc")
        s_xl = S("s_xl")
        s_xb = S("s_xb")
        s_st = [S(f"s_st{i}") for i in range(2)]

        XT = [("xT", c, f) for f in range(2) for c in range(DT)]
        XD = [("xd", c, f) for f in range(2) for c in range(DT)]
        QK = [("qk", m, c, f) for c in range(DT) for m in range(2) for f in range(2)]
        V = [("v", a) for a in range(NT // 2)]
        OUT = lambda f: [("aT", f, 0), ("aT", f, 1), ("u", f, 0), ("u", f, 1)]

        def task_at(g, t, prev, last):
            table = {0: ("f", 1), 8: ("f", 0), 2: ("mx", 1), 10: ("mx", 0)}
            if g == 0 and not prev:
                del table[0]
            if g == 3 and last:
                del table[10]
            if g == 0 and prev:
                table.update(zip((1, 3, 4, 5), OUT(1)))
            if g == 3:
                table.update(zip((9, 11, 12, 13), OUT(0)))
            if g == 0 and not last:
                table.update(zip((6, 7, 11, 12, 13, 14), XT + XD))
            if g == 1 and not last:
                table.update(zip((1, 3, 5, 6, 7, 9, 11, 13), XD[-2:] + QK))
            if g == 2 and not last:
                table.update(zip((1, 3, 4, 5, 6, 7), QK[-2:] + V))
            return table.get(t)

        class Aux:

            def __init__(self, task, b, par, g, n, ns, slot):
                self.kind, self.at = task[0], task[1:]
                self.b, self.par, self.g, self.n, self.ns, self.slot = b, par, g, n, ns, slot
                self.bank, self.slack = px, 0

        splits = lambda task: task[0] in ("qk", "mx")
        ROUND = [(g, bl) for bl, g in ((0, 1), (0, 2), (0, 3), (1, 0), (1, 1), (1, 2), (1, 3), (2, 0))]

        class Walk:

            def __init__(self, eng, do):
                self.n, self.ns, self.slot = 0, 0, 0
                first = [self.next(task, 0, 0, 0) for task in XT + XD + QK[:4] + V + QK[4:] + [("mx", 0)]]
                for a, b in zip(first[1:], first):
                    a.bank = po if a.n % 2 and a.kind != "mx" else px
                    a.slack = 1 if a.kind == b.kind or a.kind in ("xd", "qk") else 0
                do.start(first)
                self.phase(do, 0, 0, 0, prev=False)
                n0, ns0 = self.n, self.ns
                tasks = [x for g, _ in ROUND for t in range(ST) if (x := task_at(g, t, True, False))]
                dn, dns = len(tasks), sum(map(splits, tasks))
                assert dns % RES == 0
                rounds = NBAT // 2 - 1
                with eng.Fori(0, rounds) as i:
                    self.n, self.ns = n0 + dn * i, ns0 + dns * i
                    for g, bl in ROUND:
                        self.phase(do, 2 * i + bl, bl % 2, g)
                self.n, self.ns = n0 + dn * rounds, ns0 + dns * rounds
                for g, bl in ROUND[:-1]:
                    self.phase(do, 2 * rounds + bl, bl, g, last=(bl == 1))
                do.end([self.next(task, NBAT - 1, 1, 3) for task in [("f", 1)] + OUT(1)])

            def next(self, task, b, par, g):
                a = Aux(task, b, par, g, self.n, self.ns, self.slot)
                self.n = self.n + 1
                if splits(task):
                    self.ns, self.slot = self.ns + 1, (self.slot + 1) % RES
                return a

            def phase(self, do, b, par, g, prev=True, last=False):
                before = None
                for t in range(ST):
                    task = task_at(g, t, prev, last)
                    now, n, ns = None, self.n, self.ns
                    if task and task[0] in ("xT", "xd", "qk", "v"):
                        now = self.next(task, b + 1, 1 - par, g)
                    elif task == ("mx", 0):
                        now = self.next(task, *((b, par, g + 1) if g < 3 else (b + 1, 1 - par, 0)))
                    elif task == ("f", 1):
                        now = self.next(task, *((b, par, g - 1) if g > 0 else (b - 1, 1 - par, 3)))
                    elif task and task[0] in ("aT", "u") and g == 0:
                        now = self.next(task, b - 1, 1 - par, g)
                    elif task:
                        now = self.next(task, b, par, g)
                    do.step(b, par, g, t, n, ns, before, now, last)
                    before = now

        def place(c):
            return 1 if c == ST * GH - 1 else c % BANKS

        def back(c):
            return next(d for d in range(1, ST * GH) if place((c - d) % (ST * GH)) == place(c))

        unit = lambda b, g: 4 * b + g
        next_unit = lambda b, g: (b, g + 1) if g < 3 else (b + 1, 0)
        block = ctx.enter_context(nc.Block())

        @block.sync
        def _(eng):
            for s in (*s_xr, s_scr, *s_ld, *s_mr, s_xl, *s_st):
                s.open(eng)

            def load_rows(b):
                s_xn.wait(eng, 2 * b)
                for f in range(2):
                    eng.dma_start(xr[:, 4 * f:4 * f + 4, :],
                                  x_t[:, bass.ds(NT * b + 4 * f, 4), :]).then_inc(s_xr[f].sem, 16)

            def store_parts(b, c, ns):
                s_lo.wait(eng, ns)
                for g in (2 * c, 2 * c + 1):
                    s_ld[g].wait(eng, 16 * ULOADS * b)
                for m in range(2):
                    for p in range(3):
                        eng.dma_start(scr[m, 8 * c:8 * (c + 1), p, :, :], parts[:, m, p, c, :]).then_inc(s_scr.sem, 16)
                s_scr.wait(eng, 192 * b + 96 * (c + 1))

            def load_unit(b, g):
                if not (isinstance(b, int) and b == 0):
                    s_pv.wait(eng, ST * (unit(b, g) - 3))
                for m, dst, order, t0, t1 in ((0, qa[g][:, 0, :, :], Q_PARTS, 0, NQ), (1, ka[g], K_PARTS, 0, T),
                                              (0, qa[g][:, 1, :, :], Q_PARTS, NQ, T)):
                    for s, p, w in runs(order):
                        src = scr[m, GH * g:GH * (g + 1), p:p + w, :, t0:t1].rearrange("j p r t -> (p r) j t")
                        eng.dma_start(dst[HS * s:HS * (s + w), :, :], src).then_inc(s_ld[g].sem, 16)

            def load_maxima(a):
                s_lo.wait(eng, a.ns + 1)
                for p in range(MROWS):
                    eng.dma_start(qa[a.g][KROWS + p:KROWS + p + 1, a.at[0], :, :].rearrange("a j (t q) -> a (j t) q", q=P),
                                  mparts[:, p, :]).then_inc(s_mr[a.g].sem, 16)

            def store_out(a):
                f, half = a.at
                s_ac.wait(eng, a.n + 1)
                eng.dma_start(o_t[:, bass.ds(NT * a.b + 4 * f + 2 * half, 2), :],
                              yo[half][:, :, :]).then_inc(s_st[half].sem, 16)

            class Do:
                def start(self, tasks):
                    load_rows(0)
                    for c in range(DT):
                        store_parts(0, c, len(QK) // 2 * (c + 1))
                        load_unit(0, c)
                    load_maxima(tasks[-1])

                def step(self, b, par, g, t, n, ns, before, now, last):
                    if t == 0:
                        if g == 0 and not last:
                            load_rows(b + 1)
                        if g == 2:
                            s_ac.wait(eng, n)
                            eng.dma_start(xres[:, :, :], x_t[:, bass.ds(NT * b, NT), :]).then_inc(s_xl.sem, 16)
                    if now and now.kind == "mx":
                        load_maxima(now)
                    if t == 3:
                        if g < 2:
                            load_unit(b, g + 2)
                        elif g == 3 and not last:
                            load_unit(b + 1, 1)
                    if g == 2 and t == 5 and not last:
                        for c in range(DT):
                            store_parts(b + 1, c, ns)
                        load_unit(b + 1, 0)
                    if now and now.kind == "u":
                        store_out(now)

                def end(self, tasks):
                    for a in tasks[3:]:
                        store_out(a)
                    for s in s_st:
                        s.wait(eng, 16 * 2 * NBAT)

            Walk(eng, Do())

        @block.tensor
        def _(eng):
            for s in (s_ax, s_b, s_d, s_pv):
                s.open(eng)

            def scores_for_max(b, g, c):
                qh, j, qt, kh = c // CH, c % CH // NT, c % NT // 2, c % 2
                if c == 0:
                    s_ld[g].wait(eng, 16 * ULOADS * (b + 1))
                s_mx.wait(eng, 2 * CH * unit(b, g) + (c - back(c) + 1))
                eng.matmul(pb[place(c)][:, :], qa[g][0:KROWS, qh, j, qt * P:(qt + 1) * P],
                           ka[g][0:KROWS, j, kh * 512:(kh + 1) * 512], start=True, stop=True).then_inc(s_b.sem, 1)

            def scores(b, g, t, j):
                qh, kt, c = t // NT, t % NT, GH * t + j
                if kt == 0 and j == 0:
                    s_mr[g].wait(eng, 16 * MROWS * (2 * b + qh + 1))
                s_ex.wait(eng, GH * ST * unit(b, g) + (c - back(c) + 1))
                eng.matmul(pd[place(c)][:, :], ka[g][0:KROWS + MROWS, j, kt * P:(kt + 1) * P],
                           qa[g][0:KROWS + MROWS, qh, j, :], start=True, stop=True).then_inc(s_d.sem, 1)

            def times_v(b, par, g, t):
                kt = t % NT
                if kt == 0:
                    s_o.wait(eng, 2 * unit(b, g) + t // NT)
                s_ex.wait(eng, GH * ST * unit(b, g) + GH * (t + 1))
                for j in range(GH):
                    mm = eng.matmul(po[VW * j:VW * (j + 1), :], va[par][:, kt, GH * g + j, :], ex[t % 2][:, j, :],
                                    start=(kt == 0), stop=(kt == NT - 1), skip_group_check=True)
                mm.then_inc(s_pv.sem, 1)

            def aux(a):
                s_ac.wait(eng, a.n - a.slack)
                bank = a.bank
                turn = lambda src: [eng.transpose(bank[:, j * P:(j + 1) * P], src(j), k.ident[:, :]) for j in range(4)][-1]
                if a.kind == "xT":
                    c, f = a.at
                    s_xn.wait(eng, 2 * a.b + f + 1)
                    mm = turn(lambda j: xn[:, 4 * f + j, c * P:(c + 1) * P])
                elif a.kind == "xd":
                    c, f = a.at
                    for d in range(DT):
                        mm = eng.matmul(bank[:, :], w.wd[:, d, c * P:(c + 1) * P], xT[:, d, f * 512:(f + 1) * 512],
                                        start=(d == 0), stop=(d == DT - 1))
                elif a.kind == "qk":
                    m, c, f = a.at
                    mm = eng.matmul(bank[:, :], w.bd[:, m, c, :], xd[:, c, f * 512:(f + 1) * 512], start=True, stop=True)
                elif a.kind == "v":
                    for i in range(2):
                        tile = 2 * a.at[0] + i
                        for c in range(DT):
                            mm = eng.matmul(bank[:, i * D + c * P:i * D + (c + 1) * P], xd[:, c, tile * P:(tile + 1) * P],
                                            w.bd[:, 2, c, :], start=True, stop=True)
                elif a.kind == "mx":
                    s_nm.wait(eng, 2 * unit(a.b, a.g) + a.at[0] + 1)
                    mm = eng.transpose(bank[0:MR, 0:P], nm[:, :], k.ident[:, :])
                elif a.kind == "f":
                    s_o.wait(eng, 2 * unit(a.b, a.g) + a.at[0] + 1)
                    mm = turn(lambda j: os_[:, j * P:(j + 1) * P])
                elif a.kind == "aT":
                    f, c = a.at
                    mm = turn(lambda j: ao[:, 4 * f + j, c * P:(c + 1) * P])
                elif a.kind == "u":
                    f, half = a.at
                    for i in range(2):
                        q = (2 * half + i) * P
                        for c in range(DT):
                            mm = eng.matmul(bank[:, i * D:(i + 1) * D], aT[:, c, q:q + P], w.wu[:, c, :],
                                            start=(c == 0), stop=(c == DT - 1))
                mm.then_inc(s_ax.sem, 1)

            class Do:
                def start(self, tasks):
                    diagonals.turn_step(eng)
                    for a in tasks[:-1]:
                        if a.kind == "qk":
                            diagonals.ready(eng)
                        aux(a)
                    for c in range(2 * CH):
                        scores_for_max(0, 0, c)
                        if c == CH + 1:
                            aux(tasks[-1])
                    eng.wait_ge(s_one, 2)
                    eng.wait_ge(s_row, 4)
                    for j in range(GH):
                        scores(0, 0, 0, j)

                def step(self, b, par, g, t, n, ns, before, now, last):
                    b1, g1 = next_unit(b, g)
                    ahead = not (last and g == 3)
                    ends = last and g == 3 and t == ST - 1
                    for i in range(4):
                        if ahead:
                            scores_for_max(b1, g1, 4 * t + i)
                        if not ends:
                            scores(*((b, g, t + 1) if t < ST - 1 else (b1, g1, 0)), i)
                        if i == 1:
                            times_v(b, par, g, t)
                    if now:
                        aux(now)

                def end(self, tasks):
                    for a in tasks:
                        aux(a)

            Walk(eng, Do())

        @block.scalar
        def _(eng):
            for s in (s_hi, s_ex, s_ac):
                s.open(eng)

            def aux(a):
                if a is None or a.kind in ("f", "u"):
                    return
                bank = a.bank
                s_ax.wait(eng, a.n + 1)
                if a.kind == "qk":
                    m, c, f = a.at
                    s_scr.wait(eng, 192 * a.b)
                    eng.activation(parts[:, m, 0, c, f * 512:(f + 1) * 512], bank[:, :], ACT.Copy,
                                   scale=SCALE).then_inc(s_hi.sem, 1)
                    return
                if a.kind == "mx":
                    if a.at[0] == 1:
                        s_mr[a.g].wait(eng, 16 * MROWS * (2 * a.b + 1))
                    else:
                        s_mr[(a.g - 1) % 4].wait(eng, 16 * MROWS * (2 * a.b + 2 if a.g else 2 * a.b))
                    eng.activation(mparts[:, 0, :], bank[0:MR, 0:P], ACT.Copy).then_inc(s_hi.sem, 1)
                    return
                if a.kind == "v":
                    for i in range(2):
                        ins = eng.activation(va[a.par][:, 2 * a.at[0] + i, :, 0:HS],
                                             bank[:, i * D:(i + 1) * D].rearrange("p (h s) -> p h s", s=HS), ACT.Copy)
                elif a.kind == "aT":
                    ins = eng.activation(aT[:, a.at[1], :], bank[:, :], ACT.Copy)
                else:
                    c, f = a.at
                    dst = xT if a.kind == "xT" else xd
                    ins = eng.activation(dst[:, c, f * 512:(f + 1) * 512], bank[:, :], ACT.Copy)
                ins.then_inc(s_ac.sem, 1)

            class Do:
                def start(self, tasks):
                    for a in tasks:
                        if a.kind == "v":
                            eng.wait_ge(s_one, 2)
                        aux(a)

                def step(self, b, par, g, t, n, ns, before, now, last):
                    for j in range(GH):
                        s_d.wait(eng, GH * ST * unit(b, g) + (GH * t + j + 1))
                        eng.activation(ex[t % 2][:, j, :], pd[place(GH * t + j)][:, :],
                                       ACT.Exp).then_inc(s_ex.sem, 1)
                    aux(before)

                def end(self, tasks):
                    for a in tasks:
                        aux(a)

            Walk(eng, Do())

        @block.vector
        def _(eng):
            norm.open_vector(eng)
            for s in (s_xn, s_mx, s_nm, s_o, s_rc):
                s.open(eng)

            def maxima(b, g, c):
                s_b.wait(eng, 2 * CH * unit(b, g) + (c + 1))
                if c % CH == 0:
                    s_nm.wait(eng, 2 * unit(b, g) + c // CH)
                eng.tensor_reduce(mxc[:, c % CH:c % CH + 1], pb[place(c)][:, :], AX.X, ALU.max).then_inc(s_mx.sem, 1)

            def negate(b, g, qh, n):
                s_mx.wait(eng, CH * (2 * unit(b, g) + qh + 1))
                s_ax.wait(eng, n)
                eng.tensor_reduce(nm[:, :], mxc[:, :].rearrange("p (q h) -> p q h", h=2), AX.X, ALU.max,
                                  negate=True).then_inc(s_nm.sem, 1)

            ALL, FIRST, SECOND = range(4), (0, 1), (2, 3)

            def stats(b, f, tiles=ALL):
                s_xr[f].wait(eng, 16 * (b + 1))
                step = norm.tile_stats if tiles is FIRST else norm.stats_step
                step(eng, 2 * b + f, xr[:, 4 * f:4 * f + 4, :], [P] * 4, tiles)

            def apply(b, f, n, tiles=ALL):
                s_ax.wait(eng, n)
                at = slice(4 * f, 4 * f + 4)
                ins = norm.apply_step(eng, 2 * b + f, xn[:, at, :], xr[:, at, :], [P] * 4, tiles)
                if tiles is not FIRST:
                    ins.then_inc(s_xn.sem, 1)

            def aux(a):
                if a is None or a.kind not in ("qk", "mx", "f", "u"):
                    return
                bank = a.bank
                if a.kind in ("qk", "mx"):
                    s_hi.wait(eng, a.ns + 1)
                    s_lo.wait(eng, a.ns - RES + 1)
                    if a.kind == "qk":
                        m, c, f = a.at
                        eng.scalar_tensor_tensor(res[a.slot][:, :], bank[:, :], SCALE,
                                                 parts[:, m, 0, c, f * 512:(f + 1) * 512],
                                                 ALU.mult, ALU.subtract).then_inc(s_ac.sem, 1)
                    else:
                        eng.tensor_tensor(res[a.slot][0:MR, 0:P], bank[0:MR, 0:P], mparts[:, 0, :],
                                          ALU.subtract).then_inc(s_ac.sem, 1)
                    return
                s_ax.wait(eng, a.n + 1)
                if a.kind == "f":
                    u = unit(a.b, a.g)
                    v = bank[:, :].rearrange("p (t j s) -> p t j s", t=4, j=GH)
                    eng.reciprocal(rec[:, :, :], v[:, :, :, HS]).then_inc(s_rc.sem, 1)
                    s_rc.wait(eng, 2 * u + a.at[0] + 1)
                    out = ao[:, 4 * a.at[0]:4 * a.at[0] + 4, GH * HS * a.g:GH * HS * (a.g + 1)]
                    ins = eng.tensor_tensor(out.rearrange("p t (j s) -> p t j s", j=GH), v[:, :, :, 0:HS],
                                            rec[:, :, :].unsqueeze(3).broadcast_to([P, 4, GH, HS]), ALU.mult)
                else:
                    f, half = a.at
                    s_xb.wait(eng, a.b + 1)
                    s_st[half].wait(eng, 16 * (2 * a.b + f))
                    r0 = 4 * f + 2 * half
                    ins = eng.tensor_tensor(yo[half][:, :, :], bank[:, :].rearrange("p (t d) -> p t d", d=D),
                                            xres[:, r0:r0 + 2, :], ALU.add)
                ins.then_inc(s_ac.sem, 1)

            class Do:
                def start(self, tasks):
                    diagonals.spread_step(eng)
                    stats(0, 0)
                    diagonals.copy_step(eng)
                    apply(0, 0, 0)
                    stats(0, 1)
                    apply(0, 1, 0)
                    for v in va:
                        eng.memset(v[:, :, :, HS + 1:VW], 0.0)
                        eng.memset(v[:, :, :, HS:HS + 1], 1.0).then_inc(s_one, 1)
                    for a in tasks[:-1]:
                        aux(a)
                    for c in range(2 * CH):
                        maxima(0, 0, c)
                        if c % CH == CH - 1:
                            negate(0, 0, c // CH, len(tasks) if c // CH else 0)
                        if c == CH + 1:
                            aux(tasks[-1])

                def step(self, b, par, g, t, n, ns, before, now, last):
                    b1, g1 = next_unit(b, g)
                    ahead = not (last and g == 3)
                    for i in range(4):
                        if ahead:
                            maxima(b1, g1, 4 * t + i)
                        if i == 1:
                            aux(before)
                        if i == 3 and t % NT == NT - 1:
                            s_pv.wait(eng, ST * unit(b, g) + (t + 1))
                            s_ax.wait(eng, n)
                            eng.tensor_copy(os_[:, :], po[:, :]).then_inc(s_o.sem, 1)
                    if ahead and t % NT == NT - 1:
                        negate(b1, g1, t // NT, n)
                    if g == 0 and not last and 2 <= t < 10:
                        f, q = (t - 2) // 4, (t - 2) % 4
                        if q < 2:
                            stats(b + 1, f, (FIRST, SECOND)[q])
                        else:
                            apply(b + 1, f, n, (FIRST, SECOND)[q - 2])

                def end(self, tasks):
                    for a in tasks:
                        aux(a)

            Walk(eng, Do())

        @block.gpsimd
        def _(eng):
            norm.open_pool(eng)
            for s in (s_mi, s_lo, s_xb):
                s.open(eng)
            diagonals.mask_step(eng)
            eng.memset(zeros[:, :], 0.0).then_inc(s_zero, 1)
            eng.wait_ge(s_zero, 1)

            def aux(a):
                if a is None or not splits((a.kind,)):
                    return
                if a.kind == "qk":
                    m, c, f = a.at
                    mid, low = (parts[:, m, p, c, f * 512:(f + 1) * 512] for p in (1, 2))
                    r = res[a.slot][:, :]
                else:
                    mid, low = mparts[:, 1, :], mparts[:, 2, :]
                    r = res[a.slot][0:MR, 0:P]
                s_ac.wait(eng, a.n + 1)
                eng.tensor_tensor(mid, r, zeros[0:r.shape[0], :].broadcast_to(list(r.shape)), ALU.add).then_inc(s_mi.sem, 1)
                s_mi.wait(eng, a.ns + 1)
                eng.tensor_tensor(low, r, mid, ALU.subtract).then_inc(s_lo.sem, 1)

            class Do:
                def start(self, tasks):
                    for f in range(2):
                        norm.pow_step(eng, f, 4)
                    for a in tasks[:-1]:
                        aux(a)
                    s_lo.wait(eng, len(QK))
                    for i, t in enumerate(ka):
                        eng.memset(t[KROWS:KROWS + MROWS, :, :], 1.0).then_inc(s_row, 1)
                        eng.wait_ge(s_row, i + 1)
                    aux(tasks[-1])

                def step(self, b, par, g, t, n, ns, before, now, last):
                    if g == 0 and not last and t in (3, 7):
                        norm.pow_step(eng, 2 * (b + 1) + t // 4, 4)
                    aux(before)
                    if g == 2 and t == 8:
                        s_xl.wait(eng, 16 * (b + 1))
                        for q in range(0, NT, 2):
                            ins = eng.tensor_tensor(xres[:, q:q + 2, :], xres[:, q:q + 2, :],
                                                    w.bu[:, :].unsqueeze(1).broadcast_to([P, 2, D]), ALU.add)
                        ins.then_inc(s_xb.sem, 1)

                def end(self, tasks):
                    pass

            Walk(eng, Do())


_INS = ["L0_attn_x", "L0_attn_W_down", "L0_attn_tokeys", "L0_attn_toqueries", "L0_attn_tovalues", "L0_attn_W_unify",
        "L0_attn_b_unify", "L0_ffn_router_w", "L0_ffn_router_b", "L0_ffn_w1", "L0_ffn_b1", "L0_ffn_w2", "L0_ffn_b2",
        "L0_ffn_ow1", "L0_ffn_ob1", "L0_ffn_ow2", "L0_ffn_ob2"]


def program(nc, x, W_down, tokeys, toqueries, tovalues, W_unify, b_unify, router_w, router_b, w1, b1, w2, b2,
            ow1, ob1, ow2, ob2, out):
    rows = lambda a: a.rearrange("b t d -> (b t) d")
    with ExitStack() as ctx:
        k = Consts(ctx, nc)
        w = Heads(ctx, nc)
        setup(nc, k, router_w, router_b, b1, ob1, w, (W_down, toqueries, tokeys, tovalues, W_unify, b_unify))
        x1 = nc.dram_tensor("x1", (x.shape[0] * x.shape[1], D), F32).ap()
        x2 = nc.dram_tensor("x2", (x.shape[0] * x.shape[1], D), F32).ap()
        ffn(nc, k, "f1_", rows(x), x1, w1, b2, w2, ow1, ow2, ob2)
        attention(nc, k, w, x1, x2, x.shape[0])
        ffn(nc, k, "f2_", x2, rows(out), w1, b2, w2, ow1, ow2, ob2)


def kernel(**inputs):
    import numpy as np
    import concourse.bacc as bacc
    from concourse.bass_utils import run_bass_kernel_spmd

    nc = bacc.Bacc("TRN2", target_bir_lowering=False, num_devices=1)
    arrays, args = {}, []
    for name in _INS:
        a = np.ascontiguousarray(inputs[name])
        arrays[f"in_{name}"] = a
        args.append(nc.dram_tensor(f"in_{name}", a.shape, mybir.dt.from_np(a.dtype), kind="ExternalInput").ap())
    shape = inputs["L0_attn_x"].shape
    args.append(nc.dram_tensor("out_0", shape, F32, kind="ExternalOutput").ap())
    program(nc, *args)
    r = run_bass_kernel_spmd(nc, [arrays], core_ids=[0])
    return r.results[0]["out_0"]
```
